# Optimizing a Trainium2 kernel written in Bass

```python
import numpy as np
import jax
import jax.numpy as jnp

def _softmax(x, axis=-1):
    return jax.nn.softmax(x, axis=axis)

def _gelu(x):
    return jax.nn.gelu(x, approximate=True)

def _silu(x):
    return jax.nn.silu(x)

def _sigmoid(x):
    return jax.nn.sigmoid(x)

def _layernorm(x, axis=-1, eps=1e-05):
    m = jnp.mean(x, axis=axis, keepdims=True)
    v = jnp.var(x, axis=axis, keepdims=True)
    return (x - m) / jnp.sqrt(v + eps)

def _scatter_add(tgt, idx, src, axis=0):
    return tgt.at[idx].add(src)

def _segment_sum(src, seg, n):
    return jax.ops.segment_sum(src, seg, n)
kernel_name = 'mk_gnn_resnorm_d4_gnn_r16_14e615'

def setup_inputs(seed: int=0):
    np.random.seed(seed)
    _w = jnp.asarray

    def _rec_inputs():
        import jax
        import jax.numpy as jnp
        _gk = jax.random.key(seed)
        x = -0.0003713 + 1 * jax.random.normal(jax.random.fold_in(_gk, 1), (3125, 128), jnp.float32)
        _s = jax.random.randint(jax.random.fold_in(_gk, 2), (25000,), 0, 3125, jnp.int32)
        _d = jax.random.randint(jax.random.fold_in(_gk, 3), (25000,), 0, 3125, jnp.int32)
        _loop = jnp.arange(3125, dtype=jnp.int32)
        src = jnp.concatenate([_s, _d, _loop])
        dst = jnp.concatenate([_d, _s, _loop])
        _o = jnp.argsort(dst, stable=True)
        src = src[_o]
        dst = dst[_o]
        edge_attr_64 = 0.000189758 + 1.00013 * jax.random.normal(jax.random.fold_in(_gk, 12), (53125, 64), jnp.float32)
        edge_type_4 = jax.random.randint(jax.random.fold_in(_gk, 14), (53125,), 0, 4, jnp.int32)
        edge_weight = jax.random.uniform(jax.random.fold_in(_gk, 15), (53125,), jnp.float32, 0.0, 1)
        node_type_3 = jax.random.randint(jax.random.fold_in(_gk, 16), (3125,), 0, 3, jnp.int32)
        return (x, src, dst, edge_attr_64, edge_type_4, edge_weight, node_type_3)
    x, src, dst, edge_attr_64, edge_type_4, edge_weight, node_type_3 = _rec_inputs()

    def _L0_gnn_setup():
        import jax, jax.numpy as jnp
        import numpy as np
        N = 6250
        E = 40000
        D = 128
        R = 4
        ALPHA = 0.2

        def _lrelu(x):
            return jax.nn.leaky_relu(x, negative_slope=ALPHA)
        key = jax.random.key(seed)
        ks = jax.random.split(key, 14)
        s = 0.05
        return {'node_features': jax.random.normal(ks[0], (N, D), jnp.float32), 'edge_index': jax.random.randint(ks[1], (2, E), 0, N), 'edge_type': jax.random.randint(ks[2], (E,), 0, R), 'W_R': jax.random.normal(ks[3], (R, 2 * D, D), jnp.float32) * s, 'b_R': jax.random.normal(ks[4], (R, D), jnp.float32) * s, 'W_Q': jax.random.normal(ks[5], (R, D, D), jnp.float32) * s, 'b_Q': jax.random.normal(ks[6], (R, D), jnp.float32) * s, 'W_K': jax.random.normal(ks[7], (R, D, D), jnp.float32) * s, 'b_K': jax.random.normal(ks[8], (R, D), jnp.float32) * s, 'W_V': jax.random.normal(ks[9], (R, D, D), jnp.float32) * s, 'b_V': jax.random.normal(ks[10], (R, D), jnp.float32) * s, 'a_w': jax.random.normal(ks[11], (2 * D, 1), jnp.float32) * s, 'a_b': jax.random.normal(ks[12], (1,), jnp.float32) * s}
    _L0_gnn_all = _L0_gnn_setup()
    _L0_gnn_in = {k: v for k, v in _L0_gnn_all.items() if k in ('W_R', 'b_R', 'W_Q', 'b_Q', 'W_K', 'b_K', 'W_V', 'b_V', 'a_w', 'a_b')}
    del _L0_gnn_all

    def _L1_gnn_setup():
        import jax, jax.numpy as jnp
        import numpy as np
        N_NODES = 3125
        N_EDGES = 50000
        HIDDEN = 128
        REL = 64

        def _layer_norm(x, gamma, beta, eps=1e-05):
            mu = jnp.mean(x, axis=-1, keepdims=True)
            var = jnp.mean(jnp.square(x - mu), axis=-1, keepdims=True)
            return (x - mu) * jax.lax.rsqrt(var + eps) * gamma + beta
        key = jax.random.key(seed)
        ks = jax.random.split(key, 12)
        s = lambda fan_in: 1.0 / np.sqrt(fan_in)
        inp = {'node_states': jax.random.normal(ks[0], (N_NODES, HIDDEN), dtype=jnp.float32), 'edge_index': jax.random.randint(ks[1], (2, N_EDGES), 0, N_NODES, dtype=jnp.int64), 'edge_rel_emb': jax.random.normal(ks[2], (N_EDGES, REL), dtype=jnp.float32), 'W1': jax.random.uniform(ks[3], (2 * HIDDEN + REL, HIDDEN), jnp.float32, -s(2 * HIDDEN + REL), s(2 * HIDDEN + REL)), 'b1': jax.random.uniform(ks[4], (HIDDEN,), jnp.float32, -s(2 * HIDDEN + REL), s(2 * HIDDEN + REL)), 'W2': jax.random.uniform(ks[5], (HIDDEN, HIDDEN), jnp.float32, -s(HIDDEN), s(HIDDEN)), 'b2': jax.random.uniform(ks[6], (HIDDEN,), jnp.float32, -s(HIDDEN), s(HIDDEN)), 'Wn': jax.random.uniform(ks[7], (HIDDEN, HIDDEN), jnp.float32, -s(HIDDEN), s(HIDDEN)), 'bn': jax.random.uniform(ks[8], (HIDDEN,), jnp.float32, -s(HIDDEN), s(HIDDEN)), 'gamma': jnp.ones((HIDDEN,), jnp.float32), 'beta': jnp.zeros((HIDDEN,), jnp.float32)}
        return inp
    _L1_gnn_all = _L1_gnn_setup()
    _L1_gnn_in = {k: v for k, v in _L1_gnn_all.items() if k in ('W1', 'b1', 'W2', 'b2', 'Wn', 'bn', 'gamma', 'beta')}
    del _L1_gnn_all

    def _L2_gnn_setup():
        import jax, jax.numpy as jnp
        import numpy as np
        EPS = 1e-05

        def typed_linear(x, types, W):
            out = jnp.zeros((x.shape[0], W.shape[2]), x.dtype)
            for t in range(W.shape[0]):
                out = jnp.where((types == t)[:, None], x @ W[t], out)
            return out

        def layer_norm(x, g, b):
            mu = jnp.mean(x, axis=-1, keepdims=True)
            var = jnp.mean((x - mu) ** 2, axis=-1, keepdims=True)
            return (x - mu) * jax.lax.rsqrt(var + EPS) * g + b
        key = jax.random.key(seed)
        ks = jax.random.split(key, 16)
        N, E, D, H, Dh, T, C = (1250, 20000, 128, 8, 16, 3, 64)
        s = 0.05
        return {'x': jax.random.normal(ks[0], (N, D), jnp.float32), 'global_context': jax.random.normal(ks[1], (C,), jnp.float32), 'Wk': jax.random.normal(ks[2], (T, D, H * Dh), jnp.float32) * s, 'Wq': jax.random.normal(ks[3], (T, D, H * Dh), jnp.float32) * s, 'Wv': jax.random.normal(ks[4], (T, D, H * Dh), jnp.float32) * s, 'rel_att': jax.random.normal(ks[5], (H, Dh, Dh), jnp.float32) * s, 'rel_msg': jax.random.normal(ks[6], (H, Dh, Dh), jnp.float32) * s, 'rel_pri': jnp.ones((H,), jnp.float32), 'Wa': jax.random.normal(ks[7], (T, H * Dh, H * Dh), jnp.float32) * s, 'skip': jnp.ones((T,), jnp.float32), 'ln_g': jnp.ones((H * Dh,), jnp.float32), 'ln_b': jnp.zeros((H * Dh,), jnp.float32), 'film_w': jax.random.normal(ks[8], (C, 2 * D), jnp.float32) * s, 'film_b': jnp.zeros((2 * D,), jnp.float32), 'ntype': jax.random.randint(ks[9], (N,), 0, T, jnp.int32), 'src': jax.random.randint(ks[10], (E,), 0, N, jnp.int32), 'dst': jax.random.randint(ks[11], (E,), 0, N, jnp.int32)}
    _L2_gnn_all = _L2_gnn_setup()
    _L2_gnn_in = {k: v for k, v in _L2_gnn_all.items() if k in ('global_context', 'Wk', 'Wq', 'Wv', 'rel_att', 'rel_msg', 'rel_pri', 'Wa', 'skip', 'ln_g', 'ln_b', 'film_w', 'film_b')}
    del _L2_gnn_all

    def _L3_gnn_setup():
        import jax, jax.numpy as jnp
        import numpy as np
        N_NODES = 6250
        D = 128
        N_EDGES = 100000
        N_LAYERS = 3

        def _spmm(vals, rows, cols, x, n):
            gathered = vals[:, None] * x[cols]
            return jax.ops.segment_sum(gathered, rows, num_segments=n)
        key = jax.random.key(seed)
        k1, k2, k3, k4 = jax.random.split(key, 4)
        emb = jax.random.normal(k1, (N_NODES, D), dtype=jnp.float32)
        vals = jax.random.uniform(k2, (N_EDGES,), dtype=jnp.float32)
        rows = jax.random.randint(k3, (N_EDGES,), 0, N_NODES, dtype=jnp.int64 if jax.config.jax_enable_x64 else jnp.int32)
        cols = jax.random.randint(k4, (N_EDGES,), 0, N_NODES, dtype=jnp.int64 if jax.config.jax_enable_x64 else jnp.int32)
        return {'emb': emb, 'vals': vals, 'rows': rows, 'cols': cols}
    _L3_gnn_all = _L3_gnn_setup()
    _L3_gnn_in = {k: v for k, v in _L3_gnn_all.items() if k in ()}
    del _L3_gnn_all
    return {'x': x, 'src': src, 'dst': dst, 'edge_attr_64': edge_attr_64, 'edge_type_4': edge_type_4, 'edge_weight': edge_weight, 'node_type_3': node_type_3, 'L0_gnn_W_R': _L0_gnn_in['W_R'], 'L0_gnn_b_R': _L0_gnn_in['b_R'], 'L0_gnn_W_Q': _L0_gnn_in['W_Q'], 'L0_gnn_b_Q': _L0_gnn_in['b_Q'], 'L0_gnn_W_K': _L0_gnn_in['W_K'], 'L0_gnn_b_K': _L0_gnn_in['b_K'], 'L0_gnn_W_V': _L0_gnn_in['W_V'], 'L0_gnn_b_V': _L0_gnn_in['b_V'], 'L0_gnn_a_w': _L0_gnn_in['a_w'], 'L0_gnn_a_b': _L0_gnn_in['a_b'], 'L1_gnn_W1': _L1_gnn_in['W1'], 'L1_gnn_b1': _L1_gnn_in['b1'], 'L1_gnn_W2': _L1_gnn_in['W2'], 'L1_gnn_b2': _L1_gnn_in['b2'], 'L1_gnn_Wn': _L1_gnn_in['Wn'], 'L1_gnn_bn': _L1_gnn_in['bn'], 'L1_gnn_gamma': _L1_gnn_in['gamma'], 'L1_gnn_beta': _L1_gnn_in['beta'], 'L2_gnn_global_context': _L2_gnn_in['global_context'], 'L2_gnn_Wk': _L2_gnn_in['Wk'], 'L2_gnn_Wq': _L2_gnn_in['Wq'], 'L2_gnn_Wv': _L2_gnn_in['Wv'], 'L2_gnn_rel_att': _L2_gnn_in['rel_att'], 'L2_gnn_rel_msg': _L2_gnn_in['rel_msg'], 'L2_gnn_rel_pri': _L2_gnn_in['rel_pri'], 'L2_gnn_Wa': _L2_gnn_in['Wa'], 'L2_gnn_skip': _L2_gnn_in['skip'], 'L2_gnn_ln_g': _L2_gnn_in['ln_g'], 'L2_gnn_ln_b': _L2_gnn_in['ln_b'], 'L2_gnn_film_w': _L2_gnn_in['film_w'], 'L2_gnn_film_b': _L2_gnn_in['film_b']}

def reference(x, src, dst, edge_attr_64, edge_type_4, edge_weight, node_type_3, L0_gnn_W_R, L0_gnn_b_R, L0_gnn_W_Q, L0_gnn_b_Q, L0_gnn_W_K, L0_gnn_b_K, L0_gnn_W_V, L0_gnn_b_V, L0_gnn_a_w, L0_gnn_a_b, L1_gnn_W1, L1_gnn_b1, L1_gnn_W2, L1_gnn_b2, L1_gnn_Wn, L1_gnn_bn, L1_gnn_gamma, L1_gnn_beta, L2_gnn_global_context, L2_gnn_Wk, L2_gnn_Wq, L2_gnn_Wv, L2_gnn_rel_att, L2_gnn_rel_msg, L2_gnn_rel_pri, L2_gnn_Wa, L2_gnn_skip, L2_gnn_ln_g, L2_gnn_ln_b, L2_gnn_film_w, L2_gnn_film_b):
    import jax
    import jax.numpy as jnp

    def _L0_gnn_ref(node_features, edge_index, edge_type, W_R, b_R, W_Q, b_Q, W_K, b_K, W_V, b_V, a_w, a_b):
        import jax, jax.numpy as jnp
        import numpy as np
        N = 6250
        E = 40000
        D = 128
        R = 4
        ALPHA = 0.2

        def _lrelu(x):
            return jax.nn.leaky_relu(x, negative_slope=ALPHA)
        num_nodes = node_features.shape[0]
        src, tgt = (edge_index[0], edge_index[1])
        rel_in = jnp.concatenate([node_features[src], node_features[tgt]], axis=1)
        h = jnp.zeros_like(node_features)
        for r in range(R):
            mask = edge_type == r
            rel_t = _lrelu(rel_in @ W_R[r] + b_R[r])
            Q = rel_t @ W_Q[r] + b_Q[r]
            K = rel_t @ W_K[r] + b_K[r]
            V = rel_t @ W_V[r] + b_V[r]
            e = _lrelu(jnp.concatenate([Q, K], axis=1) @ a_w + a_b)[:, 0]
            e_m = jnp.where(mask, e, -1e+30)
            seg_max = jax.ops.segment_max(e_m, tgt, num_segments=num_nodes)
            seg_max = jnp.where(seg_max > -1e+29, seg_max, 0.0)
            ex = jnp.where(mask, jnp.exp(e - seg_max[tgt]), 0.0)
            denom = jax.ops.segment_sum(ex, tgt, num_segments=num_nodes)
            attn = ex / jnp.maximum(denom[tgt], 1e-16)
            h = h + jax.ops.segment_sum(V * attn[:, None], tgt, num_segments=num_nodes)
        return jax.nn.elu(h)

    def _L1_gnn_ref(node_states, edge_index, edge_rel_emb, W1, b1, W2, b2, Wn, bn, gamma, beta):
        import jax, jax.numpy as jnp
        import numpy as np
        N_NODES = 3125
        N_EDGES = 50000
        HIDDEN = 128
        REL = 64

        def _layer_norm(x, gamma, beta, eps=1e-05):
            mu = jnp.mean(x, axis=-1, keepdims=True)
            var = jnp.mean(jnp.square(x - mu), axis=-1, keepdims=True)
            return (x - mu) * jax.lax.rsqrt(var + eps) * gamma + beta
        src, dst = (edge_index[0], edge_index[1])
        m_input = jnp.concatenate([node_states[src], node_states[dst], edge_rel_emb], axis=-1)
        h = jax.nn.relu(m_input @ W1 + b1)
        messages = jax.nn.relu(h @ W2 + b2)
        agg = jax.ops.segment_sum(messages, dst, num_segments=node_states.shape[0])
        updated = node_states + jax.nn.relu(agg @ Wn + bn)
        return _layer_norm(updated, gamma, beta)

    def _L2_gnn_ref(x, global_context, Wk, Wq, Wv, rel_att, rel_msg, rel_pri, Wa, skip, ln_g, ln_b, film_w, film_b, ntype, src, dst):
        import jax, jax.numpy as jnp
        import numpy as np
        EPS = 1e-05

        def typed_linear(x, types, W):
            out = jnp.zeros((x.shape[0], W.shape[2]), x.dtype)
            for t in range(W.shape[0]):
                out = jnp.where((types == t)[:, None], x @ W[t], out)
            return out

        def layer_norm(x, g, b):
            mu = jnp.mean(x, axis=-1, keepdims=True)
            var = jnp.mean((x - mu) ** 2, axis=-1, keepdims=True)
            return (x - mu) * jax.lax.rsqrt(var + EPS) * g + b
        N, D = x.shape
        H, Dh, _ = rel_att.shape
        inv_sqrt_d = 1.0 / jnp.sqrt(jnp.asarray(Dh, x.dtype))
        k = typed_linear(x, ntype, Wk).reshape(N, H, Dh)
        q = typed_linear(x, ntype, Wq).reshape(N, H, Dh)
        v = typed_linear(x, ntype, Wv).reshape(N, H, Dh)
        kw = jnp.einsum('ehd,hdo->eho', k[src], rel_att)
        a = jnp.einsum('eho,eho->eh', kw, q[dst]) * rel_pri * inv_sqrt_d
        m = jnp.einsum('ehd,hdo->eho', v[src], rel_msg)
        amax = jax.ops.segment_max(a, dst, num_segments=N)
        ae = jnp.exp(a - amax[dst])
        asum = jax.ops.segment_sum(ae, dst, num_segments=N)
        attn = ae / asum[dst]
        h_agg = jax.ops.segment_sum(m * attn[..., None], dst, num_segments=N).reshape(N, H * Dh)
        h = typed_linear(h_agg, ntype, Wa)
        alpha = jax.nn.sigmoid(skip)[ntype][:, None]
        h = h * alpha + x * (1.0 - alpha)
        h = layer_norm(h, ln_g, ln_b)
        h = h + x
        gb = global_context @ film_w + film_b
        gamma, beta = (gb[:D], gb[D:])
        return gamma[None, :] * h + beta[None, :]

    def _L3_gnn_ref(emb, vals, rows, cols):
        import jax, jax.numpy as jnp
        import numpy as np
        N_NODES = 6250
        D = 128
        N_EDGES = 100000
        N_LAYERS = 3

        def _spmm(vals, rows, cols, x, n):
            gathered = vals[:, None] * x[cols]
            return jax.ops.segment_sum(gathered, rows, num_segments=n)
        n = emb.shape[0]
        side = _spmm(vals, rows, cols, emb, n)
        light_out = (emb + N_LAYERS * side) / (N_LAYERS + 1)
        return light_out
    edge_index = jnp.stack([src, dst])
    x = _layernorm(x + _L0_gnn_ref(x, edge_index, edge_type_4, L0_gnn_W_R, L0_gnn_b_R, L0_gnn_W_Q, L0_gnn_b_Q, L0_gnn_W_K, L0_gnn_b_K, L0_gnn_W_V, L0_gnn_b_V, L0_gnn_a_w, L0_gnn_a_b), axis=-1)
    x = _layernorm(x + _L1_gnn_ref(x, edge_index, edge_attr_64, L1_gnn_W1, L1_gnn_b1, L1_gnn_W2, L1_gnn_b2, L1_gnn_Wn, L1_gnn_bn, L1_gnn_gamma, L1_gnn_beta), axis=-1)
    x = _layernorm(x + _L2_gnn_ref(x, L2_gnn_global_context, L2_gnn_Wk, L2_gnn_Wq, L2_gnn_Wv, L2_gnn_rel_att, L2_gnn_rel_msg, L2_gnn_rel_pri, L2_gnn_Wa, L2_gnn_skip, L2_gnn_ln_g, L2_gnn_ln_b, L2_gnn_film_w, L2_gnn_film_b, node_type_3, src, dst), axis=-1)
    x = _layernorm(x + _L3_gnn_ref(x, edge_weight, src, dst), axis=-1)
    return x

_drawn_inputs = setup_inputs


def setup_inputs(seed=0):
    import zlib

    import numpy as np

    out = dict(_drawn_inputs(seed))
    spreads = {'L1_gnn_gamma': (1.0, 0.2),
     'L1_gnn_beta': (0.0, 0.1),
     'L2_gnn_rel_pri': (1.0, 0.6),
     'L2_gnn_skip': (1.0, 0.6),
     'L2_gnn_ln_g': (1.0, 0.2),
     'L2_gnn_ln_b': (0.0, 0.1),
     'L2_gnn_film_b': (0.0, 0.1)}
    factors = {'L0_gnn_W_Q': 6.936,
     'L0_gnn_b_Q': 59.633,
     'L0_gnn_W_K': 7.526,
     'L0_gnn_b_K': 64.0,
     'L0_gnn_a_w': 5.586,
     'L2_gnn_Wk': 8.0,
     'L2_gnn_Wq': 8.0,
     'L2_gnn_Wv': 2.723,
     'L2_gnn_rel_att': 8.0}
    for name, (base, spread) in spreads.items():
        noise = np.random.default_rng([zlib.crc32(name.encode()), seed]).standard_normal(out[name].shape)
        drawn = base * np.exp(spread * noise) if base else spread * noise
        out[name] = jnp.asarray(drawn.astype(out[name].dtype))
    for name, factor in factors.items():
        out[name] = (out[name] * factor).astype(out[name].dtype)
    return out
```

```python
from contextlib import ExitStack

import concourse.bass as bass
from concourse import mybir
from concourse.alu_op_type import AluOpType as ALU

ACT = mybir.ActivationFunctionType
AX = mybir.AxisListType
F32 = mybir.dt.float32
I32 = mybir.dt.int32

P = 128
N = 3125
D = 128
E = 53125
J = 4
GE = J * P
Q = -(-E // GE)
T = Q * J
R = 4
H, DH = 8, 16
NT = 3
REL = 64
CTX = 64
K4 = 4
NGRP = -(-(N + 1 + P) // GE)
NP = NGRP * GE
WIN = 32
KEYS = WIN * R
EPS = 1e-5
BIG = 3e30
NEG = 1e30
COPIES = 8


def build(nc, x, src, dst, edge_attr_64, edge_type_4, edge_weight, node_type_3,
          L0_gnn_W_R, L0_gnn_b_R, L0_gnn_W_Q, L0_gnn_b_Q, L0_gnn_W_K, L0_gnn_b_K, L0_gnn_W_V, L0_gnn_b_V,
          L0_gnn_a_w, L0_gnn_a_b, L1_gnn_W1, L1_gnn_b1, L1_gnn_W2, L1_gnn_b2, L1_gnn_Wn, L1_gnn_bn,
          L1_gnn_gamma, L1_gnn_beta, L2_gnn_global_context, L2_gnn_Wk, L2_gnn_Wq, L2_gnn_Wv,
          L2_gnn_rel_att, L2_gnn_rel_msg, L2_gnn_rel_pri, L2_gnn_Wa, L2_gnn_skip, L2_gnn_ln_g,
          L2_gnn_ln_b, L2_gnn_film_w, L2_gnn_film_b, out):
    top = ExitStack()

    def dram(name, shape, dt=F32):
        return nc.dram_tensor(name, shape, dt, kind="Internal").ap()

    xs = [dram(f"x_layer{n}", [NP, D]) for n in range(4)]
    type_pad = dram("node_type_padded", [NP], I32)
    base_row = dram("tile_base", [T], I32)
    src_row = dram("src_padded", [T * P])
    rel_table = dram("rel_src_table", [NP * R, D])
    rel_window = dram("rel_dst_table", [NP * R, D])
    rel_edges = dram("rel_edges", [Q, P, J * D])
    msg_table = dram("msg_src_table", [NP, D])
    msg_window = dram("msg_dst_table", [NP, D])
    kv_table = dram("kv_table", [NP, 2 * D])
    q_window = dram("q_table", [NP, D])
    v_edges = dram("v_edges", [Q, P, J * D])
    side = [dram(f"side_{c}", [N + P, D]) for c in range(COPIES)]

    def sb(name, shape, dt=F32):
        return top.enter_context(nc.sbuf_tensor(name, shape, dt))

    ident = sb("ident", [P, P])
    iota = sb("iota", [P, R * P])
    ones = sb("ones", [P, P])
    key_t = sb("key_t", [P, T])
    dl_t = sb("dl_t", [P, T])
    rel_idx = sb("rel_idx", [P, T], I32)
    src_idx = sb("src_idx", [P, T], I32)
    src_t = sb("src_t", [P, T])
    w_t = sb("w_t", [P, T])
    attn_t = sb("attn_t", [P, T])
    base_sb = sb("base_sb", [1, T], I32)
    typ_s = sb("typ_s", [Q, GE])
    pen = sb("pen", [Q, GE + 1])
    same = sb("same", [Q, GE + 1])
    in_first = sb("in_first", [Q, GE])
    in_last = sb("in_last", [Q, GE])
    pen_first = sb("pen_first", [Q, GE])
    pen_last = sb("pen_last", [Q, GE])
    cont = sb("cont", [H, Q + 1])
    through = sb("through", [H, Q + 2])
    wide = sb("wide", [1, 1], I32)

    def window_base(engines, q, j):
        return nc.values_load(base_sb[0:1, bass.ds(q * J + j, 1)], engines=engines, min_val=0, max_val=N,
                              skip_runtime_bounds_check_because="dst is a node")

    def lay_out():
        with ExitStack() as ctx:
            def tmp(name, shape, dt=F32):
                return ctx.enter_context(nc.sbuf_tensor(name, shape, dt))

            def sem(name):
                return ctx.enter_context(nc.semaphore(name))

            src_i, dst_i, typ_i = (tmp(n, [Q, GE], I32) for n in ("src_i", "dst_i", "typ_i"))
            w_s, src_s, dst_s, dl_s, key_s, idx_s = (tmp(n, [Q, GE]) for n in
                                                      ("w_s", "src_s", "dst_s", "dl_s", "key_s", "idx_s"))
            base_i = tmp("base_i", [Q, J], I32)
            top_s = tmp("top_s", [Q, 1])
            ends = tmp("ends", [Q, 2, H])
            rows = tmp("rows", [H, 2, Q])
            zero_x = tmp("zero_x", [P, 4 * D])
            zero_i = tmp("zero_i", [NP - N, 1], I32) if NP - N <= P else tmp("zero_i", [1, NP - N], I32)
            zeros_set, edges_in, pads_in, made, moved, turned, stored = (sem(n) for n in
                ("zeros_set", "edges_in", "pads_in", "made", "moved", "turned", "stored"))
            ps = [ctx.enter_context(nc.psum_tensor(f"lay_ps{i}", [P, J, Q], F32)) for i in range(5)]
            ps_row = ctx.enter_context(nc.psum_tensor("lay_row", [H, 2, P], F32))
            ps_top = ctx.enter_context(nc.psum_tensor("lay_top", [1, P], F32))
            last = E - (Q - 1) * GE

            with nc.Block() as block:
                @block.gpsimd
                def _(pool):
                    pool.memset(src_i[:, :], 0).then_inc(zeros_set, 1)
                    pool.memset(dst_i[:, :], N).then_inc(zeros_set, 1)
                    pool.memset(typ_i[:, :], 0).then_inc(zeros_set, 1)
                    pool.memset(w_s[:, :], 0.0).then_inc(zeros_set, 1)
                    pool.memset(zero_x[:, :], 0.0).then_inc(zeros_set, 1)
                    pool.memset(zero_i[:, :], 0).then_inc(zeros_set, 1)
                    pool.memset(ones[:, :], 1.0).then_inc(zeros_set, 1)
                    pool.memset(ident[:, :], 0.0).then_inc(made, 1)
                    pool.wait_ge(made, 1)
                    pool.affine_select(out=ident[:, :], in_=ident[:, :], compare_op=ALU.not_equal, fill=1.0,
                                       base=0, pattern=[[-1, P]], channel_multiplier=1).then_inc(made, 1)
                    pool.iota(iota[:, :], [[1, R * P]], base=0, channel_multiplier=0,
                              allow_small_or_imprecise_dtypes=True).then_inc(made, 1)

                @block.sync
                def _(sp):
                    sp.wait_ge(zeros_set, 7)
                    for to, frm in ((src_i, src), (dst_i, dst), (typ_i, edge_type_4), (w_s, edge_weight)):
                        sp.dma_start(to[0:Q - 1, :], frm[0:(Q - 1) * GE].rearrange("(q e) -> q e", e=GE)).then_inc(edges_in, 16)
                        sp.dma_start(to[Q - 1:Q, 0:last], frm[(Q - 1) * GE:E].rearrange("(q e) -> q e", q=1)).then_inc(edges_in, 16)
                    sp.dma_start(xs[0][0:N, :], x).then_inc(pads_in, 16)
                    a = N
                    while a < NP:
                        n = min(P, NP - a)
                        sp.dma_start(xs[0][a:a + n, :], zero_x[0:n, 0:D]).then_inc(pads_in, 16)
                        a += n
                    sp.dma_start(type_pad[0:N].rearrange("(a n) -> a n", a=5), node_type_3.rearrange("(a n) -> a n", a=5)).then_inc(pads_in, 16)
                    sp.dma_start(type_pad[N:NP].rearrange("(a n) -> a n", a=1), zero_i[:, :]).then_inc(pads_in, 16)
                    n_pads = 3 + -(-(NP - N) // P)
                    for c in range(COPIES):
                        a = 0
                        full = (N // (4 * P)) * 4 * P
                        while a < full:
                            sp.dma_start(side[c][a:a + 4 * P, :].rearrange("(p k) f -> p (k f)", k=4), zero_x[:, :]).then_inc(pads_in, 16)
                            a += 4 * P
                            n_pads += 1
                        while a < N + P:
                            n = min(P, N + P - a)
                            sp.dma_start(side[c][a:a + n, :], zero_x[0:n, 0:D]).then_inc(pads_in, 16)
                            a += n
                            n_pads += 1
                    sp.wait_ge(moved, 2)
                    sp.dma_start(base_row.rearrange("(q j) -> q j", j=J), base_i[:, :]).then_inc(stored, 16)
                    sp.dma_start(src_row.rearrange("(q e) -> q e", e=GE), src_s[:, :]).then_inc(stored, 16)
                    sp.wait_ge(stored, 32)
                    sp.dma_start(base_sb[:, :], base_row.rearrange("(a t) -> a t", a=1)).then_inc(stored, 16)
                    sp.wait_ge(stored, 48)
                    sp.wait_ge(pads_in, 16 * n_pads)

                @block.vector
                def _(dve):
                    dve.wait_ge(edges_in, 16 * 8)
                    dve.tensor_copy(src_s[:, :], src_i[:, :]).then_inc(moved, 1)
                    dve.tensor_copy(base_i[:, :], dst_i[:, ::P]).then_inc(moved, 1)
                    dve.tensor_copy(dst_s[:, :], dst_i[:, :]).then_inc(moved, 1)
                    dve.tensor_copy(typ_s[:, :], typ_i[:, :]).then_inc(moved, 1)
                    dve.wait_ge(moved, 4)
                    tiles = lambda a: a[:, :].rearrange("q (j e) -> q j e", e=P)
                    dve.tensor_tensor(tiles(dl_s), tiles(dst_s), tiles(dst_s)[:, :, 0:1].to_broadcast([Q, J, P]),
                                      ALU.subtract).then_inc(moved, 1)
                    dve.scalar_tensor_tensor(out=idx_s[:, :], in0=src_s[:, :], scalar=float(R), in1=typ_s[:, :],
                                             op0=ALU.mult, op1=ALU.add).then_inc(moved, 1)
                    dve.wait_ge(moved, 5)
                    dve.scalar_tensor_tensor(out=key_s[:, :], in0=dl_s[:, :], scalar=float(R), in1=typ_s[:, :],
                                             op0=ALU.mult, op1=ALU.add).then_inc(moved, 1)
                    dve.tensor_reduce(top_s[:, :], dl_s[:, :], AX.X, ALU.max).then_inc(moved, 1)
                    dve.memset(same[:, :], 0.0).then_inc(moved, 1)
                    dve.wait_ge(moved, 9)
                    dve.tensor_tensor(same[:, 1:GE], dst_s[:, 1:GE], dst_s[:, 0:GE - 1], ALU.is_equal).then_inc(moved, 1)
                    dve.tensor_scalar(in_first[:, :], dst_s[:, :], dst_s[:, 0:1], None, ALU.is_equal).then_inc(moved, 1)
                    dve.tensor_scalar(in_last[:, :], dst_s[:, :], dst_s[:, GE - 1:GE], None, ALU.is_equal).then_inc(moved, 1)
                    dve.tensor_copy(ends[:, 0, :], dst_s[:, 0:1].to_broadcast([Q, H])).then_inc(moved, 1)
                    dve.tensor_copy(ends[:, 1, :], dst_s[:, GE - 1:GE].to_broadcast([Q, H])).then_inc(moved, 1)
                    dve.wait_ge(moved, 14)
                    for to, frm in ((pen, same), (pen_first, in_first), (pen_last, in_last)):
                        dve.tensor_scalar(to[:, :], frm[:, :], 1.0, BIG, ALU.subtract, ALU.mult).then_inc(moved, 1)
                    for n, to in enumerate((dl_t, key_t, src_t, rel_idx, w_t)):
                        dve.wait_ge(turned, n + 1)
                        dve.tensor_copy(to[:, :].rearrange("p (q j) -> p j q", j=J), ps[n][:, :, :]).then_inc(moved, 1)
                    dve.wait_ge(turned, 6)
                    dve.tensor_copy(rows[:, :, :], ps_row[:, :, 0:Q]).then_inc(moved, 1)
                    dve.memset(cont[:, :], 0.0).then_inc(moved, 1)
                    dve.memset(through[:, :], 0.0).then_inc(moved, 1)
                    dve.wait_ge(moved, 25)
                    dve.tensor_copy(src_idx[:, :], src_t[:, :]).then_inc(moved, 1)
                    dve.tensor_tensor(cont[:, 1:Q], rows[:, 0, 1:Q], rows[:, 1, 0:Q - 1], ALU.is_equal).then_inc(moved, 1)
                    dve.tensor_tensor(through[:, 1:Q + 1], rows[:, 0, :], rows[:, 1, :], ALU.is_equal).then_inc(moved, 1)
                    dve.wait_ge(turned, 7)
                    dve.tensor_reduce(wide[:, :], ps_top[:, 0:Q], AX.X, ALU.max).then_inc(moved, 1)

                @block.tensor
                def _(pe):
                    pe.wait_ge(made, 2)
                    for n, (frm, ready) in enumerate(((dl_s, 5), (key_s, 7), (src_s, 7), (idx_s, 7), (w_s, 7))):
                        pe.wait_ge(moved, ready)
                        for j in range(J):
                            turn = pe.transpose(ps[n][:, j, :], frm[:, j * P:(j + 1) * P], ident[0:Q, 0:Q])
                        turn.then_inc(turned, 1)
                    pe.wait_ge(moved, 14)
                    for n in range(2):
                        turn = pe.transpose(ps_row[:, n, 0:Q], ends[:, n, :], ident[0:Q, 0:Q])
                    turn.then_inc(turned, 1)
                    pe.transpose(ps_top[:, 0:Q], top_s[:, :], ident[0:Q, 0:Q]).then_inc(turned, 1)


    def rows_of(table, g, width):
        flat = table.rearrange("(a k) f -> a (k f)", k=K4)
        return flat[bass.ds(g * P, P), :].rearrange("p (k f) -> p k f", f=width)

    def across(vector, n, parts=P):
        return vector.rearrange("(a n) -> a n", a=1).broadcast_to([parts, n])

    def scope(ctx, tag):
        taken = []

        def sem(name):
            taken.append(nc.alloc_semaphore(f"{tag}_{name}"))
            return taken[-1]

        def give_back():
            nc.clear_and_free_semaphores(taken)
            nc.all_engine_barrier()

        ctx.callback(give_back)
        return (lambda name, shape, dt=F32: ctx.enter_context(nc.sbuf_tensor(f"{tag}_{name}", shape, dt)),
                lambda name, shape: ctx.enter_context(nc.psum_tensor(f"{tag}_{name}", shape, F32)),
                sem,
                lambda name: [sem(f"{name}{s}") for s in range(2)])

    def both_ways(eng, program):
        reach = nc.values_load(wide[0:1, 0:1], engines=[eng.engine], min_val=0, max_val=P - 1,
                               skip_runtime_bounds_check_because="every node has an edge of its own")
        with eng.If(reach < WIN):
            program(1)
        with eng.Else():
            program(P // WIN)

    def pairs(eng, body):
        body(0, True)
        with eng.Fori(1, Q // 2) as i:
            body(i, False)

    def rel_tables(u_keys, e_bias, agg, share):
        with ExitStack() as ctx:
            tmp, psum, sem, pair = scope(ctx, "t0")
            w_up, w_low = tmp("w_up", [P, R, D]), tmp("w_low", [P, R, D])
            b_all = tmp("b_all", [P, R * D])
            wq, wk = tmp("wq", [P, R, D]), tmp("wk", [P, R, D])
            a_all = tmp("a_all", [P, 2 * D])
            bq, bk = tmp("bq", [Q, R, D]), tmp("bk", [Q, R, D])
            ab = tmp("ab", [Q, 1])
            junk = tmp("junk", [P, 4 * R, D])
            u_part, u_col = tmp("u_part", [P, 2, R]), tmp("u_col", [P, R])
            c_part = tmp("c_part", [Q, 2, R])
            u_rows, spread = tmp("u_rows", [R, D]), tmp("spread", [R, P])
            xg, xt = tmp("xg", [P, K4, D]), tmp("xt", [P, K4, D])
            up, low = tmp("up", [P, K4, R * D]), tmp("low", [P, K4, R * D])
            ps_x, ps_u = psum("ps_x", [P, K4, D]), psum("ps_u", [P, D])
            ps_up = [psum(f"ps_up{n}", [P, R * D]) for n in range(2)]
            ps_low = [psum(f"ps_low{n}", [P, R * D]) for n in range(2)]
            weights_in, dots, u_mm, u_copied, x_in, turned, xt_ready, up_mm, low_mm, up_out, low_out, up_st, low_st, cleared = (
                sem(n) for n in ("weights_in", "dots", "u_mm", "u_copied", "x_in", "turned", "xt_ready", "up_mm", "low_mm",
                                 "up_out", "low_out", "up_st", "low_st", "cleared"))

            with nc.Block() as block:
                @block.sync
                def _(sp):
                    for to, frm in ((w_up, L0_gnn_W_R[:, 0:D, :]), (w_low, L0_gnn_W_R[:, D:2 * D, :]), (wq, L0_gnn_W_Q), (wk, L0_gnn_W_K)):
                        sp.dma_start(to[:, :, :], frm.rearrange("r f g -> f r g")).then_inc(weights_in, 16)
                    sp.dma_start(b_all[:, :], across(L0_gnn_b_R.rearrange("r f -> (r f)"), R * D)).then_inc(weights_in, 16)
                    sp.dma_start(a_all[:, :], across(L0_gnn_a_w.rearrange("f a -> (f a)"), 2 * D)).then_inc(weights_in, 16)
                    for to, frm in ((bq, L0_gnn_b_Q), (bk, L0_gnn_b_K)):
                        sp.dma_start(to[:, :, :].rearrange("q r f -> q (r f)"), across(frm.rearrange("r f -> (r f)"), R * D, Q)).then_inc(weights_in, 16)
                    sp.dma_start(ab[:, :], across(L0_gnn_a_b, 1, Q)).then_inc(weights_in, 16)
                    sp.dma_start(xg[:, :, :], rows_of(xs[0], 0, D)).then_inc(x_in, 16)

                    def store(g):
                        sp.wait_ge(up_out, 4 * (g + 1))
                        sp.dma_start(rows_of(rel_table.rearrange("(n r) f -> n (r f)", r=R), g, R * D), up[:, :, :]).then_inc(up_st, 16)
                        sp.wait_ge(low_out, 4 * (g + 1))
                        sp.dma_start(rows_of(rel_window.rearrange("(n r) f -> n (r f)", r=R), g, R * D), low[:, :, :]).then_inc(low_st, 16)

                    with sp.Fori(0, NGRP - 1) as g:
                        sp.wait_ge(turned, g + 1)
                        sp.dma_start(xg[:, :, :], rows_of(xs[0], g + 1, D)).then_inc(x_in, 16)
                        store(g)
                    store(NGRP - 1)
                    sp.wait_ge(up_st, 16 * NGRP)
                    sp.wait_ge(low_st, 16 * NGRP)

                @block.gpsimd
                def _(pool):
                    pool.memset(agg[:, :], 0.0).then_inc(cleared, 1)
                    pool.memset(share[:, :], 0.0).then_inc(cleared, 1)

                @block.tensor
                def _(pe):
                    pe.wait_ge(dots, 1)
                    pe.transpose(ps_u[0:R, :], u_col[:, :], ident[:, :]).then_inc(u_mm, 1)
                    pe.wait_ge(u_copied, 2)
                    pe.matmul(ps_u[:, :], spread[:, :], u_rows[:, :], start=True, stop=True).then_inc(u_mm, 1)
                    pe.wait_ge(weights_in, 16 * 9)
                    with pe.Fori(0, NGRP) as g:
                        pe.wait_ge(x_in, 16 * (g + 1))
                        pe.wait_ge(xt_ready, g)
                        for k in range(K4):
                            turn = pe.transpose(ps_x[:, k, :], xg[:, k, :], ident[:, :])
                        turn.then_inc(turned, 1)
                        pe.wait_ge(xt_ready, g + 1)
                        for k in range(K4):
                            pe.wait_ge(up_out, 4 * g + max(k - 1, 0))
                            pe.matmul(ps_up[k % 2][:, :], xt[:, k, :], w_up[:, :, :].rearrange("f r g -> f (r g)"), start=True, stop=True).then_inc(up_mm, 1)
                            pe.wait_ge(low_out, 4 * g + max(k - 1, 0))
                            pe.matmul(ps_low[k % 2][:, :], xt[:, k, :], w_low[:, :, :].rearrange("f r g -> f (r g)"), start=True, stop=True).then_inc(low_mm, 1)

                @block.scalar
                def _(act):
                    with act.Fori(0, NGRP) as g:
                        act.wait_ge(turned, g + 1)
                        act.wait_ge(low_mm, 4 * g)
                        act.copy(xt[:, :, :], ps_x[:, :, :]).then_inc(xt_ready, 1)
                        act.wait_ge(up_st, 16 * g)
                        for k in range(K4):
                            act.wait_ge(up_mm, 4 * g + k + 1)
                            act.copy(up[:, k, :], ps_up[k % 2][:, :]).then_inc(up_out, 1)

                @block.vector
                def _(dve):
                    dve.wait_ge(weights_in, 16 * 9)
                    for n, (w, b) in enumerate(((wq, bq), (wk, bk))):
                        for r in range(R):
                            dve.tensor_tensor_reduce(junk[:, 2 * R * n + r, :], w[:, r, :], a_all[:, n * D:(n + 1) * D], 1.0, 0.0,
                                                     ALU.mult, ALU.add, u_part[:, n, r:r + 1]).then_inc(cleared, 1)
                            dve.tensor_tensor_reduce(junk[0:Q, 2 * R * n + R + r, :], b[:, r, :], a_all[0:Q, n * D:(n + 1) * D], 1.0, 0.0,
                                                     ALU.mult, ALU.add, c_part[:, n, r:r + 1]).then_inc(cleared, 1)
                    dve.wait_ge(cleared, 2 + 4 * R)
                    dve.tensor_tensor(u_col[:, :], u_part[:, 0, :], u_part[:, 1, :], ALU.add).then_inc(dots, 1)
                    dve.tensor_tensor(e_bias[:, :], c_part[:, 0, :], c_part[:, 1, :], ALU.add).then_inc(dots, 1)
                    dve.wait_ge(dots, 2)
                    dve.tensor_scalar(e_bias[:, :], e_bias[:, :], ab[:, 0:1], None, ALU.add).then_inc(dots, 1)
                    dve.wait_ge(u_mm, 1)
                    dve.tensor_copy(u_rows[:, :], ps_u[0:R, :]).then_inc(u_copied, 1)
                    dve.tensor_copy(spread[:, :].rearrange("r (n c) -> r n c", c=R),
                                    ident[0:R, 0:R].unsqueeze(1).to_broadcast([R, WIN, R])).then_inc(u_copied, 1)
                    dve.wait_ge(u_mm, 2)
                    dve.tensor_copy(u_keys[:, :], ps_u[:, :]).then_inc(u_copied, 1)
                    with dve.Fori(0, NGRP) as g:
                        dve.wait_ge(low_st, 16 * g)
                        for k in range(K4):
                            dve.wait_ge(low_mm, 4 * g + k + 1)
                            dve.tensor_tensor(low[:, k, :], ps_low[k % 2][:, :], b_all[:, :], ALU.add).then_inc(low_out, 1)

    def rel_scores(u_keys, e_t):
        with ExitStack() as ctx:
            tmp, psum, sem, pair = scope(ctx, "e0")
            idx = tmp("idx", [P, 2, J], I32)
            gathered, window, onehot, spread, rel = (tmp(n, [P, 2, J, D]) for n in ("gathered", "window", "onehot", "spread", "rel"))
            junk = tmp("junk", [P, J, D])
            e_now = tmp("e_now", [P, 2, J])
            ps_t, ps_r, ps_u = ([psum(f"{n}{s}", [P, J, D]) for s in range(2)] for n in ("ps_t", "ps_r", "ps_u"))
            staged, src_in, win_in, marked, turned, copied, used, summed, rel_made, rel_st, e_made, dotted = (pair(n) for n in
                ("staged", "src_in", "win_in", "marked", "turned", "copied", "used", "summed", "rel_made", "rel_st", "e_made", "dotted"))

            def sync_program(sp, nw):
                def store(q, i, s):
                    sp.wait_ge(rel_made[s], i + 1)
                    sp.dma_start(rel_edges[bass.ds(q, 1), :, :].rearrange("a p f -> (a p) f"),
                                 rel[:, s, :, :].rearrange("p j f -> p (j f)")).then_inc(rel_st[s], 16)

                def body(i, first):
                    for s in range(2):
                        for w in range(nw):
                            sp.wait_ge(used[s], i * nw + w)
                            sp.nop(nofuse=True)
                            for j in range(J):
                                base = window_base([sp.engine], 2 * i + s, j)
                                sp.dma_start(window[:, s, j, :], rel_window[bass.ds(base * R + w * KEYS, KEYS), :]).then_inc(win_in[s], 16)
                        if not (first and s == 0):
                            store(2 * i + s - 1, i - 1 + s, 1 - s)
                pairs(sp, body)
                store(Q - 1, Q // 2 - 1, 1)
                for s in range(2):
                    sp.wait_ge(rel_st[s], 16 * (Q // 2))

            def pe_program(pe, nw):
                def expand(i, s):
                    for w in range(nw):
                        c = i * nw + w
                        if w == 0:
                            pe.wait_ge(dotted[s], i)
                            pe.wait_ge(src_in[s], 16 * J * (i + 1))
                            pe.matmul(ps_r[s][:, :, :], ident[:, :], gathered[:, s, :, :], start=True, stop=False, skip_group_check=True)
                        pe.wait_ge(win_in[s], 16 * J * (c + 1))
                        pe.wait_ge(copied[s], c + 1)
                        for j in range(J):
                            pe.matmul(ps_r[s][:, j, :], spread[:, s, j, :], window[:, s, j, :], start=False, stop=(w == nw - 1), skip_group_check=True)
                            mm = pe.matmul(ps_u[s][:, j, :], spread[:, s, j, :], u_keys[:, :], start=(w == 0), stop=(w == nw - 1), skip_group_check=True)
                        mm.then_inc(used[s], 1)
                        if w < nw - 1:
                            turn(i, s, w + 1)

                def turn(i, s, w):
                    c = i * nw + w
                    pe.wait_ge(marked[s], c + 1)
                    pe.wait_ge(copied[s], c)
                    for j in range(J):
                        mm = pe.transpose(ps_t[s][:, j, :], onehot[:, s, j, :], ident[:, :])
                    mm.then_inc(turned[s], 1)

                def body(i, first):
                    for s in range(2):
                        turn(i, s, 0)
                        if not (first and s == 0):
                            expand(i - 1 + s, 1 - s)
                pairs(pe, body)
                expand(Q // 2 - 1, 1)

            def act_program(act, nw):
                def body(i, first):
                    for s in range(2):
                        act.wait_ge(src_in[s], 16 * J * i)
                        act.copy(idx[:, s, :], rel_idx[:, bass.ds((2 * i + s) * J, J)]).then_inc(staged[s], 1)
                        for w in range(nw):
                            act.wait_ge(turned[s], i * nw + w + 1)
                            act.wait_ge(used[s], i * nw + w)
                            act.copy(spread[:, s, :, :], ps_t[s][:, :, :]).then_inc(copied[s], 1)
                pairs(act, body)

            def dve_program(dve, nw):
                def mark(i, s):
                    for w in range(nw):
                        dve.wait_ge(turned[s], i * nw + w)
                        for j in range(J):
                            mk = dve.tensor_scalar(onehot[:, s, j, :], iota[:, w * KEYS:(w + 1) * KEYS],
                                                   key_t[:, bass.ds((2 * i + s) * J + j, 1)], None, ALU.is_equal)
                        mk.then_inc(marked[s], 1)

                def score(i, s):
                    q = 2 * i + s
                    dve.wait_ge(used[s], (i + 1) * nw)
                    dve.wait_ge(rel_st[s], 16 * i)
                    dve.tensor_scalar(junk[:, :, :], ps_r[s][:, :, :], 0.2, None, ALU.mult).then_inc(summed[s], 1)
                    dve.wait_ge(summed[s], i + 1)
                    dve.tensor_tensor(rel[:, s, :, :], junk[:, :, :], ps_r[s][:, :, :], ALU.max).then_inc(rel_made[s], 1)
                    dve.wait_ge(rel_made[s], i + 1)
                    for j in range(J):
                        dot = dve.tensor_tensor_reduce(junk[:, j, :], rel[:, s, j, :], ps_u[s][:, j, :], 1.0, 0.0, ALU.mult, ALU.add, e_now[:, s, j:j + 1])
                    dot.then_inc(dotted[s], 1)
                    dve.wait_ge(dotted[s], i + 1)
                    dve.tensor_copy(e_t[:, bass.ds(q * J, J)], e_now[:, s, :]).then_inc(e_made[s], 1)

                def body(i, first):
                    for s in range(2):
                        mark(i, s)
                        if not (first and s == 0):
                            score(i - 1 + s, 1 - s)
                pairs(dve, body)
                score(Q // 2 - 1, 1)

            with nc.Block() as block:
                @block.gpsimd
                def _(pool):
                    def body(i, first):
                        for s in range(2):
                            pool.wait_ge(staged[s], i + 1)
                            pool.wait_ge(dotted[s], i)
                            pool.nop(nofuse=True)
                            for j in range(J):
                                pool.indirect_dma_start(gathered[:, s, j, :], None, rel_table,
                                                        bass.IndirectOffsetOnAxis(ap=idx[:, s, j:j + 1], axis=0)).then_inc(src_in[s], 16)
                    pairs(pool, body)

                @block.sync
                def _(sp):
                    both_ways(sp, lambda nw: sync_program(sp, nw))

                @block.tensor
                def _(pe):
                    both_ways(pe, lambda nw: pe_program(pe, nw))

                @block.scalar
                def _(act):
                    both_ways(act, lambda nw: act_program(act, nw))

                @block.vector
                def _(dve):
                    both_ways(dve, lambda nw: dve_program(dve, nw))

    def segment_totals(ctx, tag, n):
        tmp, psum, sem, pair = scope(ctx, tag)
        ends, rows = tmp("ends", [Q, 2, n]), tmp("rows", [n, 2, Q + 2])
        chain, gate, links = tmp("chain", [n, 2, Q]), tmp("gate", [n, 2, Q]), tmp("links", [n, 2, Q])
        back = tmp("back", [Q, 2, n])
        ps_rows, ps_back = psum("ps_rows", [n, 2, Q + 2]), psum("ps_back", [Q, 2, n])
        done, turned = sem("done"), sem("turned")
        mine = 2 * n + 9 + 2 * n

        def vector(dve, call, largest, values, scratch):
            at = call * mine
            for k in range(n):
                gates = pen if largest else same
                dve.tensor_tensor_scan(scratch[k], gates[:, 0:GE], values[k], -BIG if largest else 0.0,
                                       ALU.add if largest else ALU.mult, ALU.max if largest else ALU.add).then_inc(done, 1)
            for k in range(n):
                dve.wait_ge(done, at + k + 1)
                dve.tensor_tensor_scan(values[k][:, ::-1], pen[:, GE:0:-1], scratch[k][:, ::-1], -BIG, ALU.add, ALU.max).then_inc(done, 1)
            at += 2 * n
            dve.wait_ge(done, at)
            for k in range(n):
                dve.tensor_copy(ends[:, 0, k:k + 1], values[k][:, 0:1])
                last = dve.tensor_copy(ends[:, 1, k:k + 1], values[k][:, GE - 1:GE])
            last.then_inc(done, 1)
            dve.memset(rows[:, :, :], -NEG if largest else 0.0).then_inc(done, 1)
            dve.tensor_tensor(links[:, 0, :], cont[0:n, 0:Q], through[0:n, 0:Q], ALU.mult).then_inc(done, 1)
            dve.tensor_tensor(links[:, 1, :], cont[0:n, 1:Q + 1], through[0:n, 2:Q + 2], ALU.mult).then_inc(done, 1)
            dve.wait_ge(done, at + 4)
            dve.wait_ge(turned, 2 * call + 1)
            dve.tensor_copy(rows[:, :, 1:Q + 1], ps_rows[:, :, 0:Q]).then_inc(done, 1)
            dve.wait_ge(done, at + 5)
            for way, (which, other) in enumerate(((cont[0:n, 0:Q], rows[:, 1, 0:Q]), (cont[0:n, 1:Q + 1], rows[:, 0, 2:Q + 2]))):
                if largest:
                    dve.tensor_scalar(chain[:, way, :], which, 1.0, BIG, ALU.subtract, ALU.mult)
                    got = dve.tensor_scalar(gate[:, way, :], links[:, way, :], 1.0, BIG, ALU.subtract, ALU.mult)
                else:
                    dve.tensor_tensor(chain[:, way, :], which, other, ALU.mult)
                    got = dve.tensor_copy(gate[:, way, :], links[:, way, :])
            got.then_inc(done, 1)
            dve.wait_ge(done, at + 6)
            if largest:
                dve.tensor_tensor(chain[:, 0, :], chain[:, 0, :], rows[:, 1, 0:Q], ALU.add)
                dve.tensor_tensor(chain[:, 1, :], chain[:, 1, :], rows[:, 0, 2:Q + 2], ALU.add).then_inc(done, 1)
            else:
                dve.tensor_copy(rows[:, 0, 0:1], rows[:, 0, 0:1]).then_inc(done, 1)
            dve.wait_ge(done, at + 7)
            op0, op1, start = (ALU.add, ALU.max, -NEG) if largest else (ALU.mult, ALU.add, 0.0)
            dve.tensor_tensor_scan(links[:, 0, :], gate[:, 0, :], chain[:, 0, :], start, op0, op1)
            dve.tensor_tensor_scan(links[:, 1, ::-1], gate[:, 1, ::-1], chain[:, 1, ::-1], start, op0, op1).then_inc(done, 1)
            dve.wait_ge(turned, 2 * call + 2)
            dve.tensor_copy(back[:, :, :], ps_back[:, :, :]).then_inc(done, 1)
            at += 9
            dve.wait_ge(done, at)
            for way, where in enumerate((pen_first, pen_last) if largest else (in_first, in_last)):
                for k in range(n):
                    dve.wait_ge(done, at + way * n)
                    dve.scalar_tensor_tensor(out=values[k], in0=where[:, :], scalar=back[:, way, k:k + 1], in1=values[k],
                                             op0=op0, op1=op1).then_inc(done, 1)
            dve.wait_ge(done, at + 2 * n)

        def tensor(pe, call):
            pe.wait_ge(done, call * mine + 2 * n + 1)
            for way in range(2):
                mm = pe.transpose(ps_rows[:, way, 0:Q], ends[:, way, :], ident[0:Q, 0:Q])
            mm.then_inc(turned, 1)
            pe.wait_ge(done, call * mine + 2 * n + 8)
            for way in range(2):
                mm = pe.transpose(ps_back[:, way, :], links[:, way, :], ident[0:n, 0:n])
            mm.then_inc(turned, 1)

        return vector, tensor

    def rel_softmax(e_t, e_bias):
        with ExitStack() as ctx:
            tmp, psum, sem, pair = scope(ctx, "s0")
            e_s, top_s, ex, total = (tmp(n, [Q, GE]) for n in ("e_s", "top_s", "ex", "total"))
            mask, val, scratch = tmp("mask", [Q, R, GE]), tmp("val", [Q, R, GE]), tmp("scratch", [Q, R, GE])
            ps_e = psum("ps_e", [Q, J, P])
            ps_a = psum("ps_a", [P, J, Q])
            turned, step, exped = sem("turned"), sem("step"), sem("exped")
            totals_v, totals_t = segment_totals(ctx, "s0t", R)
            vals, scr = [val[:, r, :] for r in range(R)], [scratch[:, r, :] for r in range(R)]
            n_select = 2 * R

            with nc.Block() as block:
                @block.tensor
                def _(pe):
                    for j in range(J):
                        mm = pe.transpose(ps_e[:, j, :], e_t[:, j::J], ident[:, :])
                    mm.then_inc(turned, 1)
                    totals_t(pe, 0)
                    totals_t(pe, 1)
                    pe.wait_ge(step, 4 + 3 * R + n_select + 2 + R + n_select + 3)
                    for j in range(J):
                        mm = pe.transpose(ps_a[:, j, :], total[:, j * P:(j + 1) * P], ident[0:Q, 0:Q])
                    mm.then_inc(turned, 1)

                @block.scalar
                def _(act):
                    act.wait_ge(step, 4 + 3 * R + n_select + 2)
                    act.activation(ex[:, :], e_s[:, :], ACT.Exp).then_inc(exped, 1)

                @block.vector
                def _(dve):
                    for r in range(R):
                        dve.tensor_scalar(mask[:, r, :], typ_s[:, :], float(r), None, ALU.is_equal).then_inc(step, 1)
                    dve.wait_ge(turned, 1)
                    dve.wait_ge(step, R)
                    dve.tensor_copy(e_s[:, :], ps_e[:, :, :].rearrange("q j e -> q (j e)")).then_inc(step, 1)
                    for r in range(R):
                        dve.wait_ge(step, R + 1 + r)
                        dve.scalar_tensor_tensor(out=e_s[:, :], in0=mask[:, r, :], scalar=e_bias[:, r:r + 1], in1=e_s[:, :],
                                                 op0=ALU.mult, op1=ALU.add).then_inc(step, 1)
                    dve.wait_ge(step, 2 * R + 1)
                    dve.scalar_tensor_tensor(out=top_s[:, :], in0=e_s[:, :], scalar=0.2, in1=e_s[:, :],
                                             op0=ALU.mult, op1=ALU.max).then_inc(step, 1)
                    dve.wait_ge(step, 2 * R + 2)
                    dve.tensor_copy(e_s[:, :], top_s[:, :]).then_inc(step, 1)
                    dve.wait_ge(step, 2 * R + 3)
                    for r in range(R):
                        dve.tensor_scalar(vals[r], mask[:, r, :], 1.0, NEG, ALU.subtract, ALU.mult)
                    dve.memset(total[:, :], 0.0).then_inc(step, 1)
                    dve.wait_ge(step, 2 * R + 4)
                    for r in range(R):
                        dve.tensor_tensor(vals[r], vals[r], e_s[:, :], ALU.add).then_inc(step, 1)
                    at = 3 * R + 4
                    dve.wait_ge(step, at)
                    totals_v(dve, 0, True, vals, scr)

                    def select(at):
                        for r in range(R):
                            dve.tensor_tensor(scr[r], mask[:, r, :], vals[r], ALU.mult).then_inc(step, 1)
                        for r in range(R):
                            dve.wait_ge(step, at + R + r)
                            dve.tensor_tensor(total[:, :], total[:, :], scr[r], ALU.add).then_inc(step, 1)
                        dve.wait_ge(step, at + 2 * R)

                    select(at)
                    at += n_select
                    dve.tensor_tensor(e_s[:, :], e_s[:, :], total[:, :], ALU.subtract).then_inc(step, 1)
                    dve.wait_ge(step, at + 1)
                    dve.memset(total[:, :], 0.0).then_inc(step, 1)
                    at += 2 + R
                    dve.wait_ge(exped, 1)
                    for r in range(R):
                        dve.tensor_tensor(vals[r], mask[:, r, :], ex[:, :], ALU.mult).then_inc(step, 1)
                    at += 0
                    dve.wait_ge(step, at)
                    totals_v(dve, 1, False, vals, scr)
                    select(at)
                    at += n_select
                    dve.tensor_scalar(total[:, :], total[:, :], 1e-16, None, ALU.max).then_inc(step, 1)
                    dve.wait_ge(step, at + 1)
                    dve.reciprocal(top_s[:, :], total[:, :]).then_inc(step, 1)
                    dve.wait_ge(step, at + 2)
                    dve.tensor_tensor(total[:, :], top_s[:, :], ex[:, :], ALU.mult).then_inc(step, 1)
                    dve.wait_ge(turned, 2)
                    dve.tensor_copy(attn_t[:, :].rearrange("p (q j) -> p j q", j=J), ps_a[:, :, :]).then_inc(step, 1)

    def rel_sums(agg, share):
        with ExitStack() as ctx:
            tmp, psum, sem, pair = scope(ctx, "g0")
            rel, onehot = tmp("rel", [P, 2, J, D]), tmp("onehot", [P, 2, J, KEYS])
            ps_g = [psum(f"ps_g{s}", [P, J, KEYS]) for s in range(2)]
            ps_w = [psum(f"ps_w{s}", [1, J, KEYS]) for s in range(2)]
            rel_in, marked, used = (pair(n) for n in ("rel_in", "marked", "used"))
            added, shared = sem("added"), sem("shared")

            def sync_program(sp, nw):
                with sp.Fori(0, Q // 2) as i:
                    for s in range(2):
                        sp.wait_ge(used[s], i * nw)
                        sp.dma_start(rel[:, s, :, :].rearrange("p j f -> p (j f)"),
                                     rel_edges[bass.ds(2 * i + s, 1), :, :].rearrange("a p f -> (a p) f")).then_inc(rel_in[s], 16)

            def pe_program(pe, nw):
                def body(i, first):
                    for s in range(2):
                        pe.wait_ge(rel_in[s], 16 * (i + 1))
                        for w in range(nw):
                            pe.wait_ge(marked[s], i * nw + w + 1)
                            if w > 0 or not first:
                                steps = (2 * i + s) * nw + w if w > 0 else (2 * i + s - 1) * nw
                                pe.wait_ge(added, J * steps)
                                pe.wait_ge(shared, J * steps)
                            for j in range(J):
                                pe.matmul(ps_g[s][:, j, :], rel[:, s, j, :], onehot[:, s, j, :], start=True, stop=True)
                            pe.matmul(ps_w[s][:, :, :], ones[:, 0:1], onehot[:, s, :, :], start=True, stop=True).then_inc(used[s], 1)
                pairs(pe, body)

            def dve_program(dve, nw):
                def mark(i, s, w):
                    dve.wait_ge(used[s], i * nw + w)
                    for j in range(J):
                        t = (2 * i + s) * J + j
                        mk = dve.tensor_scalar(onehot[:, s, j, :], iota[:, w * KEYS:(w + 1) * KEYS], key_t[:, bass.ds(t, 1)],
                                               attn_t[:, bass.ds(t, 1)], ALU.is_equal, ALU.mult)
                    mk.then_inc(marked[s], 1)

                def add(i, s, w):
                    dve.wait_ge(used[s], i * nw + w + 1)
                    dve.nop(nofuse=True)
                    for j in range(J):
                        base = window_base([dve.engine], 2 * i + s, j)
                        n = ((2 * i + s) * nw + w) * J + j
                        to = bass.ds(base * R + w * KEYS, KEYS)
                        dve.wait_ge(added, n)
                        dve.tensor_tensor(agg[:, to], agg[:, to], ps_g[s][:, j, :], ALU.add).then_inc(added, 1)
                        dve.wait_ge(shared, n)
                        dve.tensor_tensor(share[0:1, to], share[0:1, to], ps_w[s][:, j, :], ALU.add).then_inc(shared, 1)

                def body(i, first):
                    for s in range(2):
                        mark(i, s, 0)
                        if not (first and s == 0):
                            add(i - 1 + s, 1 - s, nw - 1)
                        for w in range(1, nw):
                            add(i, s, w - 1)
                            mark(i, s, w)
                pairs(dve, body)
                add(Q // 2 - 1, 1, nw - 1)

            with nc.Block() as block:
                @block.sync
                def _(sp):
                    both_ways(sp, lambda nw: sync_program(sp, nw))

                @block.tensor
                def _(pe):
                    both_ways(pe, lambda nw: pe_program(pe, nw))

                @block.vector
                def _(dve):
                    both_ways(dve, lambda nw: dve_program(dve, nw))

    def norm_stats(dve, rows, stats, mean_var, var_eps, done, at):
        for k in range(K4):
            st = dve.bn_stats(stats[:, k, :], rows[:, k, :])
        st.then_inc(done, 1)
        dve.wait_ge(done, at + 1)
        dve.nop(nofuse=True)
        for k in range(K4):
            st = dve.bn_aggr(mean_var[:, k, :], stats[:, k, :])
        st.then_inc(done, 1)
        dve.wait_ge(done, at + 2)
        dve.tensor_scalar(var_eps[:, :], mean_var[:, :, 1], EPS, None, ALU.add).then_inc(done, 1)

    def norm_apply(dve, out_rows, rows, mean_var, root, inverse, done, at):
        dve.reciprocal(inverse[:, :], root[:, :]).then_inc(done, 1)
        dve.wait_ge(done, at + 1)
        for k in range(K4):
            st = dve.tensor_scalar(out_rows[:, k, :], rows[:, k, :], mean_var[:, k, 0:1], inverse[:, k:k + 1], ALU.subtract, ALU.mult)
        st.then_inc(done, 1)

    def rel_nodes(agg, share):
        with ExitStack() as ctx:
            tmp, psum, sem, pair = scope(ctx, "n0")
            wv, bv = tmp("wv", [P, R, D]), tmp("bv", [1, R, D])
            w_src, w_dst, b1 = tmp("w_src", [P, D]), tmp("w_dst", [P, D]), tmp("b1", [P, D])
            part, part_w = tmp("part", [P, GE * R]), tmp("part_w", [1, GE * R])
            xg, low, ex, h, y, x1, xt = (tmp(n, [P, K4, D]) for n in ("xg", "low", "ex", "h", "y", "x1", "xt"))
            src_rows, dst_rows = tmp("src_rows", [P, K4, D]), tmp("dst_rows", [P, K4, D])
            stats, mean_var = tmp("stats", [P, K4, 6]), tmp("mean_var", [P, K4, 2])
            var_eps, root, inverse = (tmp(n, [P, K4]) for n in ("var_eps", "root", "inverse"))
            ps_h, ps_x, ps_s, ps_d = (psum(n, [P, K4, D]) for n in ("ps_h", "ps_x", "ps_s", "ps_d"))
            weights_in, x_in, parts, h_mm, exped, rooted, vec, turned, xt_ready, tab_mm, src_out, stored = (sem(n) for n in
                ("weights_in", "x_in", "parts", "h_mm", "exped", "rooted", "vec", "turned", "xt_ready", "tab_mm", "src_out", "stored"))
            V = 9

            with nc.Block() as block:
                @block.sync
                def _(sp):
                    sp.dma_start(wv[:, :, :], L0_gnn_W_V.rearrange("r f g -> f r g")).then_inc(weights_in, 16)
                    sp.dma_start(bv[:, :, :].rearrange("a r f -> a (r f)"), across(L0_gnn_b_V.rearrange("r f -> (r f)"), R * D, 1)).then_inc(weights_in, 16)
                    sp.dma_start(w_src[:, :], L1_gnn_W1[0:D, :]).then_inc(weights_in, 16)
                    sp.dma_start(w_dst[:, :], L1_gnn_W1[D:2 * D, :]).then_inc(weights_in, 16)
                    sp.dma_start(b1[:, :], across(L1_gnn_b1, D)).then_inc(weights_in, 16)
                    with sp.Fori(0, NGRP) as g:
                        sp.wait_ge(vec, V * g)
                        sp.dma_start(xg[:, :, :], rows_of(xs[0], g, D)).then_inc(x_in, 16)
                        sp.wait_ge(vec, V * g + 8)
                        sp.dma_start(rows_of(xs[1], g, D), x1[:, :, :]).then_inc(stored, 16)
                        sp.wait_ge(src_out, g + 1)
                        sp.dma_start(rows_of(msg_table, g, D), src_rows[:, :, :]).then_inc(stored, 16)
                        sp.wait_ge(vec, V * g + 9)
                        sp.dma_start(rows_of(msg_window, g, D), dst_rows[:, :, :]).then_inc(stored, 16)
                    sp.wait_ge(stored, 48 * NGRP)

                @block.tensor
                def _(pe):
                    pe.wait_ge(weights_in, 16 * 5)
                    with pe.Fori(0, NGRP) as g:
                        pe.wait_ge(parts, 2 * (g + 1))
                        pe.wait_ge(vec, V * g + 0)
                        by_node = part[:, :].rearrange("f (n k r) -> f n k r", k=K4, r=R)
                        by_node_w = part_w[:, :].rearrange("f (n k r) -> f n k r", k=K4, r=R)
                        for k in range(K4):
                            for r in range(R):
                                pe.matmul(ps_h[:, k, :], by_node[:, :, k, r], wv[:, r, :], start=(r == 0), stop=False, skip_group_check=True)
                                mm = pe.matmul(ps_h[:, k, :], by_node_w[:, :, k, r], bv[:, r, :], start=False, stop=(r == R - 1), skip_group_check=True)
                        mm.then_inc(h_mm, 1)
                        pe.wait_ge(vec, V * g + 8)
                        for k in range(K4):
                            mm = pe.transpose(ps_x[:, k, :], x1[:, k, :], ident[:, :])
                        mm.then_inc(turned, 1)
                        pe.wait_ge(xt_ready, g + 1)
                        for k in range(K4):
                            pe.matmul(ps_s[:, k, :], xt[:, k, :], w_src[:, :], start=True, stop=True)
                            mm = pe.matmul(ps_d[:, k, :], xt[:, k, :], w_dst[:, :], start=True, stop=True)
                        mm.then_inc(tab_mm, 1)

                @block.scalar
                def _(act):
                    with act.Fori(0, NGRP) as g:
                        act.wait_ge(h_mm, g)
                        act.copy(part[:, :], agg[:, bass.ds(g * GE * R, GE * R)]).then_inc(parts, 1)
                        act.copy(part_w[:, :], share[0:1, bass.ds(g * GE * R, GE * R)]).then_inc(parts, 1)
                        act.wait_ge(vec, V * g + 1)
                        act.activation(ex[:, :, :], low[:, :, :], ACT.Exp).then_inc(exped, 1)
                        act.wait_ge(vec, V * g + 6)
                        act.activation(root[:, :], var_eps[:, :], ACT.Sqrt).then_inc(rooted, 1)
                        act.wait_ge(turned, g + 1)
                        act.copy(xt[:, :, :], ps_x[:, :, :]).then_inc(xt_ready, 1)
                        act.wait_ge(tab_mm, g + 1)
                        act.wait_ge(stored, 48 * g)
                        act.copy(src_rows[:, :, :], ps_s[:, :, :]).then_inc(src_out, 1)

                @block.vector
                def _(dve):
                    dve.wait_ge(weights_in, 16 * 5)
                    with dve.Fori(0, NGRP) as g:
                        dve.wait_ge(h_mm, g + 1)
                        dve.tensor_scalar(low[:, :, :], ps_h[:, :, :], 0.0, None, ALU.min).then_inc(vec, 1)
                        dve.wait_ge(exped, g + 1)
                        dve.scalar_tensor_tensor(out=h[:, :, :], in0=ps_h[:, :, :], scalar=0.0, in1=ex[:, :, :],
                                                 op0=ALU.max, op1=ALU.add).then_inc(vec, 1)
                        dve.wait_ge(vec, V * g + 2)
                        dve.wait_ge(x_in, 16 * (g + 1))
                        dve.scalar_tensor_tensor(out=y[:, :, :], in0=h[:, :, :], scalar=-1.0, in1=xg[:, :, :],
                                                 op0=ALU.add, op1=ALU.add).then_inc(vec, 1)
                        dve.wait_ge(vec, V * g + 3)
                        norm_stats(dve, y, stats, mean_var, var_eps, vec, V * g + 3)
                        dve.wait_ge(rooted, g + 1)
                        dve.wait_ge(stored, 48 * g)
                        norm_apply(dve, x1, y, mean_var, root, inverse, vec, V * g + 6)
                        dve.wait_ge(tab_mm, g + 1)
                        dve.tensor_tensor(dst_rows[:, :, :], ps_d[:, :, :], b1[:, :].unsqueeze(1).to_broadcast([P, K4, D]), ALU.add).then_inc(vec, 1)

    def mark_nodes(dve, onehot, s, q, nw):
        for w in range(nw):
            mk = dve.tensor_tensor(onehot[:, s, w, :, :], iota[:, w * WIN:(w + 1) * WIN].unsqueeze(1).to_broadcast([P, J, WIN]),
                                   dl_t[:, bass.ds(q * J, J)].unsqueeze(2).to_broadcast([P, J, WIN]), ALU.is_equal)
        return mk

    def spread_nodes(act, spread, ps_t, s, nw):
        for w in range(nw):
            for j in range(J):
                cp = act.copy(spread[j * WIN:(j + 1) * WIN, s, w, j, :], ps_t[s][j * WIN:(j + 1) * WIN, w, :])
        return cp

    def load_windows(sp, window, s, table, q, nw, loaded):
        for j in range(J):
            base = window_base([sp.engine], q, j)
            for w in range(nw):
                sp.dma_start(window[j * WIN:(j + 1) * WIN, s, w, :], table[bass.ds(base + w * WIN, WIN), :]).then_inc(loaded, 16)

    def add_windows(dve, sums, ps_a, s, q, nw, added):
        n = q * (J * nw)
        for j in range(J):
            base = window_base([dve.engine], q, j)
            for w in range(nw):
                to = bass.ds(base + w * WIN, WIN)
                dve.wait_ge(added, n + j * nw + w)
                dve.tensor_tensor(sums[:, to], sums[:, to], ps_a[s][:, w, j, :], ALU.add).then_inc(added, 1)

    def messages(agg1):
        with ExitStack() as ctx:
            tmp, psum, sem, pair = scope(ctx, "e1")
            NWM = P // WIN
            idx = tmp("idx", [P, 2, J], I32)
            w_edge, w2, b2 = tmp("w_edge", [REL, D]), tmp("w2", [P, D]), tmp("b2", [1, J, D])
            gathered, hidden, message = (tmp(n, [P, 2, J, D]) for n in ("gathered", "hidden", "message"))
            attr, attr_t = tmp("attr", [P, 2, J, REL]), tmp("attr_t", [REL, 2, J, P])
            onehot = tmp("onehot", [P, 2, NWM, J, WIN])
            spread, window = tmp("spread", [P, 2, NWM, J, P]), tmp("window", [P, 2, NWM, D])
            ps_t = [psum(f"ps_t{s}", [P, NWM, P]) for s in range(2)]
            ps_h = [psum(f"ps_h{s}", [P, J, P]) for s in range(2)]
            ps_e, ps_m = psum("ps_e", [REL, J, P]), psum("ps_m", [P, J, D])
            ps_a = [psum(f"ps_a{s}", [P, NWM, J, WIN]) for s in range(2)]
            cleared, weights_in, attr_turned, attr_copied, m_mm, m_out, added = (sem(n) for n in
                ("cleared", "weights_in", "attr_turned", "attr_copied", "m_mm", "m_out", "added"))
            staged, src_in, win_in, attr_in, marked, turned, copied, h_mm, h_out, a_mm = (pair(n) for n in
                ("staged", "src_in", "win_in", "attr_in", "marked", "turned", "copied", "h_mm", "h_out", "a_mm"))
            full = (E - (Q - 1) * GE) // P
            rest = E - (Q - 1) * GE - full * P

            def sync_program(sp, nw):
                for to, frm in ((w_edge[:, :], L1_gnn_W1[2 * D:, :]), (w2[:, :], L1_gnn_W2)):
                    sp.dma_start(to, frm).then_inc(weights_in, 16)
                for j in range(J):
                    sp.dma_start(b2[:, j, :], across(L1_gnn_b2, D, 1)).then_inc(weights_in, 16)

                def body(i, first, last=False):
                    for s in range(2):
                        sp.wait_ge(h_mm[s], i)
                        sp.nop(nofuse=True)
                        if last and s == 1:
                            rows = edge_attr_64[(Q - 1) * GE:(Q - 1) * GE + full * P, :]
                            sp.dma_start(attr[:, s, 0:full, :], rows.rearrange("(j p) f -> p j f", p=P)).then_inc(attr_in[s], 16)
                            sp.dma_start(attr[0:rest, s, full, :], edge_attr_64[E - rest:E, :]).then_inc(attr_in[s], 16)
                        else:
                            rows = edge_attr_64[bass.ds((2 * i + s) * GE, GE), :]
                            sp.dma_start(attr[:, s, :, :], rows.rearrange("(j p) f -> p j f", p=P)).then_inc(attr_in[s], 16)
                        load_windows(sp, window, s, msg_window, 2 * i + s, nw, win_in[s])
                with sp.Fori(0, Q // 2 - 1) as i:
                    body(i, False)
                body(Q // 2 - 1, False, last=True)

            def pe_program(pe, nw):
                pe.wait_ge(weights_in, 16 * (2 + J))

                def turn(i, s, last):
                    pe.wait_ge(attr_copied, 2 * i + s)
                    pe.wait_ge(attr_in[s], 16 * (i + 1) + (16 * s if last else 0))
                    pe.wait_ge(copied[s], i)
                    pe.wait_ge(marked[s], i + 1)
                    for w in range(nw):
                        mm = pe.transpose(ps_t[s][:, w, :], onehot[:, s, w, :, :].rearrange("p j n -> p (j n)"), ident[:, :])
                    mm.then_inc(turned[s], 1)
                    for j in range(J):
                        mm = pe.transpose(ps_e[:, j, :], attr[:, s, j, :], ident[:, :])
                    mm.then_inc(attr_turned, 1)

                def hide(i, s):
                    pe.wait_ge(src_in[s], 16 * J * (i + 1))
                    pe.wait_ge(win_in[s], 16 * J * nw * (i + 1))
                    pe.wait_ge(copied[s], i + 1)
                    pe.wait_ge(attr_copied, 2 * i + s + 1)
                    pe.wait_ge(h_out[s], i)
                    for w in range(nw):
                        pe.matmul(ps_h[s][:, :, :], window[:, s, w, :], spread[:, s, w, :, :], start=(w == 0), stop=False, skip_group_check=True)
                    pe.matmul(ps_h[s][:, :, :], w_edge[:, :], attr_t[:, s, :, :], start=False, stop=False, skip_group_check=True)
                    for j in range(J):
                        mm = pe.matmul(ps_h[s][:, j, :], gathered[:, s, j, :], ident[:, :], start=False, stop=True, skip_group_check=True)
                    mm.then_inc(h_mm[s], 1)

                def send(i, s):
                    pe.wait_ge(h_out[s], i + 1)
                    pe.wait_ge(m_out, 2 * i + s)
                    pe.matmul(ps_m[:, :, :], ones[0:1, :], b2[:, :, :], start=True, stop=False, skip_group_check=True)
                    for j in range(J):
                        mm = pe.matmul(ps_m[:, j, :], hidden[:, s, j, :], w2[:, :], start=False, stop=True, skip_group_check=True)
                    mm.then_inc(m_mm, 1)

                def collect(i, s, first):
                    pe.wait_ge(m_out, 2 * i + s + 1)
                    if not first:
                        pe.wait_ge(added, J * nw * (2 * i + s - 1))
                    for w in range(nw):
                        for j in range(J):
                            mm = pe.matmul(ps_a[s][:, w, j, :], message[:, s, j, :], onehot[:, s, w, j, :], start=True, stop=True)
                    mm.then_inc(a_mm[s], 1)

                def body(i, first, last=False):
                    for s in range(2):
                        turn(i, s, last)
                        if not (first and s == 0):
                            collect(i - 1 + s, 1 - s, first)
                        hide(i, s)
                        send(i, s)
                body(0, True)
                with pe.Fori(1, Q // 2 - 1) as i:
                    body(i, False)
                body(Q // 2 - 1, False, last=True)
                collect(Q // 2 - 1, 1, False)

            def act_program(act, nw):
                act.wait_ge(cleared, 2)
                with act.Fori(0, Q // 2) as i:
                    for s in range(2):
                        act.wait_ge(src_in[s], 16 * J * i)
                        act.copy(idx[:, s, :], src_idx[:, bass.ds((2 * i + s) * J, J)]).then_inc(staged[s], 1)
                        act.wait_ge(turned[s], i + 1)
                        act.wait_ge(h_mm[s], i)
                        spread_nodes(act, spread, ps_t, s, nw).then_inc(copied[s], 1)
                        act.wait_ge(attr_turned, 2 * i + s + 1)
                        act.copy(attr_t[:, s, :, :], ps_e[:, :, :]).then_inc(attr_copied, 1)
                        act.wait_ge(h_mm[s], i + 1)
                        act.wait_ge(m_mm, 2 * i)
                        act.activation(hidden[:, s, :, :], ps_h[s][:, :, :], ACT.Relu).then_inc(h_out[s], 1)
                        act.wait_ge(m_mm, 2 * i + s + 1)
                        act.wait_ge(a_mm[s], i)
                        act.activation(message[:, s, :, :], ps_m[:, :, :], ACT.Relu).then_inc(m_out, 1)

            def dve_program(dve, nw):
                dve.memset(spread[:, :, :, :, :], 0.0).then_inc(cleared, 1)
                dve.memset(agg1[:, :], 0.0).then_inc(cleared, 1)
                dve.wait_ge(cleared, 2)

                def add(i, s):
                    dve.wait_ge(a_mm[s], i + 1)
                    dve.nop(nofuse=True)
                    add_windows(dve, agg1, ps_a, s, 2 * i + s, nw, added)

                def body(i, first):
                    for s in range(2):
                        dve.wait_ge(a_mm[s], i)
                        mark_nodes(dve, onehot, s, 2 * i + s, nw).then_inc(marked[s], 1)
                        if not (first and s == 0):
                            add(i - 1 + s, 1 - s)
                pairs(dve, body)
                add(Q // 2 - 1, 1)

            with nc.Block() as block:
                @block.gpsimd
                def _(pool):
                    with pool.Fori(0, Q // 2) as i:
                        for s in range(2):
                            pool.wait_ge(staged[s], i + 1)
                            pool.wait_ge(h_mm[s], i)
                            pool.nop(nofuse=True)
                            for j in range(J):
                                pool.indirect_dma_start(gathered[:, s, j, :], None, msg_table,
                                                        bass.IndirectOffsetOnAxis(ap=idx[:, s, j:j + 1], axis=0)).then_inc(src_in[s], 16)

                @block.sync
                def _(sp):
                    both_ways(sp, lambda nw: sync_program(sp, nw))

                @block.tensor
                def _(pe):
                    both_ways(pe, lambda nw: pe_program(pe, nw))

                @block.scalar
                def _(act):
                    both_ways(act, lambda nw: act_program(act, nw))

                @block.vector
                def _(dve):
                    both_ways(dve, lambda nw: dve_program(dve, nw))

    def message_nodes(agg1):
        with ExitStack() as ctx:
            tmp, psum, sem, pair = scope(ctx, "n1")
            C = 3 * D
            wn, bn, gamma, beta = tmp("wn", [P, D]), tmp("bn", [P, D]), tmp("gamma", [P, D]), tmp("beta", [P, D])
            wk, wv, wkt = tmp("wk", [P, NT, D]), tmp("wv", [P, NT, D]), tmp("wkt", [P, 2, NT, D])
            w_all = tmp("w_all", [P, NT, C])
            att, msg, pri = tmp("att", [P, H, DH]), tmp("msg", [P, H, DH]), tmp("pri", [P, H])
            types, mask = tmp("types", [P, NGRP, K4], I32), tmp("mask", [P, NT, NGRP * K4])
            part = tmp("part", [P, GE])
            xg, r1, y, z, v, x2 = (tmp(n, [P, K4, D]) for n in ("xg", "r1", "y", "z", "v", "x2"))
            masked, xt = tmp("masked", [P, NT, K4, D]), tmp("xt", [P, NT, K4, D])
            rows = tmp("rows", [P, K4, C])
            stats, mean_var = tmp("stats", [P, K4, 6]), tmp("mean_var", [P, K4, 2])
            var_eps, root, inverse = (tmp(n, [P, K4]) for n in ("var_eps", "root", "inverse"))
            ps_h = psum("ps_h", [P, K4, D])
            ps_x = [psum(f"ps_x{n}", [P, K4, D]) for n in range(NT)]
            ps_r = [psum(f"ps_r{k}", [P, 512]) for k in range(K4)]
            weights_in, x_in, parts, h_mm, rooted, vec, turned, xt_ready, tab_mm, rows_out, stored, ready, w_mm, w_out = (sem(n) for n in
                ("weights_in", "x_in", "parts", "h_mm", "rooted", "vec", "turned", "xt_ready", "tab_mm", "rows_out", "stored", "ready", "w_mm", "w_out"))
            V = 17

            with nc.Block() as block:
                @block.gpsimd
                def _(pool):
                    pool.memset(att[:, :, :], 0.0).then_inc(ready, 1)
                    pool.memset(msg[:, :, :], 0.0).then_inc(ready, 1)

                @block.sync
                def _(sp):
                    sp.dma_start(wn[:, :], L1_gnn_Wn).then_inc(weights_in, 16)
                    for to, frm in ((bn, L1_gnn_bn), (gamma, L1_gnn_gamma), (beta, L1_gnn_beta)):
                        sp.dma_start(to[:, :], across(frm, D)).then_inc(weights_in, 16)
                    sp.dma_start(wk[:, :, :], L2_gnn_Wk.rearrange("t f c -> f t c")).then_inc(weights_in, 16)
                    sp.dma_start(wv[:, :, :], L2_gnn_Wv.rearrange("t f c -> f t c")).then_inc(weights_in, 16)
                    sp.dma_start(w_all[:, :, 2 * D:3 * D], L2_gnn_Wq.rearrange("t f c -> f t c")).then_inc(weights_in, 16)
                    sp.dma_start(pri[:, :], across(L2_gnn_rel_pri, H)).then_inc(weights_in, 16)
                    sp.dma_start(types[:, :, :], type_pad.rearrange("(g p k) -> p g k", p=P, k=K4)).then_inc(weights_in, 16)
                    sp.wait_ge(ready, 2)
                    for h in range(H):
                        sp.dma_start(att[h * DH:(h + 1) * DH, h, :], L2_gnn_rel_att[h, :, :]).then_inc(weights_in, 16)
                        sp.dma_start(msg[h * DH:(h + 1) * DH, h, :], L2_gnn_rel_msg[h, :, :]).then_inc(weights_in, 16)
                    with sp.Fori(0, NGRP) as g:
                        sp.wait_ge(vec, 7 + V * g)
                        sp.dma_start(xg[:, :, :], rows_of(xs[1], g, D)).then_inc(x_in, 16)
                        sp.wait_ge(vec, 7 + V * g + 16)
                        sp.dma_start(rows_of(xs[2], g, D), x2[:, :, :]).then_inc(stored, 16)
                        sp.wait_ge(rows_out, K4 * (g + 1))
                        sp.dma_start(rows_of(kv_table, g, 2 * D), rows[:, :, 0:2 * D]).then_inc(stored, 16)
                        sp.dma_start(rows_of(q_window, g, D), rows[:, :, 2 * D:3 * D]).then_inc(stored, 16)
                    sp.wait_ge(stored, 48 * NGRP)

                @block.tensor
                def _(pe):
                    pe.wait_ge(weights_in, 16 * (9 + 2 * H))
                    for n, w in enumerate((wk, wv)):
                        for t in range(NT):
                            mm = pe.transpose(ps_x[n][:, t, :], w[:, t, :], ident[:, :])
                        mm.then_inc(w_mm, 1)
                    pe.wait_ge(w_out, 2)
                    pe.wait_ge(vec, 1)
                    for t in range(NT):
                        pe.matmul(ps_r[t][:, 0:D], wkt[:, 0, t, :], att[:, :, :].rearrange("c h o -> c (h o)"), start=True, stop=True)
                        mm = pe.matmul(ps_r[t][:, D:2 * D], wkt[:, 1, t, :], msg[:, :, :].rearrange("c h o -> c (h o)"), start=True, stop=True)
                    mm.then_inc(w_mm, 1)
                    pe.wait_ge(w_out, 3)
                    with pe.Fori(0, NGRP) as g:
                        pe.wait_ge(parts, g + 1)
                        pe.wait_ge(vec, 7 + V * g)
                        for k in range(K4):
                            mm = pe.matmul(ps_h[:, k, :], part[:, k::K4], wn[:, :], start=True, stop=True)
                        mm.then_inc(h_mm, 1)
                        pe.wait_ge(vec, 7 + V * g + 17)
                        pe.wait_ge(xt_ready, NT * g)
                        for t in range(NT):
                            for k in range(K4):
                                mm = pe.transpose(ps_x[t][:, k, :], masked[:, t, k, :], ident[:, :])
                            mm.then_inc(turned, 1)
                        pe.wait_ge(xt_ready, NT * (g + 1))
                        pe.wait_ge(rows_out, K4 * g)
                        for k in range(K4):
                            for t in range(NT):
                                mm = pe.matmul(ps_r[k][:, 0:C], xt[:, t, k, :], w_all[:, t, :], start=(t == 0), stop=(t == NT - 1))
                            mm.then_inc(tab_mm, 1)

                @block.scalar
                def _(act):
                    for n in range(2):
                        act.wait_ge(w_mm, n + 1)
                        act.copy(wkt[:, n, :, :], ps_x[n][:, 0:NT, :]).then_inc(w_out, 1)
                    act.wait_ge(w_mm, 3)
                    act.wait_ge(weights_in, 16 * (9 + 2 * H))
                    for t in range(NT):
                        cp = act.copy(w_all[:, t, 0:2 * D], ps_r[t][:, 0:2 * D])
                    cp.then_inc(w_out, 1)
                    with act.Fori(0, NGRP) as g:
                        act.wait_ge(h_mm, g)
                        act.copy(part[:, :], agg1[:, bass.ds(g * GE, GE)]).then_inc(parts, 1)
                        act.wait_ge(vec, 7 + V * g + 6)
                        act.activation(root[:, :], var_eps[:, :], ACT.Sqrt).then_inc(rooted, 1)
                        act.wait_ge(vec, 7 + V * g + 14)
                        act.activation(root[:, :], var_eps[:, :], ACT.Sqrt).then_inc(rooted, 1)
                        for t in range(NT):
                            act.wait_ge(turned, NT * g + t + 1)
                            act.copy(xt[:, t, :, :], ps_x[t][:, :, :]).then_inc(xt_ready, 1)
                        act.wait_ge(stored, 48 * g)
                        for k in range(K4):
                            act.wait_ge(tab_mm, K4 * g + k + 1)
                            act.copy(rows[:, k, :], ps_r[k][:, 0:C]).then_inc(rows_out, 1)

                @block.vector
                def _(dve):
                    dve.wait_ge(weights_in, 16 * (9 + 2 * H))
                    dve.tensor_scalar(pri[:, :], pri[:, :], DH ** -0.5, None, ALU.mult).then_inc(ready, 1)
                    dve.wait_ge(ready, 3)
                    dve.tensor_tensor(att[:, :, :], att[:, :, :], pri[:, :].unsqueeze(2).to_broadcast([P, H, DH]), ALU.mult).then_inc(vec, 1)
                    for t in range(NT):
                        dve.tensor_scalar(mask[:, t, :], types[:, :, :].rearrange("p g k -> p (g k)"), float(t), None, ALU.is_equal).then_inc(vec, 2)
                    dve.wait_ge(vec, 7)
                    wide_b = lambda a: a[:, :].unsqueeze(1).to_broadcast([P, K4, D])
                    with dve.Fori(0, NGRP) as g:
                        at = 7 + V * g
                        dve.wait_ge(h_mm, g + 1)
                        dve.tensor_tensor(r1[:, :, :], ps_h[:, :, :], wide_b(bn), ALU.add).then_inc(vec, 1)
                        dve.wait_ge(vec, at + 1)
                        dve.wait_ge(x_in, 16 * (g + 1))
                        dve.scalar_tensor_tensor(out=y[:, :, :], in0=r1[:, :, :], scalar=0.0, in1=xg[:, :, :],
                                                 op0=ALU.max, op1=ALU.add).then_inc(vec, 2)
                        dve.wait_ge(vec, at + 3)
                        norm_stats(dve, y, stats, mean_var, var_eps, vec, at + 3)
                        dve.wait_ge(rooted, 2 * g + 1)
                        norm_apply(dve, z, y, mean_var, root, inverse, vec, at + 6)
                        dve.wait_ge(vec, at + 8)
                        dve.tensor_tensor(v[:, :, :], z[:, :, :], wide_b(gamma), ALU.mult).then_inc(vec, 1)
                        dve.wait_ge(vec, at + 9)
                        dve.tensor_tensor(z[:, :, :], v[:, :, :], wide_b(beta), ALU.add).then_inc(vec, 1)
                        dve.wait_ge(vec, at + 10)
                        dve.tensor_tensor(y[:, :, :], z[:, :, :], xg[:, :, :], ALU.add).then_inc(vec, 1)
                        dve.wait_ge(vec, at + 11)
                        norm_stats(dve, y, stats, mean_var, var_eps, vec, at + 11)
                        dve.wait_ge(rooted, 2 * g + 2)
                        dve.wait_ge(stored, 48 * g)
                        norm_apply(dve, x2, y, mean_var, root, inverse, vec, at + 14)
                        dve.wait_ge(vec, at + 16)
                        for t in range(NT):
                            for k in range(K4):
                                mk = dve.tensor_scalar(masked[:, t, k, :], x2[:, k, :], mask[:, t, bass.ds(g * K4 + k, 1)], None, ALU.mult)
                        mk.then_inc(vec, 1)

    def head_scores(a_t):
        with ExitStack() as ctx:
            tmp, psum, sem, pair = scope(ctx, "e2")
            NWM = P // WIN
            idx = tmp("idx", [P, 2, J], I32)
            gathered = tmp("gathered", [P, 2, J, 2 * D])
            product = tmp("product", [P, J, D])
            onehot = tmp("onehot", [P, 2, NWM, J, WIN])
            spread, window = tmp("spread", [P, 2, NWM, J, P]), tmp("window", [P, 2, NWM, D])
            ps_t = [psum(f"ps_t{s}", [P, NWM, P]) for s in range(2)]
            ps_q = [psum(f"ps_q{s}", [P, J, D]) for s in range(2)]
            cleared = sem("cleared")
            staged, src_in, win_in, marked, turned, copied, q_mm, multiplied, reduced, v_st = (pair(n) for n in
                ("staged", "src_in", "win_in", "marked", "turned", "copied", "q_mm", "multiplied", "reduced", "v_st"))

            def sync_program(sp, nw):
                def store(q, i, s):
                    sp.wait_ge(src_in[s], 16 * J * (i + 1))
                    sp.dma_start(v_edges[bass.ds(q, 1), :, :].rearrange("a p (j f) -> (a p) j f", f=D), gathered[:, s, :, D:2 * D]).then_inc(v_st[s], 16)

                def body(i, first):
                    for s in range(2):
                        sp.wait_ge(q_mm[s], i)
                        sp.nop(nofuse=True)
                        load_windows(sp, window, s, q_window, 2 * i + s, nw, win_in[s])
                        if not (first and s == 0):
                            store(2 * i + s - 1, i - 1 + s, 1 - s)
                pairs(sp, body)
                store(Q - 1, Q // 2 - 1, 1)
                for s in range(2):
                    sp.wait_ge(v_st[s], 16 * (Q // 2))

            def pe_program(pe, nw):
                def expand(i, s):
                    pe.wait_ge(win_in[s], 16 * J * nw * (i + 1))
                    pe.wait_ge(copied[s], i + 1)
                    pe.wait_ge(multiplied[s], i)
                    for j in range(J):
                        for w in range(nw):
                            mm = pe.matmul(ps_q[s][:, j, :], spread[:, s, w, j, :], window[:, s, w, :], start=(w == 0), stop=(w == nw - 1))
                    mm.then_inc(q_mm[s], 1)

                def body(i, first):
                    for s in range(2):
                        pe.wait_ge(marked[s], i + 1)
                        pe.wait_ge(copied[s], i)
                        for w in range(nw):
                            mm = pe.transpose(ps_t[s][:, w, :], onehot[:, s, w, :, :].rearrange("p j n -> p (j n)"), ident[:, :])
                        mm.then_inc(turned[s], 1)
                        if not (first and s == 0):
                            expand(i - 1 + s, 1 - s)
                pairs(pe, body)
                expand(Q // 2 - 1, 1)

            def act_program(act, nw):
                act.wait_ge(cleared, 1)
                with act.Fori(0, Q // 2) as i:
                    for s in range(2):
                        act.wait_ge(src_in[s], 16 * J * i)
                        act.copy(idx[:, s, :], src_idx[:, bass.ds((2 * i + s) * J, J)]).then_inc(staged[s], 1)
                        act.wait_ge(turned[s], i + 1)
                        act.wait_ge(q_mm[s], i)
                        spread_nodes(act, spread, ps_t, s, nw).then_inc(copied[s], 1)

            def dve_program(dve, nw):
                dve.memset(spread[:, :, :, :, :], 0.0).then_inc(cleared, 1)

                def score(i, s, first):
                    dve.wait_ge(q_mm[s], i + 1)
                    dve.wait_ge(src_in[s], 16 * J * (i + 1))
                    if s == 1 or not first:
                        dve.wait_ge(reduced[1 - s], i + s)
                    dve.tensor_tensor(product[:, :, :], gathered[:, s, :, 0:D], ps_q[s][:, :, :], ALU.mult).then_inc(multiplied[s], 1)
                    dve.wait_ge(multiplied[s], i + 1)
                    dve.tensor_reduce(a_t[:, bass.ds((2 * i + s) * J * H, J * H)], product[:, :, :].rearrange("p j (h o) -> p (j h) o", o=DH),
                                      AX.X, ALU.add).then_inc(reduced[s], 1)

                def body(i, first):
                    for s in range(2):
                        dve.wait_ge(turned[s], i)
                        mark_nodes(dve, onehot, s, 2 * i + s, nw).then_inc(marked[s], 1)
                        if not (first and s == 0):
                            score(i - 1 + s, 1 - s, first)
                pairs(dve, body)
                score(Q // 2 - 1, 1, False)

            with nc.Block() as block:
                @block.gpsimd
                def _(pool):
                    with pool.Fori(0, Q // 2) as i:
                        for s in range(2):
                            pool.wait_ge(staged[s], i + 1)
                            pool.wait_ge(multiplied[s], i)
                            pool.wait_ge(v_st[s], 16 * i)
                            pool.nop(nofuse=True)
                            for j in range(J):
                                pool.indirect_dma_start(gathered[:, s, j, :], None, kv_table,
                                                        bass.IndirectOffsetOnAxis(ap=idx[:, s, j:j + 1], axis=0)).then_inc(src_in[s], 16)

                @block.sync
                def _(sp):
                    both_ways(sp, lambda nw: sync_program(sp, nw))

                @block.tensor
                def _(pe):
                    both_ways(pe, lambda nw: pe_program(pe, nw))

                @block.scalar
                def _(act):
                    both_ways(act, lambda nw: act_program(act, nw))

                @block.vector
                def _(dve):
                    both_ways(dve, lambda nw: dve_program(dve, nw))

    def head_softmax(a_t):
        with ExitStack() as ctx:
            tmp, psum, sem, pair = scope(ctx, "s2")
            val, ex, scratch = (tmp(n, [Q, H, GE]) for n in ("val", "ex", "scratch"))
            ps_s = [psum(f"ps_s{n}", [Q, J, P]) for n in range(2)]
            ps_b = [psum(f"ps_b{n}", [P, J, Q]) for n in range(2)]
            turned, moved, step, exped, back, placed = (sem(n) for n in ("turned", "moved", "step", "exped", "back", "placed"))
            totals_v, totals_t = segment_totals(ctx, "s2t", H)
            heads = lambda a: [a[:, h, :] for h in range(H)]
            scores = a_t[:, :].rearrange("p (q j h) -> p q j h", j=J, h=H)

            with nc.Block() as block:
                @block.tensor
                def _(pe):
                    for h in range(H):
                        if h >= 2:
                            pe.wait_ge(moved, h - 1)
                        for j in range(J):
                            mm = pe.transpose(ps_s[h % 2][:, j, :], scores[:, :, j, h], ident[:, :])
                        mm.then_inc(turned, 1)
                    totals_t(pe, 0)
                    totals_t(pe, 1)
                    for h in range(H):
                        pe.wait_ge(step, 2 * H + h + 1)
                        if h >= 2:
                            pe.wait_ge(placed, 2 * H + h - 1)
                        for j in range(J):
                            mm = pe.transpose(ps_b[h % 2][:, j, :], val[:, h, j * P:(j + 1) * P], ident[0:Q, 0:Q])
                        mm.then_inc(back, 1)

                @block.scalar
                def _(act):
                    for h in range(H):
                        act.wait_ge(turned, h + 1)
                        act.copy(ex[:, h, :], ps_s[h % 2][:, :, :].rearrange("q j e -> q (j e)")).then_inc(moved, 1)
                    for h in range(H):
                        act.wait_ge(step, H + h + 1)
                        act.activation(ex[:, h, :], ex[:, h, :], ACT.Exp).then_inc(exped, 1)

                @block.vector
                def _(dve):
                    for h in range(H):
                        dve.wait_ge(moved, h + 1)
                        dve.tensor_copy(val[:, h, :], ex[:, h, :]).then_inc(step, 1)
                    dve.wait_ge(step, H)
                    totals_v(dve, 0, True, heads(val), heads(scratch))
                    for h in range(H):
                        dve.tensor_tensor(ex[:, h, :], ex[:, h, :], val[:, h, :], ALU.subtract).then_inc(step, 1)
                    dve.wait_ge(exped, H)
                    for h in range(H):
                        cp = dve.tensor_copy(val[:, h, :], ex[:, h, :]).then_inc(placed, 1)
                    dve.wait_ge(placed, H)
                    totals_v(dve, 1, False, heads(val), heads(scratch))
                    for h in range(H):
                        dve.reciprocal(scratch[:, h, :], val[:, h, :]).then_inc(placed, 1)
                    for h in range(H):
                        dve.wait_ge(placed, H + h + 1)
                        dve.tensor_tensor(val[:, h, :], ex[:, h, :], scratch[:, h, :], ALU.mult).then_inc(step, 1)
                    for h in range(H):
                        dve.wait_ge(back, h + 1)
                        dve.tensor_copy(scores[:, :, :, h].rearrange("p q j -> p j q"), ps_b[h % 2][:, :, :]).then_inc(placed, 1)

    def head_sums(a_t, agg2):
        with ExitStack() as ctx:
            tmp, psum, sem, pair = scope(ctx, "g2")
            NWM = P // WIN
            v, weighted = tmp("v", [P, 2, J, D]), tmp("weighted", [P, 2, J, D])
            onehot = tmp("onehot", [P, 2, NWM, J, WIN])
            ps_a = [psum(f"ps_a{s}", [P, NWM, J, WIN]) for s in range(2)]
            cleared, added = sem("cleared"), sem("added")
            v_in, made, a_mm = pair("v_in"), pair("made"), pair("a_mm")

            def pe_program(pe, nw):
                def body(i, first):
                    for s in range(2):
                        pe.wait_ge(made[s], i + 1)
                        if not first:
                            pe.wait_ge(added, J * nw * (2 * i + s - 1))
                        for w in range(nw):
                            for j in range(J):
                                mm = pe.matmul(ps_a[s][:, w, j, :], weighted[:, s, j, :], onehot[:, s, w, j, :], start=True, stop=True)
                        mm.then_inc(a_mm[s], 1)
                pairs(pe, body)

            def dve_program(dve, nw):
                dve.memset(agg2[:, :], 0.0).then_inc(cleared, 1)
                dve.wait_ge(cleared, 1)

                def add(i, s):
                    dve.wait_ge(a_mm[s], i + 1)
                    dve.nop(nofuse=True)
                    add_windows(dve, agg2, ps_a, s, 2 * i + s, nw, added)

                def body(i, first):
                    for s in range(2):
                        dve.wait_ge(a_mm[s], i)
                        dve.wait_ge(v_in[s], 16 * (i + 1))
                        mark_nodes(dve, onehot, s, 2 * i + s, nw)
                        dve.tensor_tensor(weighted[:, s, :, :].rearrange("p j (h o) -> p (j h) o", o=DH),
                                          v[:, s, :, :].rearrange("p j (h o) -> p (j h) o", o=DH),
                                          a_t[:, bass.ds((2 * i + s) * J * H, J * H)].unsqueeze(2).to_broadcast([P, J * H, DH]), ALU.mult).then_inc(made[s], 1)
                        if not (first and s == 0):
                            add(i - 1 + s, 1 - s)
                pairs(dve, body)
                add(Q // 2 - 1, 1)

            with nc.Block() as block:
                @block.sync
                def _(sp):
                    with sp.Fori(0, Q // 2) as i:
                        for s in range(2):
                            sp.wait_ge(made[s], i)
                            sp.dma_start(v[:, s, :, :].rearrange("p j f -> p (j f)"),
                                         v_edges[bass.ds(2 * i + s, 1), :, :].rearrange("a p f -> (a p) f")).then_inc(v_in[s], 16)

                @block.tensor
                def _(pe):
                    both_ways(pe, lambda nw: pe_program(pe, nw))

                @block.vector
                def _(dve):
                    both_ways(dve, lambda nw: dve_program(dve, nw))

    def head_nodes(agg2):
        with ExitStack() as ctx:
            tmp, psum, sem, pair = scope(ctx, "n2")
            wa = tmp("wa", [P, NT, D])
            ln_g, ln_b, film_b, film = tmp("ln_g", [P, D]), tmp("ln_b", [P, D]), tmp("film_b", [P, 2 * D]), tmp("film", [P, 2 * D])
            film_w, context, context_all = tmp("film_w", [CTX, 2 * D]), tmp("context", [CTX, 1]), tmp("context_all", [CTX, P])
            skip, alpha = tmp("skip", [P, NT]), tmp("alpha", [P, NT])
            types, mask = tmp("types", [P, NGRP, K4], I32), tmp("mask", [P, NT, NGRP * K4])
            keep = tmp("keep", [P, NGRP * K4])
            part = tmp("part", [P, GE])
            xg, y, z, v, x3 = (tmp(n, [P, K4, D]) for n in ("xg", "y", "z", "v", "x3"))
            stats, mean_var = tmp("stats", [P, K4, 6]), tmp("mean_var", [P, K4, 2])
            var_eps, root, inverse = (tmp(n, [P, K4]) for n in ("var_eps", "root", "inverse"))
            ps_h = [psum(f"ps_h{k}", [P, 512]) for k in range(K4)]
            ps_f = psum("ps_f", [P, 2 * D])
            weights_in, x_in, parts, h_mm, rooted, vec, pre, stored, film_mm, sig = (sem(n) for n in
                ("weights_in", "x_in", "parts", "h_mm", "rooted", "vec", "pre", "stored", "film_mm", "sig"))
            V = 20
            n_pre = 1 + NT + NT + 2 + NT

            with nc.Block() as block:
                @block.sync
                def _(sp):
                    sp.dma_start(wa[:, :, :], L2_gnn_Wa.rearrange("t f c -> f t c")).then_inc(weights_in, 16)
                    for to, frm, n in ((ln_g, L2_gnn_ln_g, D), (ln_b, L2_gnn_ln_b, D), (film_b, L2_gnn_film_b, 2 * D), (skip, L2_gnn_skip, NT)):
                        sp.dma_start(to[:, :], across(frm, n)).then_inc(weights_in, 16)
                    sp.dma_start(film_w[:, :], L2_gnn_film_w).then_inc(weights_in, 16)
                    sp.dma_start(context[:, :], L2_gnn_global_context.rearrange("(c a) -> c a", a=1)).then_inc(weights_in, 16)
                    sp.dma_start(types[:, :, :], type_pad.rearrange("(g p k) -> p g k", p=P, k=K4)).then_inc(weights_in, 16)
                    with sp.Fori(0, NGRP) as g:
                        sp.wait_ge(vec, V * g)
                        sp.dma_start(xg[:, :, :], rows_of(xs[2], g, D)).then_inc(x_in, 16)
                        sp.wait_ge(vec, V * g + V)
                        sp.dma_start(rows_of(xs[3], g, D), x3[:, :, :]).then_inc(stored, 16)
                    sp.wait_ge(stored, 16 * NGRP)

                @block.tensor
                def _(pe):
                    pe.wait_ge(weights_in, 16 * 8)
                    pe.wait_ge(pre, 1)
                    pe.matmul(ps_f[:, :], context_all[:, :], film_w[:, :], start=True, stop=True).then_inc(film_mm, 1)
                    with pe.Fori(0, NGRP) as g:
                        pe.wait_ge(parts, g + 1)
                        pe.wait_ge(vec, V * g)
                        for k in range(K4):
                            mm = pe.matmul(ps_h[k][:, 0:NT * D], part[:, k::K4], wa[:, :, :].rearrange("f t c -> f (t c)"), start=True, stop=True)
                        mm.then_inc(h_mm, 1)

                @block.scalar
                def _(act):
                    act.wait_ge(weights_in, 16 * 8)
                    act.activation(alpha[:, :], skip[:, :], ACT.Sigmoid).then_inc(sig, 1)
                    with act.Fori(0, NGRP) as g:
                        act.wait_ge(h_mm, g)
                        act.copy(part[:, :], agg2[:, bass.ds(g * GE, GE)]).then_inc(parts, 1)
                        act.wait_ge(vec, V * g + 7)
                        act.activation(root[:, :], var_eps[:, :], ACT.Sqrt).then_inc(rooted, 1)
                        act.wait_ge(vec, V * g + 18)
                        act.activation(root[:, :], var_eps[:, :], ACT.Sqrt).then_inc(rooted, 1)

                @block.vector
                def _(dve):
                    dve.wait_ge(weights_in, 16 * 8)
                    dve.tensor_copy(context_all[:, :], context[:, 0:1].to_broadcast([CTX, P])).then_inc(pre, 1)
                    for t in range(NT):
                        dve.tensor_scalar(mask[:, t, :], types[:, :, :].rearrange("p g k -> p (g k)"), float(t), None, ALU.is_equal).then_inc(pre, 1)
                    dve.wait_ge(pre, 1 + NT)
                    dve.wait_ge(sig, 1)
                    for t in range(NT):
                        dve.tensor_scalar(mask[:, t, :], mask[:, t, :], alpha[:, t:t + 1], None, ALU.mult).then_inc(pre, 1)
                    dve.wait_ge(film_mm, 1)
                    dve.tensor_tensor(film[:, :], ps_f[:, :], film_b[:, :], ALU.add).then_inc(pre, 1)
                    dve.memset(keep[:, :], 1.0).then_inc(pre, 1)
                    for t in range(NT):
                        dve.wait_ge(pre, 1 + 2 * NT + 2 + t)
                        dve.tensor_tensor(keep[:, :], keep[:, :], mask[:, t, :], ALU.subtract).then_inc(pre, 1)
                    dve.wait_ge(pre, n_pre)
                    wide_b = lambda a: a.unsqueeze(1).to_broadcast([P, K4, D])
                    with dve.Fori(0, NGRP) as g:
                        at = V * g
                        dve.wait_ge(h_mm, g + 1)
                        dve.wait_ge(x_in, 16 * (g + 1))
                        for k in range(K4):
                            st = dve.tensor_scalar(y[:, k, :], xg[:, k, :], keep[:, bass.ds(g * K4 + k, 1)], None, ALU.mult)
                        st.then_inc(vec, 1)
                        for t in range(NT):
                            dve.wait_ge(vec, at + 1 + t)
                            to, frm = ((z, y), (y, z), (z, y))[t]
                            for k in range(K4):
                                st = dve.scalar_tensor_tensor(out=to[:, k, :], in0=ps_h[k][:, t * D:(t + 1) * D], scalar=mask[:, t, bass.ds(g * K4 + k, 1)],
                                                              in1=frm[:, k, :], op0=ALU.mult, op1=ALU.add)
                            st.then_inc(vec, 1)
                        dve.wait_ge(vec, at + 4)
                        norm_stats(dve, z, stats, mean_var, var_eps, vec, at + 4)
                        dve.wait_ge(rooted, 2 * g + 1)
                        norm_apply(dve, y, z, mean_var, root, inverse, vec, at + 7)
                        at = at + 9
                        dve.wait_ge(vec, at)
                        dve.tensor_tensor(v[:, :, :], y[:, :, :], wide_b(ln_g[:, :]), ALU.mult).then_inc(vec, 1)
                        dve.wait_ge(vec, at + 1)
                        dve.tensor_tensor(y[:, :, :], v[:, :, :], wide_b(ln_b[:, :]), ALU.add).then_inc(vec, 1)
                        dve.wait_ge(vec, at + 2)
                        dve.tensor_tensor(v[:, :, :], y[:, :, :], xg[:, :, :], ALU.add).then_inc(vec, 1)
                        dve.wait_ge(vec, at + 3)
                        dve.tensor_tensor(y[:, :, :], v[:, :, :], wide_b(film[:, 0:D]), ALU.mult).then_inc(vec, 1)
                        dve.wait_ge(vec, at + 4)
                        dve.tensor_tensor(v[:, :, :], y[:, :, :], wide_b(film[:, D:2 * D]), ALU.add).then_inc(vec, 1)
                        at = at + 5
                        dve.wait_ge(vec, at)
                        dve.tensor_tensor(z[:, :, :], v[:, :, :], xg[:, :, :], ALU.add).then_inc(vec, 1)
                        dve.wait_ge(vec, at + 1)
                        norm_stats(dve, z, stats, mean_var, var_eps, vec, at + 1)
                        dve.wait_ge(rooted, 2 * g + 2)
                        dve.wait_ge(stored, 16 * g)
                        norm_apply(dve, x3, z, mean_var, root, inverse, vec, at + 4)

    def propagate():
        with ExitStack() as ctx:
            tmp, psum, sem, pair = scope(ctx, "e3")
            NWM = P // WIN
            src_all = tmp("src_all", [P, 2, J, P])
            equal = tmp("equal", [P, 2, J, P])
            junk, below, spare = tmp("junk", [P, J, P]), tmp("below", [P, P]), tmp("spare", [P, 1])
            earlier, again, shift = tmp("earlier", [P, 2, J]), tmp("again", [P, 2, J]), tmp("shift", [P, 2, J])
            row = tmp("row", [P, 2, J], I32)
            weighted, merged = tmp("weighted", [P, 2, J, D]), tmp("merged", [P, 2, J, D])
            onehot = tmp("onehot", [P, 2, NWM, J, WIN])
            spread, window = tmp("spread", [P, 2, NWM, J, P]), tmp("window", [P, 2, NWM, D])
            ps_t = [psum(f"ps_t{s}", [P, NWM, P]) for s in range(2)]
            ps_y = [psum(f"ps_y{s}", [P, J, D]) for s in range(2)]
            ps_z = [psum(f"ps_z{s}", [P, J, D]) for s in range(2)]
            cleared = sem("cleared")
            src_in, win_in, marked, turned, copied, y_mm, y_out, compared, z_mm, z_out, placed, counted = (pair(n) for n in
                ("src_in", "win_in", "marked", "turned", "copied", "y_mm", "y_out", "compared", "z_mm", "z_out", "placed", "counted"))
            sent = [sem(f"sent{c}") for c in range(COPIES)]

            def sync_program(sp, nw):
                with sp.Fori(0, Q // 2) as i:
                    for s in range(2):
                        sp.wait_ge(counted[s], i)
                        sp.dma_start(src_all[:, s, :, :].rearrange("p j e -> p (j e)"),
                                     src_row.rearrange("(q e) -> q e", e=GE)[bass.ds(2 * i + s, 1), :].broadcast_to([P, GE])).then_inc(src_in[s], 16)
                        sp.wait_ge(y_mm[s], i)
                        sp.nop(nofuse=True)
                        load_windows(sp, window, s, xs[3], 2 * i + s, nw, win_in[s])

            def pe_program(pe, nw):
                def expand(i, s):
                    pe.wait_ge(win_in[s], 16 * J * nw * (i + 1))
                    pe.wait_ge(copied[s], i + 1)
                    pe.wait_ge(y_out[s], i)
                    for j in range(J):
                        for w in range(nw):
                            mm = pe.matmul(ps_y[s][:, j, :], spread[:, s, w, j, :], window[:, s, w, :], start=(w == 0), stop=(w == nw - 1))
                    mm.then_inc(y_mm[s], 1)

                def merge(i, s):
                    pe.wait_ge(compared[s], i + 1)
                    pe.wait_ge(y_out[s], i + 1)
                    pe.wait_ge(z_out[s], i)
                    for j in range(J):
                        mm = pe.matmul(ps_z[s][:, j, :], equal[:, s, j, :], weighted[:, s, j, :], start=True, stop=True)
                    mm.then_inc(z_mm[s], 1)

                def body(i, first):
                    for s in range(2):
                        pe.wait_ge(marked[s], i + 1)
                        pe.wait_ge(copied[s], i)
                        for w in range(nw):
                            mm = pe.transpose(ps_t[s][:, w, :], onehot[:, s, w, :, :].rearrange("p j n -> p (j n)"), ident[:, :])
                        mm.then_inc(turned[s], 1)
                        if not (first and s == 0):
                            merge(i - 1 + s, 1 - s)
                        expand(i, s)
                pairs(pe, body)
                merge(Q // 2 - 1, 1)

            def act_program(act, nw):
                act.wait_ge(cleared, 3)

                def body(i, first):
                    for s in range(2):
                        act.wait_ge(turned[s], i + 1)
                        act.wait_ge(y_mm[s], i)
                        spread_nodes(act, spread, ps_t, s, nw).then_inc(copied[s], 1)
                        if not (first and s == 0):
                            merged_out(i - 1 + s, 1 - s, s)

                def merged_out(i, s, turn):
                    act.wait_ge(z_mm[s], i + 1)
                    for j in range(J):
                        act.wait_ge(sent[s * J + j], 16 * i)
                    act.copy(merged[:, s, :, :], ps_z[s][:, :, :]).then_inc(z_out[s], 1)
                pairs(act, body)
                merged_out(Q // 2 - 1, 1, 0)

            def dve_program(dve, nw):
                dve.memset(spread[:, :, :, :, :], 0.0).then_inc(cleared, 1)
                dve.tensor_scalar(spare[:, :], ident[:, 0:1], 0.0, None, ALU.mult).then_inc(cleared, 1)
                dve.wait_ge(cleared, 3)
                dve.tensor_tensor_reduce(junk[:, 0, :], ident[:, :], iota[:, 0:P], 1.0, 0.0, ALU.mult, ALU.add, spare[:, :]).then_inc(cleared, 1)
                dve.wait_ge(cleared, 4)
                dve.tensor_scalar(below[:, :], iota[:, 0:P], spare[:, 0:1], None, ALU.is_lt).then_inc(cleared, 1)
                dve.wait_ge(cleared, 5)
                dve.tensor_scalar(spare[:, :], spare[:, :], float(N), None, ALU.add).then_inc(cleared, 1)
                dve.wait_ge(cleared, 6)

                def weigh(i, s):
                    dve.wait_ge(y_mm[s], i + 1)
                    dve.wait_ge(z_mm[s], i)
                    dve.tensor_tensor(weighted[:, s, :, :], ps_y[s][:, :, :],
                                      w_t[:, bass.ds((2 * i + s) * J, J)].unsqueeze(2).to_broadcast([P, J, D]), ALU.mult).then_inc(y_out[s], 1)

                def compare(i, s):
                    q = 2 * i + s
                    dve.wait_ge(src_in[s], 16 * (i + 1))
                    dve.wait_ge(z_mm[s], i)
                    for j in range(J):
                        eq = dve.tensor_scalar(equal[:, s, j, :], src_all[:, s, j, :], src_t[:, bass.ds(q * J + j, 1)], None, ALU.is_equal)
                    eq.then_inc(compared[s], 1)
                    dve.wait_ge(compared[s], i + 1)
                    for j in range(J):
                        cnt = dve.tensor_tensor_reduce(junk[:, j, :], equal[:, s, j, :], below[:, :], 1.0, 0.0, ALU.mult, ALU.add, earlier[:, s, j:j + 1])
                    cnt.then_inc(counted[s], 1)
                    dve.wait_ge(counted[s], i + 1)
                    dve.tensor_scalar(again[:, s, :], earlier[:, s, :], 0.0, None, ALU.is_gt)
                    dve.tensor_scalar(shift[:, s, :], src_t[:, bass.ds(q * J, J)], spare[:, 0:1], -1.0, ALU.subtract, ALU.mult).then_inc(placed[s], 1)
                    dve.wait_ge(placed[s], 3 * i + 1)
                    dve.tensor_tensor(shift[:, s, :], shift[:, s, :], again[:, s, :], ALU.mult).then_inc(placed[s], 1)
                    dve.wait_ge(placed[s], 3 * i + 2)
                    for j in range(J):
                        dve.wait_ge(sent[s * J + j], 16 * i)
                    dve.tensor_tensor(row[:, s, :], shift[:, s, :], src_t[:, bass.ds(q * J, J)], ALU.add).then_inc(placed[s], 1)

                def body(i, first):
                    for s in range(2):
                        dve.wait_ge(turned[s], i)
                        mark_nodes(dve, onehot, s, 2 * i + s, nw).then_inc(marked[s], 1)
                        if s == 1 or not first:
                            dve.wait_ge(counted[1 - s], i + s)
                        compare(i, s)
                        weigh(i, s)
                pairs(dve, body)

            with nc.Block() as block:
                @block.gpsimd
                def _(pool):
                    pool.memset(junk[:, 1, 0:1], 0.0).then_inc(cleared, 1)
                    with pool.Fori(0, Q // 2) as i:
                        for s in range(2):
                            pool.wait_ge(z_out[s], i + 1)
                            pool.wait_ge(placed[s], 3 * (i + 1))
                            for j in range(J):
                                c = s * J + j
                                pool.wait_ge(sent[c], 16 * i)
                                pool.nop(nofuse=True)
                                pool.indirect_dma_start(side[c], bass.IndirectOffsetOnAxis(ap=row[:, s, j:j + 1], axis=0),
                                                        merged[:, s, j, :], None, compute_op=ALU.add).then_inc(sent[c], 16)
                    for c in range(COPIES):
                        pool.wait_ge(sent[c], 16 * (Q // 2))

                @block.sync
                def _(sp):
                    both_ways(sp, lambda nw: sync_program(sp, nw))

                @block.tensor
                def _(pe):
                    both_ways(pe, lambda nw: pe_program(pe, nw))

                @block.scalar
                def _(act):
                    both_ways(act, lambda nw: act_program(act, nw))

                @block.vector
                def _(dve):
                    both_ways(dve, lambda nw: dve_program(dve, nw))

    def last_nodes():
        with ExitStack() as ctx:
            tmp, psum, sem, pair = scope(ctx, "n3")
            xg, total, y, z = (tmp(n, [P, K4, D]) for n in ("xg", "total", "y", "z"))
            parts = tmp("parts", [P, COPIES, K4, D])
            stats, mean_var = tmp("stats", [P, K4, 6]), tmp("mean_var", [P, K4, 2])
            var_eps, root, inverse = (tmp(n, [P, K4]) for n in ("var_eps", "root", "inverse"))
            x_in, rooted, vec, stored = sem("x_in"), sem("rooted"), sem("vec"), sem("stored")
            V = COPIES + 7
            whole = N // GE
            rest = N - whole * GE

            with nc.Block() as block:
                @block.sync
                def _(sp):
                    def body(g, rows):
                        parts_n = rows // K4
                        sp.wait_ge(vec, V * g)
                        if rows == GE:
                            sp.dma_start(xg[:, :, :], rows_of(xs[3], g, D)).then_inc(x_in, 16)
                            for c in range(COPIES):
                                flat = side[c][0:whole * GE, :].rearrange("(a k) f -> a (k f)", k=K4)
                                sp.dma_start(parts[:, c, :, :].rearrange("p k f -> p (k f)"), flat[bass.ds(g * P, P), :]).then_inc(x_in, 16)
                        else:
                            sp.dma_start(xg[:, :, :], rows_of(xs[3], g, D)).then_inc(x_in, 16)
                            for c in range(COPIES):
                                flat = side[c][whole * GE:whole * GE + parts_n * K4, :].rearrange("(a k) f -> a (k f)", k=K4)
                                sp.dma_start(parts[0:parts_n, c, :, :].rearrange("p k f -> p (k f)"), flat).then_inc(x_in, 16)
                        sp.wait_ge(vec, V * (g + 1))
                        if rows == GE:
                            flat = out[0:whole * GE, :].rearrange("(a k) f -> a (k f)", k=K4)
                            sp.dma_start(flat[bass.ds(g * P, P), :], z[:, :, :].rearrange("p k f -> p (k f)")).then_inc(stored, 16)
                        else:
                            n = rest // K4
                            sp.dma_start(out[whole * GE:whole * GE + n * K4, :].rearrange("(a k) f -> a (k f)", k=K4),
                                         z[0:n, :, :].rearrange("p k f -> p (k f)")).then_inc(stored, 16)
                            left = rest - n * K4
                            sp.dma_start(out[N - left:N, :].rearrange("(a k) f -> a (k f)", k=left),
                                         z[n:n + 1, 0:left, :].rearrange("p k f -> p (k f)")).then_inc(stored, 16)
                    with sp.Fori(0, whole) as g:
                        body(g, GE)
                    body(whole, -(-rest // K4) * K4)
                    sp.wait_ge(stored, 16 * (whole + 2))

                @block.scalar
                def _(act):
                    with act.Fori(0, whole + 1) as g:
                        act.wait_ge(vec, V * g + V - 2)
                        act.activation(root[:, :], var_eps[:, :], ACT.Sqrt).then_inc(rooted, 1)

                @block.vector
                def _(dve):
                    with dve.Fori(0, whole + 1) as g:
                        at = V * g
                        dve.wait_ge(x_in, 16 * (COPIES + 1) * (g + 1))
                        dve.tensor_tensor(total[:, :, :], parts[:, 0, :, :], parts[:, 1, :, :], ALU.add).then_inc(vec, 1)
                        for c in range(2, COPIES):
                            dve.wait_ge(vec, at + c - 1)
                            dve.tensor_tensor(total[:, :, :], total[:, :, :], parts[:, c, :, :], ALU.add).then_inc(vec, 1)
                        at = at + COPIES - 1
                        dve.wait_ge(vec, at)
                        dve.scalar_tensor_tensor(out=y[:, :, :], in0=total[:, :, :], scalar=3.0, in1=xg[:, :, :],
                                                 op0=ALU.mult, op1=ALU.add).then_inc(vec, 1)
                        dve.wait_ge(vec, at + 1)
                        dve.tensor_scalar(y[:, :, :], y[:, :, :], 0.25, None, ALU.mult).then_inc(vec, 1)
                        dve.wait_ge(vec, at + 2)
                        dve.tensor_tensor(total[:, :, :], y[:, :, :], xg[:, :, :], ALU.add).then_inc(vec, 1)
                        dve.wait_ge(vec, at + 3)
                        norm_stats(dve, total, stats, mean_var, var_eps, vec, at + 3)
                        dve.wait_ge(rooted, g + 1)
                        dve.wait_ge(stored, 16 * g)
                        norm_apply(dve, z, total, mean_var, root, inverse, vec, at + 6)

    lay_out()
    with ExitStack() as layer0:
        agg = layer0.enter_context(nc.sbuf_tensor("agg0", [P, NP * R], F32))
        share = layer0.enter_context(nc.sbuf_tensor("share", [1, NP * R], F32))
        with ExitStack() as edges0:
            u_keys = edges0.enter_context(nc.sbuf_tensor("u_keys", [P, D], F32))
            e_bias = edges0.enter_context(nc.sbuf_tensor("e_bias", [Q, R], F32))
            e_t = edges0.enter_context(nc.sbuf_tensor("e_t", [P, T], F32))
            rel_tables(u_keys, e_bias, agg, share)
            rel_scores(u_keys, e_t)
            rel_softmax(e_t, e_bias)
        rel_sums(agg, share)
        rel_nodes(agg, share)
    layer1 = top.enter_context(ExitStack())
    agg1 = layer1.enter_context(nc.sbuf_tensor("agg1", [P, NP], F32))
    messages(agg1)
    message_nodes(agg1)
    layer1.close()
    with ExitStack() as layer2:
        a_t = layer2.enter_context(nc.sbuf_tensor("a_t", [P, T * H], F32))
        agg2 = layer2.enter_context(nc.sbuf_tensor("agg2", [P, NP], F32))
        head_scores(a_t)
        head_softmax(a_t)
        head_sums(a_t, agg2)
        head_nodes(agg2)
    propagate()
    last_nodes()
    top.close()


OUT = ((N, D), "float32")


def kernel(**inputs):
    import numpy as np
    import concourse.bacc as bacc
    from concourse.bass_utils import run_bass_kernel_spmd

    nc = bacc.Bacc("TRN2", target_bir_lowering=False, num_devices=1)
    arrays, args = {}, {}
    for name, value in inputs.items():
        a = np.ascontiguousarray(value)
        arrays[f"in_{name}_dram"] = a
        args[name] = nc.dram_tensor(f"in_{name}_dram", a.shape, mybir.dt.from_np(a.dtype), kind="ExternalInput").ap()
    args["out"] = nc.dram_tensor("out_0_dram", OUT[0], mybir.dt.from_np(np.dtype(OUT[1])), kind="ExternalOutput").ap()
    build(nc, **args)
    result = run_bass_kernel_spmd(nc, [arrays], core_ids=[0])
    return result.results[0]["out_0_dram"]
```

```python
from contextlib import ExitStack

import concourse.bass as bass
from concourse import mybir
from concourse.alu_op_type import AluOpType as ALU

ACT = mybir.ActivationFunctionType
AX = mybir.AxisListType
F32 = mybir.dt.float32
I32 = mybir.dt.int32

P = 128
N = 3125
D = 128
E = 53125
J = 4
GE = J * P
Q = -(-E // GE)
T = Q * J
R = 4
H, DH = 8, 16
NT = 3
REL = 64
CTX = 64
K4 = 4
NGRP = -(-(N + 1 + P) // GE)
NP = NGRP * GE
WIN = 32
KEYS = WIN * R
EPS = 1e-5
BIG = 3e30
NEG = 1e30
COPIES = 8
U = 4


def build(nc, x, src, dst, edge_attr_64, edge_type_4, edge_weight, node_type_3,
          L0_gnn_W_R, L0_gnn_b_R, L0_gnn_W_Q, L0_gnn_b_Q, L0_gnn_W_K, L0_gnn_b_K, L0_gnn_W_V, L0_gnn_b_V,
          L0_gnn_a_w, L0_gnn_a_b, L1_gnn_W1, L1_gnn_b1, L1_gnn_W2, L1_gnn_b2, L1_gnn_Wn, L1_gnn_bn,
          L1_gnn_gamma, L1_gnn_beta, L2_gnn_global_context, L2_gnn_Wk, L2_gnn_Wq, L2_gnn_Wv,
          L2_gnn_rel_att, L2_gnn_rel_msg, L2_gnn_rel_pri, L2_gnn_Wa, L2_gnn_skip, L2_gnn_ln_g,
          L2_gnn_ln_b, L2_gnn_film_w, L2_gnn_film_b, out):
    top = ExitStack()

    def dram(name, shape, dt=F32):
        return nc.dram_tensor(name, shape, dt, kind="Internal").ap()

    xs = [dram(f"x_layer{n}", [NP, D]) for n in range(4)]
    type_pad = dram("node_type_padded", [NP], I32)
    base_row = dram("tile_base", [T], I32)
    src_row = dram("src_padded", [T * P])
    rel_table = dram("rel_src_table", [NP * R, D])
    rel_window = dram("rel_dst_table", [NP * R, D])
    rel_edges = dram("rel_edges", [Q, P, J * D])
    msg_table = dram("msg_src_table", [NP, D])
    msg_window = dram("msg_dst_table", [NP, D])
    kv_table = dram("kv_table", [NP, 2 * D])
    q_window = dram("q_table", [NP, D])
    v_edges = dram("v_edges", [Q, P, J * D])
    side = [dram(f"side_{c}", [N + P, D]) for c in range(COPIES)]

    def sb(name, shape, dt=F32):
        return top.enter_context(nc.sbuf_tensor(name, shape, dt))

    ident = sb("ident", [P, P])
    iota = sb("iota", [P, R * P])
    ones = sb("ones", [P, P])
    key_t = sb("key_t", [P, T])
    dl_t = sb("dl_t", [P, T])
    rel_idx = sb("rel_idx", [P, T], I32)
    src_idx = sb("src_idx", [P, T], I32)
    src_t = sb("src_t", [P, T])
    w_t = sb("w_t", [P, T])
    attn_t = sb("attn_t", [P, T])
    base_sb = sb("base_sb", [1, T], I32)
    typ_s = sb("typ_s", [Q, GE])
    pen = sb("pen", [Q, GE + 1])
    same = sb("same", [Q, GE + 1])
    in_first = sb("in_first", [Q, GE])
    in_last = sb("in_last", [Q, GE])
    pen_first = sb("pen_first", [Q, GE])
    pen_last = sb("pen_last", [Q, GE])
    cont = sb("cont", [H, Q + 1])
    through = sb("through", [H, Q + 2])
    wide = sb("wide", [1, 1], I32)

    def window_base(engines, q, j):
        return nc.values_load(base_sb[0:1, bass.ds(q * J + j, 1)], engines=engines, min_val=0, max_val=N,
                              skip_runtime_bounds_check_because="dst is a node")

    def lay_out():
        with ExitStack() as ctx:
            def tmp(name, shape, dt=F32):
                return ctx.enter_context(nc.sbuf_tensor(name, shape, dt))

            def sem(name):
                return ctx.enter_context(nc.semaphore(name))

            src_i, dst_i, typ_i = (tmp(n, [Q, GE], I32) for n in ("src_i", "dst_i", "typ_i"))
            w_s, src_s, dst_s, dl_s, key_s, idx_s = (tmp(n, [Q, GE]) for n in
                                                      ("w_s", "src_s", "dst_s", "dl_s", "key_s", "idx_s"))
            base_i = tmp("base_i", [Q, J], I32)
            top_s = tmp("top_s", [Q, 1])
            ends = tmp("ends", [Q, 2, H])
            rows = tmp("rows", [H, 2, Q])
            zero_x = tmp("zero_x", [P, 4 * D])
            zero_i = tmp("zero_i", [NP - N, 1], I32) if NP - N <= P else tmp("zero_i", [1, NP - N], I32)
            zeros_set, edges_in, pads_in, made, moved, turned, stored = (sem(n) for n in
                ("zeros_set", "edges_in", "pads_in", "made", "moved", "turned", "stored"))
            ps = [ctx.enter_context(nc.psum_tensor(f"lay_ps{i}", [P, J, Q], F32)) for i in range(5)]
            ps_row = ctx.enter_context(nc.psum_tensor("lay_row", [H, 2, P], F32))
            ps_top = ctx.enter_context(nc.psum_tensor("lay_top", [1, P], F32))
            last = E - (Q - 1) * GE

            with nc.Block() as block:
                @block.gpsimd
                def _(pool):
                    pool.memset(src_i[:, :], 0).then_inc(zeros_set, 1)
                    pool.memset(dst_i[:, :], N).then_inc(zeros_set, 1)
                    pool.memset(typ_i[:, :], 0).then_inc(zeros_set, 1)
                    pool.memset(w_s[:, :], 0.0).then_inc(zeros_set, 1)
                    pool.memset(zero_x[:, :], 0.0).then_inc(zeros_set, 1)
                    pool.memset(zero_i[:, :], 0).then_inc(zeros_set, 1)
                    pool.memset(ones[:, :], 1.0).then_inc(zeros_set, 1)
                    pool.memset(ident[:, :], 0.0).then_inc(made, 1)
                    pool.wait_ge(made, 1)
                    pool.affine_select(out=ident[:, :], in_=ident[:, :], compare_op=ALU.not_equal, fill=1.0,
                                       base=0, pattern=[[-1, P]], channel_multiplier=1).then_inc(made, 1)
                    pool.iota(iota[:, :], [[1, R * P]], base=0, channel_multiplier=0,
                              allow_small_or_imprecise_dtypes=True).then_inc(made, 1)

                @block.sync
                def _(sp):
                    sp.wait_ge(zeros_set, 7)
                    for to, frm in ((src_i, src), (dst_i, dst), (typ_i, edge_type_4), (w_s, edge_weight)):
                        sp.dma_start(to[0:Q - 1, :], frm[0:(Q - 1) * GE].rearrange("(q e) -> q e", e=GE)).then_inc(edges_in, 16)
                        sp.dma_start(to[Q - 1:Q, 0:last], frm[(Q - 1) * GE:E].rearrange("(q e) -> q e", q=1)).then_inc(edges_in, 16)
                    sp.dma_start(xs[0][0:N, :], x).then_inc(pads_in, 16)
                    a = N
                    while a < NP:
                        n = min(P, NP - a)
                        sp.dma_start(xs[0][a:a + n, :], zero_x[0:n, 0:D]).then_inc(pads_in, 16)
                        a += n
                    sp.dma_start(type_pad[0:N].rearrange("(a n) -> a n", a=5), node_type_3.rearrange("(a n) -> a n", a=5)).then_inc(pads_in, 16)
                    sp.dma_start(type_pad[N:NP].rearrange("(a n) -> a n", a=1), zero_i[:, :]).then_inc(pads_in, 16)
                    n_pads = 3 + -(-(NP - N) // P)
                    for c in range(COPIES):
                        a = 0
                        full = (N // (4 * P)) * 4 * P
                        while a < full:
                            sp.dma_start(side[c][a:a + 4 * P, :].rearrange("(p k) f -> p (k f)", k=4), zero_x[:, :]).then_inc(pads_in, 16)
                            a += 4 * P
                            n_pads += 1
                        while a < N + P:
                            n = min(P, N + P - a)
                            sp.dma_start(side[c][a:a + n, :], zero_x[0:n, 0:D]).then_inc(pads_in, 16)
                            a += n
                            n_pads += 1
                    sp.wait_ge(moved, 2)
                    sp.dma_start(base_row.rearrange("(q j) -> q j", j=J), base_i[:, :]).then_inc(stored, 16)
                    sp.dma_start(src_row.rearrange("(q e) -> q e", e=GE), src_s[:, :]).then_inc(stored, 16)
                    sp.wait_ge(stored, 32)
                    sp.dma_start(base_sb[:, :], base_row.rearrange("(a t) -> a t", a=1)).then_inc(stored, 16)
                    sp.wait_ge(stored, 48)
                    sp.wait_ge(pads_in, 16 * n_pads)

                @block.vector
                def _(dve):
                    dve.wait_ge(edges_in, 16 * 8)
                    dve.tensor_copy(src_s[:, :], src_i[:, :]).then_inc(moved, 1)
                    dve.tensor_copy(base_i[:, :], dst_i[:, ::P]).then_inc(moved, 1)
                    dve.tensor_copy(dst_s[:, :], dst_i[:, :]).then_inc(moved, 1)
                    dve.tensor_copy(typ_s[:, :], typ_i[:, :]).then_inc(moved, 1)
                    dve.wait_ge(moved, 4)
                    tiles = lambda a: a[:, :].rearrange("q (j e) -> q j e", e=P)
                    dve.tensor_tensor(tiles(dl_s), tiles(dst_s), tiles(dst_s)[:, :, 0:1].to_broadcast([Q, J, P]),
                                      ALU.subtract).then_inc(moved, 1)
                    dve.scalar_tensor_tensor(out=idx_s[:, :], in0=src_s[:, :], scalar=float(R), in1=typ_s[:, :],
                                             op0=ALU.mult, op1=ALU.add).then_inc(moved, 1)
                    dve.wait_ge(moved, 5)
                    dve.scalar_tensor_tensor(out=key_s[:, :], in0=dl_s[:, :], scalar=float(R), in1=typ_s[:, :],
                                             op0=ALU.mult, op1=ALU.add).then_inc(moved, 1)
                    dve.tensor_reduce(top_s[:, :], dl_s[:, :], AX.X, ALU.max).then_inc(moved, 1)
                    dve.memset(same[:, :], 0.0).then_inc(moved, 1)
                    dve.wait_ge(moved, 9)
                    dve.tensor_tensor(same[:, 1:GE], dst_s[:, 1:GE], dst_s[:, 0:GE - 1], ALU.is_equal).then_inc(moved, 1)
                    dve.tensor_scalar(in_first[:, :], dst_s[:, :], dst_s[:, 0:1], None, ALU.is_equal).then_inc(moved, 1)
                    dve.tensor_scalar(in_last[:, :], dst_s[:, :], dst_s[:, GE - 1:GE], None, ALU.is_equal).then_inc(moved, 1)
                    dve.tensor_copy(ends[:, 0, :], dst_s[:, 0:1].to_broadcast([Q, H])).then_inc(moved, 1)
                    dve.tensor_copy(ends[:, 1, :], dst_s[:, GE - 1:GE].to_broadcast([Q, H])).then_inc(moved, 1)
                    dve.wait_ge(moved, 14)
                    for to, frm in ((pen, same), (pen_first, in_first), (pen_last, in_last)):
                        dve.tensor_scalar(to[:, :], frm[:, :], 1.0, BIG, ALU.subtract, ALU.mult).then_inc(moved, 1)
                    for n, to in enumerate((dl_t, key_t, src_t, rel_idx, w_t)):
                        dve.wait_ge(turned, n + 1)
                        dve.tensor_copy(to[:, :].rearrange("p (q j) -> p j q", j=J), ps[n][:, :, :]).then_inc(moved, 1)
                    dve.wait_ge(turned, 6)
                    dve.tensor_copy(rows[:, :, :], ps_row[:, :, 0:Q]).then_inc(moved, 1)
                    dve.memset(cont[:, :], 0.0).then_inc(moved, 1)
                    dve.memset(through[:, :], 0.0).then_inc(moved, 1)
                    dve.wait_ge(moved, 25)
                    dve.tensor_copy(src_idx[:, :], src_t[:, :]).then_inc(moved, 1)
                    dve.tensor_tensor(cont[:, 1:Q], rows[:, 0, 1:Q], rows[:, 1, 0:Q - 1], ALU.is_equal).then_inc(moved, 1)
                    dve.tensor_tensor(through[:, 1:Q + 1], rows[:, 0, :], rows[:, 1, :], ALU.is_equal).then_inc(moved, 1)
                    dve.wait_ge(turned, 7)
                    dve.tensor_reduce(wide[:, :], ps_top[:, 0:Q], AX.X, ALU.max).then_inc(moved, 1)

                @block.tensor
                def _(pe):
                    pe.wait_ge(made, 2)
                    for n, (frm, ready) in enumerate(((dl_s, 5), (key_s, 7), (src_s, 7), (idx_s, 7), (w_s, 7))):
                        pe.wait_ge(moved, ready)
                        for j in range(J):
                            turn = pe.transpose(ps[n][:, j, :], frm[:, j * P:(j + 1) * P], ident[0:Q, 0:Q])
                        turn.then_inc(turned, 1)
                    pe.wait_ge(moved, 14)
                    for n in range(2):
                        turn = pe.transpose(ps_row[:, n, 0:Q], ends[:, n, :], ident[0:Q, 0:Q])
                    turn.then_inc(turned, 1)
                    pe.transpose(ps_top[:, 0:Q], top_s[:, :], ident[0:Q, 0:Q]).then_inc(turned, 1)


    def rows_of(table, g, width):
        flat = table.rearrange("(a k) f -> a (k f)", k=K4)
        return flat[bass.ds(g * P, P), :].rearrange("p (k f) -> p k f", f=width)

    def across(vector, n, parts=P):
        return vector.rearrange("(a n) -> a n", a=1).broadcast_to([parts, n])

    def scope(ctx, tag, slots=2):
        taken = []

        def sem(name):
            taken.append(nc.alloc_semaphore(f"{tag}_{name}"))
            return taken[-1]

        def give_back():
            nc.clear_and_free_semaphores(taken)
            nc.all_engine_barrier()

        ctx.callback(give_back)
        return (lambda name, shape, dt=F32: ctx.enter_context(nc.sbuf_tensor(f"{tag}_{name}", shape, dt)),
                lambda name, shape: ctx.enter_context(nc.psum_tensor(f"{tag}_{name}", shape, F32)),
                sem,
                lambda name, n=slots: [sem(f"{name}{s}") for s in range(n)])

    def both_ways(eng, program):
        reach = nc.values_load(wide[0:1, 0:1], engines=[eng.engine], min_val=0, max_val=P - 1,
                               skip_runtime_bounds_check_because="every node has an edge of its own")
        with eng.If(reach < WIN):
            program(1)
        with eng.Else():
            program(P // WIN)

    def pairs(eng, body):
        body(0, True)
        with eng.Fori(1, Q // 2) as i:
            body(i, False)

    def pipeline(eng, *stages):
        def turn(i, first=False, last=False):
            for u in range(U):
                for work, lag in stages:
                    if not (first and u < lag) and not (last and u >= lag):
                        work(U * i + (u - lag), lambda slots, n=u - lag: (n % slots, (U // slots) * i + n // slots))
        turn(0, first=True)
        with eng.Fori(1, Q // U) as i:
            turn(i)
        turn(Q // U, last=True)

    def hold(eng, semaphore, count):
        if not (isinstance(count, int) and count <= 0):
            eng.wait_ge(semaphore, count)

    def over_groups(eng, work):
        work(0, False)
        with eng.Fori(1, NGRP - 1) as g:
            work(g, False)
        work(NGRP - 1, True)

    def gathers(pool, slots, numbers, all_numbers, staged, to, table, src_in, freed):
        def gather(q, at):
            s, c = at(slots)
            for semaphore, adds in freed:
                hold(pool, semaphore[s], adds * c)
            pool.nop(nofuse=True)
            pool.tensor_copy(numbers[:, s, :], all_numbers[:, bass.ds(q * J, J)]).then_inc(staged[s], 1)
            pool.wait_ge(staged[s], c + 1)
            pool.nop(nofuse=True)
            for j in range(J):
                pool.indirect_dma_start(to[:, s, j, :], None, table,
                                        bass.IndirectOffsetOnAxis(ap=numbers[:, s, j:j + 1], axis=0)).then_inc(src_in[s], 16)
        pipeline(pool, (gather, 0))

    def rel_tables(u_keys, e_bias, agg, share):
        with ExitStack() as ctx:
            tmp, psum, sem, pair = scope(ctx, "t0")
            w_up, w_low = tmp("w_up", [P, R, D]), tmp("w_low", [P, R, D])
            b_all = tmp("b_all", [P, R * D])
            wq, wk = tmp("wq", [P, R, D]), tmp("wk", [P, R, D])
            a_all = tmp("a_all", [P, 2 * D])
            bq, bk = tmp("bq", [Q, R, D]), tmp("bk", [Q, R, D])
            ab = tmp("ab", [Q, 1])
            junk = tmp("junk", [P, 4 * R, D])
            u_part, u_col = tmp("u_part", [P, 2, R]), tmp("u_col", [P, R])
            c_part = tmp("c_part", [Q, 2, R])
            u_rows, spread = tmp("u_rows", [R, D]), tmp("spread", [R, P])
            xg, xt = tmp("xg", [P, K4, D]), tmp("xt", [P, K4, D])
            up, low = tmp("up", [P, K4, R * D]), tmp("low", [P, K4, R * D])
            ps_x, ps_u = psum("ps_x", [P, K4, D]), psum("ps_u", [P, D])
            ps_up = [psum(f"ps_up{n}", [P, R * D]) for n in range(2)]
            ps_low = [psum(f"ps_low{n}", [P, R * D]) for n in range(2)]
            weights_in, dots, u_mm, u_copied, x_in, turned, xt_ready, up_mm, low_mm, up_out, low_out, up_st, low_st, cleared = (
                sem(n) for n in ("weights_in", "dots", "u_mm", "u_copied", "x_in", "turned", "xt_ready", "up_mm", "low_mm",
                                 "up_out", "low_out", "up_st", "low_st", "cleared"))

            with nc.Block() as block:
                @block.sync
                def _(sp):
                    for to, frm in ((w_up, L0_gnn_W_R[:, 0:D, :]), (w_low, L0_gnn_W_R[:, D:2 * D, :]), (wq, L0_gnn_W_Q), (wk, L0_gnn_W_K)):
                        sp.dma_start(to[:, :, :], frm.rearrange("r f g -> f r g")).then_inc(weights_in, 16)
                    sp.dma_start(b_all[:, :], across(L0_gnn_b_R.rearrange("r f -> (r f)"), R * D)).then_inc(weights_in, 16)
                    sp.dma_start(a_all[:, :], across(L0_gnn_a_w.rearrange("f a -> (f a)"), 2 * D)).then_inc(weights_in, 16)
                    for to, frm in ((bq, L0_gnn_b_Q), (bk, L0_gnn_b_K)):
                        sp.dma_start(to[:, :, :].rearrange("q r f -> q (r f)"), across(frm.rearrange("r f -> (r f)"), R * D, Q)).then_inc(weights_in, 16)
                    sp.dma_start(ab[:, :], across(L0_gnn_a_b, 1, Q)).then_inc(weights_in, 16)
                    sp.dma_start(xg[:, :, :], rows_of(xs[0], 0, D)).then_inc(x_in, 16)

                    def store(g):
                        sp.wait_ge(up_out, 4 * (g + 1))
                        sp.dma_start(rows_of(rel_table.rearrange("(n r) f -> n (r f)", r=R), g, R * D), up[:, :, :]).then_inc(up_st, 16)
                        sp.wait_ge(low_out, 4 * (g + 1))
                        sp.dma_start(rows_of(rel_window.rearrange("(n r) f -> n (r f)", r=R), g, R * D), low[:, :, :]).then_inc(low_st, 16)

                    with sp.Fori(0, NGRP - 1) as g:
                        sp.wait_ge(turned, g + 1)
                        sp.dma_start(xg[:, :, :], rows_of(xs[0], g + 1, D)).then_inc(x_in, 16)
                        store(g)
                    store(NGRP - 1)
                    sp.wait_ge(up_st, 16 * NGRP)
                    sp.wait_ge(low_st, 16 * NGRP)

                @block.gpsimd
                def _(pool):
                    pool.memset(agg[:, :], 0.0).then_inc(cleared, 1)
                    pool.memset(share[:, :], 0.0).then_inc(cleared, 1)

                @block.tensor
                def _(pe):
                    pe.wait_ge(dots, 1)
                    pe.transpose(ps_u[0:R, :], u_col[:, :], ident[:, :]).then_inc(u_mm, 1)
                    pe.wait_ge(u_copied, 2)
                    pe.matmul(ps_u[:, :], spread[:, :], u_rows[:, :], start=True, stop=True).then_inc(u_mm, 1)
                    pe.wait_ge(weights_in, 16 * 9)
                    with pe.Fori(0, NGRP) as g:
                        pe.wait_ge(x_in, 16 * (g + 1))
                        pe.wait_ge(xt_ready, g)
                        for k in range(K4):
                            turn = pe.transpose(ps_x[:, k, :], xg[:, k, :], ident[:, :])
                        turn.then_inc(turned, 1)
                        pe.wait_ge(xt_ready, g + 1)
                        for k in range(K4):
                            pe.wait_ge(up_out, 4 * g + max(k - 1, 0))
                            pe.matmul(ps_up[k % 2][:, :], xt[:, k, :], w_up[:, :, :].rearrange("f r g -> f (r g)"), start=True, stop=True).then_inc(up_mm, 1)
                            pe.wait_ge(low_out, 4 * g + max(k - 1, 0))
                            pe.matmul(ps_low[k % 2][:, :], xt[:, k, :], w_low[:, :, :].rearrange("f r g -> f (r g)"), start=True, stop=True).then_inc(low_mm, 1)

                @block.scalar
                def _(act):
                    with act.Fori(0, NGRP) as g:
                        act.wait_ge(turned, g + 1)
                        act.wait_ge(low_mm, 4 * g)
                        act.copy(xt[:, :, :], ps_x[:, :, :]).then_inc(xt_ready, 1)
                        act.wait_ge(up_st, 16 * g)
                        for k in range(K4):
                            act.wait_ge(up_mm, 4 * g + k + 1)
                            act.copy(up[:, k, :], ps_up[k % 2][:, :]).then_inc(up_out, 1)

                @block.vector
                def _(dve):
                    dve.wait_ge(weights_in, 16 * 9)
                    for n, (w, b) in enumerate(((wq, bq), (wk, bk))):
                        for r in range(R):
                            dve.tensor_tensor_reduce(junk[:, 2 * R * n + r, :], w[:, r, :], a_all[:, n * D:(n + 1) * D], 1.0, 0.0,
                                                     ALU.mult, ALU.add, u_part[:, n, r:r + 1]).then_inc(cleared, 1)
                            dve.tensor_tensor_reduce(junk[0:Q, 2 * R * n + R + r, :], b[:, r, :], a_all[0:Q, n * D:(n + 1) * D], 1.0, 0.0,
                                                     ALU.mult, ALU.add, c_part[:, n, r:r + 1]).then_inc(cleared, 1)
                    dve.wait_ge(cleared, 2 + 4 * R)
                    dve.tensor_tensor(u_col[:, :], u_part[:, 0, :], u_part[:, 1, :], ALU.add).then_inc(dots, 1)
                    dve.tensor_tensor(e_bias[:, :], c_part[:, 0, :], c_part[:, 1, :], ALU.add).then_inc(dots, 1)
                    dve.wait_ge(dots, 2)
                    dve.tensor_scalar(e_bias[:, :], e_bias[:, :], ab[:, 0:1], None, ALU.add).then_inc(dots, 1)
                    dve.wait_ge(u_mm, 1)
                    dve.tensor_copy(u_rows[:, :], ps_u[0:R, :]).then_inc(u_copied, 1)
                    dve.tensor_copy(spread[:, :].rearrange("r (n c) -> r n c", c=R),
                                    ident[0:R, 0:R].unsqueeze(1).to_broadcast([R, WIN, R])).then_inc(u_copied, 1)
                    dve.wait_ge(u_mm, 2)
                    dve.tensor_copy(u_keys[:, :], ps_u[:, :]).then_inc(u_copied, 1)
                    with dve.Fori(0, NGRP) as g:
                        dve.wait_ge(low_st, 16 * g)
                        for k in range(K4):
                            dve.wait_ge(low_mm, 4 * g + k + 1)
                            dve.tensor_tensor(low[:, k, :], ps_low[k % 2][:, :], b_all[:, :], ALU.add).then_inc(low_out, 1)

    def rel_scores(u_keys, e_t):
        with ExitStack() as ctx:
            tmp, psum, sem, pair = scope(ctx, "e0")
            S = 4
            idx = tmp("idx", [P, S, J], I32)
            gathered, window, rel = (tmp(n, [P, S, J, D]) for n in ("gathered", "window", "rel"))
            onehot, spread = tmp("onehot", [P, 2, J, KEYS]), tmp("spread", [P, 2, J, P])
            low, junk = tmp("low", [P, 2, J, D]), tmp("junk", [P, 2, J, D])
            e_now = tmp("e_now", [P, 2, J])
            ps_t, ps_r, ps_u = ([psum(f"{n}{s}", [P, J, D]) for s in range(2)] for n in ("ps_t", "ps_r", "ps_u"))
            staged, src_in, win_in, rel_made, rel_st = (pair(n, S) for n in ("staged", "src_in", "win_in", "rel_made", "rel_st"))
            used = pair("used", S)
            marked, turned, copied, added, dotted, e_made = (pair(n) for n in ("marked", "turned", "copied", "added", "dotted", "e_made"))

            def lags(nw, narrow):
                return narrow if nw == 1 else 0

            def sync_program(sp, nw):
                def load(q, at):
                    s, c = at(S)
                    for w in range(nw):
                        hold(sp, used[s], c * nw + w)
                        sp.nop(nofuse=True)
                        for j in range(J):
                            base = window_base([sp.engine], q, j)
                            sp.dma_start(window[:, s, j, :], rel_window[bass.ds(base * R + w * KEYS, KEYS), :]).then_inc(win_in[s], 16)

                def store(q, at):
                    s, c = at(S)
                    sp.wait_ge(rel_made[s], c + 1)
                    sp.dma_start(rel_edges[bass.ds(q, 1), :, :].rearrange("a p f -> (a p) f"),
                                 rel[:, s, :, :].rearrange("p j f -> p (j f)")).then_inc(rel_st[s], 16)

                pipeline(sp, (load, 0), (store, lags(nw, 3)))
                for s in range(S):
                    sp.wait_ge(rel_st[s], 16 * (Q // S))

            def pe_program(pe, nw):
                def turn(q, at, w=0):
                    s, c = at(2)
                    pe.wait_ge(marked[s], c * nw + w + 1)
                    hold(pe, copied[s], c * nw + w)
                    for j in range(J):
                        mm = pe.transpose(ps_t[s][:, j, :], onehot[:, s, j, :], ident[:, :])
                    mm.then_inc(turned[s], 1)

                def expand(q, at):
                    s, c = at(2)
                    s4, c4 = at(S)
                    hold(pe, dotted[s], c)
                    for w in range(nw):
                        if w > 0:
                            turn(q, at, w)
                        pe.wait_ge(win_in[s4], 16 * J * (c4 * nw + w + 1))
                        pe.wait_ge(copied[s], c * nw + w + 1)
                        for j in range(J):
                            pe.matmul(ps_r[s][:, j, :], spread[:, s, j, :], window[:, s4, j, :], start=(w == 0 and (nw == 1 or j == 0)), stop=(w == nw - 1), skip_group_check=True)
                            mm = pe.matmul(ps_u[s][:, j, :], spread[:, s, j, :], u_keys[:, :], start=(w == 0 and (nw == 1 or j == 0)), stop=(w == nw - 1), skip_group_check=True)
                        mm.then_inc(used[s4], 1)
                pipeline(pe, (turn, 0), (expand, lags(nw, 1)))

            def act_program(act, nw):
                def copy(q, at):
                    s, c = at(2)
                    for w in range(nw):
                        act.wait_ge(turned[s], c * nw + w + 1)
                        if w > 0:
                            s4, c4 = at(S)
                            act.wait_ge(used[s4], c4 * nw + w)
                        else:
                            s4, c4 = at(S)
                            before = (s4 + 2) % S
                            hold(act, used[before], (c4 + (1 if s4 >= 2 else 0)) * nw)
                        act.copy(spread[:, s, :, :], ps_t[s][:, :, :]).then_inc(copied[s], 1)
                pipeline(act, (copy, 0))

            def dve_program(dve, nw):
                def mark(q, at):
                    s, c = at(2)
                    for w in range(nw):
                        hold(dve, turned[s], c * nw + w)
                        for j in range(J):
                            mk = dve.tensor_scalar(onehot[:, s, j, :], iota[:, w * KEYS:(w + 1) * KEYS],
                                                   key_t[:, bass.ds(q * J + j, 1)], None, ALU.is_equal)
                        mk.then_inc(marked[s], 1)

                def add(q, at):
                    s, c = at(2)
                    s4, c4 = at(S)
                    dve.wait_ge(used[s4], (c4 + 1) * nw)
                    dve.wait_ge(src_in[s4], 16 * J * (c4 + 1))
                    hold(dve, dotted[s], c)
                    dve.tensor_tensor(low[:, s, :, :], gathered[:, s4, :, :], ps_r[s][:, :, :], ALU.add).then_inc(added[s], 1)

                def score(q, at):
                    s, c = at(2)
                    s4, c4 = at(S)
                    dve.wait_ge(added[s], c + 1)
                    hold(dve, rel_st[s4], 16 * c4)
                    dve.scalar_tensor_tensor(out=rel[:, s4, :, :], in0=low[:, s, :, :], scalar=0.2, in1=low[:, s, :, :],
                                             op0=ALU.mult, op1=ALU.max).then_inc(rel_made[s4], 1)

                def dot(q, at):
                    s, c = at(2)
                    s4, c4 = at(S)
                    dve.wait_ge(rel_made[s4], c4 + 1)
                    hold(dve, e_made[s], c)
                    for j in range(J):
                        dt = dve.tensor_tensor_reduce(junk[:, s, j, :], rel[:, s4, j, :], ps_u[s][:, j, :], 1.0, 0.0, ALU.mult, ALU.add, e_now[:, s, j:j + 1])
                    dt.then_inc(dotted[s], 1)
                    dve.wait_ge(dotted[s], c + 1)
                    dve.tensor_copy(e_t[:, bass.ds(q * J, J)], e_now[:, s, :]).then_inc(e_made[s], 1)
                pipeline(dve, (mark, 0), (add, lags(nw, 2)), (score, lags(nw, 2)), (dot, lags(nw, 2)))

            with nc.Block() as block:
                @block.gpsimd
                def _(pool):
                    gathers(pool, S, idx, rel_idx, staged, gathered, rel_table, src_in, [(rel_made, 1)])

                @block.sync
                def _(sp):
                    both_ways(sp, lambda nw: sync_program(sp, nw))

                @block.tensor
                def _(pe):
                    both_ways(pe, lambda nw: pe_program(pe, nw))

                @block.scalar
                def _(act):
                    both_ways(act, lambda nw: act_program(act, nw))

                @block.vector
                def _(dve):
                    both_ways(dve, lambda nw: dve_program(dve, nw))

    def segment_totals(ctx, tag, n):
        tmp, psum, sem, pair = scope(ctx, tag)
        ends, rows = tmp("ends", [Q, 2, n]), tmp("rows", [n, 2, Q + 2])
        chain, gate, links = tmp("chain", [n, 2, Q]), tmp("gate", [n, 2, Q]), tmp("links", [n, 2, Q])
        back = tmp("back", [Q, 2, n])
        ps_rows, ps_back = psum("ps_rows", [n, 2, Q + 2]), psum("ps_back", [Q, 2, n])
        done, turned = sem("done"), sem("turned")
        mine = 2 * n + 9 + 2 * n

        def vector(dve, call, largest, values, scratch):
            at = call * mine
            for k in range(n):
                gates = pen if largest else same
                dve.tensor_tensor_scan(scratch[k], gates[:, 0:GE], values[k], -BIG if largest else 0.0,
                                       ALU.add if largest else ALU.mult, ALU.max if largest else ALU.add).then_inc(done, 1)
            for k in range(n):
                dve.wait_ge(done, at + k + 1)
                dve.tensor_tensor_scan(values[k][:, ::-1], pen[:, GE:0:-1], scratch[k][:, ::-1], -BIG, ALU.add, ALU.max).then_inc(done, 1)
            at += 2 * n
            dve.wait_ge(done, at)
            for k in range(n):
                dve.tensor_copy(ends[:, 0, k:k + 1], values[k][:, 0:1])
                last = dve.tensor_copy(ends[:, 1, k:k + 1], values[k][:, GE - 1:GE])
            last.then_inc(done, 1)
            dve.memset(rows[:, :, :], -NEG if largest else 0.0).then_inc(done, 1)
            dve.tensor_tensor(links[:, 0, :], cont[0:n, 0:Q], through[0:n, 0:Q], ALU.mult).then_inc(done, 1)
            dve.tensor_tensor(links[:, 1, :], cont[0:n, 1:Q + 1], through[0:n, 2:Q + 2], ALU.mult).then_inc(done, 1)
            dve.wait_ge(done, at + 4)
            dve.wait_ge(turned, 2 * call + 1)
            dve.tensor_copy(rows[:, :, 1:Q + 1], ps_rows[:, :, 0:Q]).then_inc(done, 1)
            dve.wait_ge(done, at + 5)
            for way, (which, other) in enumerate(((cont[0:n, 0:Q], rows[:, 1, 0:Q]), (cont[0:n, 1:Q + 1], rows[:, 0, 2:Q + 2]))):
                if largest:
                    dve.tensor_scalar(chain[:, way, :], which, 1.0, BIG, ALU.subtract, ALU.mult)
                    got = dve.tensor_scalar(gate[:, way, :], links[:, way, :], 1.0, BIG, ALU.subtract, ALU.mult)
                else:
                    dve.tensor_tensor(chain[:, way, :], which, other, ALU.mult)
                    got = dve.tensor_copy(gate[:, way, :], links[:, way, :])
            got.then_inc(done, 1)
            dve.wait_ge(done, at + 6)
            if largest:
                dve.tensor_tensor(chain[:, 0, :], chain[:, 0, :], rows[:, 1, 0:Q], ALU.add)
                dve.tensor_tensor(chain[:, 1, :], chain[:, 1, :], rows[:, 0, 2:Q + 2], ALU.add).then_inc(done, 1)
            else:
                dve.tensor_copy(rows[:, 0, 0:1], rows[:, 0, 0:1]).then_inc(done, 1)
            dve.wait_ge(done, at + 7)
            op0, op1, start = (ALU.add, ALU.max, -NEG) if largest else (ALU.mult, ALU.add, 0.0)
            dve.tensor_tensor_scan(links[:, 0, :], gate[:, 0, :], chain[:, 0, :], start, op0, op1)
            dve.tensor_tensor_scan(links[:, 1, ::-1], gate[:, 1, ::-1], chain[:, 1, ::-1], start, op0, op1).then_inc(done, 1)
            dve.wait_ge(turned, 2 * call + 2)
            dve.tensor_copy(back[:, :, :], ps_back[:, :, :]).then_inc(done, 1)
            at += 9
            dve.wait_ge(done, at)
            for way, where in enumerate((pen_first, pen_last) if largest else (in_first, in_last)):
                for k in range(n):
                    dve.wait_ge(done, at + way * n)
                    dve.scalar_tensor_tensor(out=values[k], in0=where[:, :], scalar=back[:, way, k:k + 1], in1=values[k],
                                             op0=op0, op1=op1).then_inc(done, 1)
            dve.wait_ge(done, at + 2 * n)

        def tensor(pe, call):
            pe.wait_ge(done, call * mine + 2 * n + 1)
            for way in range(2):
                mm = pe.transpose(ps_rows[:, way, 0:Q], ends[:, way, :], ident[0:Q, 0:Q])
            mm.then_inc(turned, 1)
            pe.wait_ge(done, call * mine + 2 * n + 8)
            for way in range(2):
                mm = pe.transpose(ps_back[:, way, :], links[:, way, :], ident[0:n, 0:n])
            mm.then_inc(turned, 1)

        return vector, tensor

    def rel_softmax(e_t, e_bias):
        with ExitStack() as ctx:
            tmp, psum, sem, pair = scope(ctx, "s0")
            e_s, top_s, ex, total = (tmp(n, [Q, GE]) for n in ("e_s", "top_s", "ex", "total"))
            mask, val, scratch = tmp("mask", [Q, R, GE]), tmp("val", [Q, R, GE]), tmp("scratch", [Q, R, GE])
            ps_e = psum("ps_e", [Q, J, P])
            ps_a = psum("ps_a", [P, J, Q])
            turned, step, exped = sem("turned"), sem("step"), sem("exped")
            totals_v, totals_t = segment_totals(ctx, "s0t", R)
            vals, scr = [val[:, r, :] for r in range(R)], [scratch[:, r, :] for r in range(R)]
            n_select = 2 * R

            with nc.Block() as block:
                @block.tensor
                def _(pe):
                    for j in range(J):
                        mm = pe.transpose(ps_e[:, j, :], e_t[:, j::J], ident[:, :])
                    mm.then_inc(turned, 1)
                    totals_t(pe, 0)
                    totals_t(pe, 1)
                    pe.wait_ge(step, 4 + 3 * R + n_select + 2 + R + n_select + 3)
                    for j in range(J):
                        mm = pe.transpose(ps_a[:, j, :], total[:, j * P:(j + 1) * P], ident[0:Q, 0:Q])
                    mm.then_inc(turned, 1)

                @block.scalar
                def _(act):
                    act.wait_ge(step, 4 + 3 * R + n_select + 2)
                    act.activation(ex[:, :], e_s[:, :], ACT.Exp).then_inc(exped, 1)

                @block.vector
                def _(dve):
                    for r in range(R):
                        dve.tensor_scalar(mask[:, r, :], typ_s[:, :], float(r), None, ALU.is_equal).then_inc(step, 1)
                    dve.wait_ge(turned, 1)
                    dve.wait_ge(step, R)
                    dve.tensor_copy(e_s[:, :], ps_e[:, :, :].rearrange("q j e -> q (j e)")).then_inc(step, 1)
                    for r in range(R):
                        dve.wait_ge(step, R + 1 + r)
                        dve.scalar_tensor_tensor(out=e_s[:, :], in0=mask[:, r, :], scalar=e_bias[:, r:r + 1], in1=e_s[:, :],
                                                 op0=ALU.mult, op1=ALU.add).then_inc(step, 1)
                    dve.wait_ge(step, 2 * R + 1)
                    dve.scalar_tensor_tensor(out=top_s[:, :], in0=e_s[:, :], scalar=0.2, in1=e_s[:, :],
                                             op0=ALU.mult, op1=ALU.max).then_inc(step, 1)
                    dve.wait_ge(step, 2 * R + 2)
                    dve.tensor_copy(e_s[:, :], top_s[:, :]).then_inc(step, 1)
                    dve.wait_ge(step, 2 * R + 3)
                    for r in range(R):
                        dve.tensor_scalar(vals[r], mask[:, r, :], 1.0, NEG, ALU.subtract, ALU.mult)
                    dve.memset(total[:, :], 0.0).then_inc(step, 1)
                    dve.wait_ge(step, 2 * R + 4)
                    for r in range(R):
                        dve.tensor_tensor(vals[r], vals[r], e_s[:, :], ALU.add).then_inc(step, 1)
                    at = 3 * R + 4
                    dve.wait_ge(step, at)
                    totals_v(dve, 0, True, vals, scr)

                    def select(at):
                        for r in range(R):
                            dve.tensor_tensor(scr[r], mask[:, r, :], vals[r], ALU.mult).then_inc(step, 1)
                        for r in range(R):
                            dve.wait_ge(step, at + R + r)
                            dve.tensor_tensor(total[:, :], total[:, :], scr[r], ALU.add).then_inc(step, 1)
                        dve.wait_ge(step, at + 2 * R)

                    select(at)
                    at += n_select
                    dve.tensor_tensor(e_s[:, :], e_s[:, :], total[:, :], ALU.subtract).then_inc(step, 1)
                    dve.wait_ge(step, at + 1)
                    dve.memset(total[:, :], 0.0).then_inc(step, 1)
                    at += 2 + R
                    dve.wait_ge(exped, 1)
                    for r in range(R):
                        dve.tensor_tensor(vals[r], mask[:, r, :], ex[:, :], ALU.mult).then_inc(step, 1)
                    at += 0
                    dve.wait_ge(step, at)
                    totals_v(dve, 1, False, vals, scr)
                    select(at)
                    at += n_select
                    dve.tensor_scalar(total[:, :], total[:, :], 1e-16, None, ALU.max).then_inc(step, 1)
                    dve.wait_ge(step, at + 1)
                    dve.reciprocal(top_s[:, :], total[:, :]).then_inc(step, 1)
                    dve.wait_ge(step, at + 2)
                    dve.tensor_tensor(total[:, :], top_s[:, :], ex[:, :], ALU.mult).then_inc(step, 1)
                    dve.wait_ge(turned, 2)
                    dve.tensor_copy(attn_t[:, :].rearrange("p (q j) -> p j q", j=J), ps_a[:, :, :]).then_inc(step, 1)

    def rel_sums(agg, share):
        with ExitStack() as ctx:
            tmp, psum, sem, pair = scope(ctx, "g0")
            rel, onehot = tmp("rel", [P, 2, J, D]), tmp("onehot", [P, 2, J, KEYS])
            ps_g = [psum(f"ps_g{s}", [P, J, KEYS]) for s in range(2)]
            ps_w = [psum(f"ps_w{s}", [1, J, KEYS]) for s in range(2)]
            shares = tmp("shares", [1, 2, J, KEYS])
            rel_in, marked, used, moved = (pair(n) for n in ("rel_in", "marked", "used", "moved"))
            added, shared = sem("added"), sem("shared")

            def sync_program(sp, nw):
                with sp.Fori(0, Q // 2) as i:
                    for s in range(2):
                        sp.wait_ge(used[s], i * nw)
                        sp.dma_start(rel[:, s, :, :].rearrange("p j f -> p (j f)"),
                                     rel_edges[bass.ds(2 * i + s, 1), :, :].rearrange("a p f -> (a p) f")).then_inc(rel_in[s], 16)

            def pe_program(pe, nw):
                def body(i, first):
                    for s in range(2):
                        pe.wait_ge(rel_in[s], 16 * (i + 1))
                        for w in range(nw):
                            pe.wait_ge(marked[s], i * nw + w + 1)
                            if w > 0 or not first:
                                steps = (2 * i + s) * nw + w if w > 0 else (2 * i + s - 1) * nw
                                pe.wait_ge(added, J * steps)
                                pe.wait_ge(moved[s], i * nw + w)
                            for j in range(J):
                                pe.matmul(ps_g[s][:, j, :], rel[:, s, j, :], onehot[:, s, j, :], start=True, stop=True)
                            pe.matmul(ps_w[s][:, :, :], ones[:, 0:1], onehot[:, s, :, :], start=True, stop=True).then_inc(used[s], 1)
                pairs(pe, body)

            def dve_program(dve, nw):
                def mark(i, s, w):
                    dve.wait_ge(used[s], i * nw + w)
                    for j in range(J):
                        t = (2 * i + s) * J + j
                        mk = dve.tensor_scalar(onehot[:, s, j, :], iota[:, w * KEYS:(w + 1) * KEYS], key_t[:, bass.ds(t, 1)],
                                               attn_t[:, bass.ds(t, 1)], ALU.is_equal, ALU.mult)
                    mk.then_inc(marked[s], 1)

                def add(i, s, w):
                    dve.wait_ge(used[s], i * nw + w + 1)
                    dve.nop(nofuse=True)
                    for j in range(J):
                        base = window_base([dve.engine], 2 * i + s, j)
                        n = ((2 * i + s) * nw + w) * J + j
                        to = bass.ds(base * R + w * KEYS, KEYS)
                        dve.wait_ge(added, n)
                        dve.tensor_tensor(agg[:, to], agg[:, to], ps_g[s][:, j, :], ALU.add).then_inc(added, 1)

                def body(i, first):
                    for s in range(2):
                        mark(i, s, 0)
                        if not (first and s == 0):
                            add(i - 1 + s, 1 - s, nw - 1)
                        for w in range(1, nw):
                            add(i, s, w - 1)
                            mark(i, s, w)
                pairs(dve, body)
                add(Q // 2 - 1, 1, nw - 1)

            def pool_program(pool, nw):
                def add_shares(q, at):
                    s, c = at(2)
                    for w in range(nw):
                        pool.wait_ge(moved[s], c * nw + w + 1)
                        pool.nop(nofuse=True)
                        for j in range(J):
                            base = window_base([pool.engine], q, j)
                            n = (q * nw + w) * J + j
                            to = bass.ds(base * R + w * KEYS, KEYS)
                            hold(pool, shared, n)
                            pool.tensor_tensor(share[0:1, to], share[0:1, to], shares[:, s, j, :], ALU.add).then_inc(shared, 1)
                pipeline(pool, (add_shares, 0))

            def act_program(act, nw):
                def move(q, at):
                    s, c = at(2)
                    for w in range(nw):
                        act.wait_ge(used[s], c * nw + w + 1)
                        if w > 0:
                            act.wait_ge(shared, J * (q * nw + w))
                        elif not isinstance(q, int) or q >= 2:
                            act.wait_ge(shared, J * (q - 1) * nw)
                        act.copy(shares[:, s, :, :], ps_w[s][:, :, :]).then_inc(moved[s], 1)
                pipeline(act, (move, 0))

            with nc.Block() as block:
                @block.gpsimd
                def _(pool):
                    both_ways(pool, lambda nw: pool_program(pool, nw))

                @block.scalar
                def _(act):
                    both_ways(act, lambda nw: act_program(act, nw))

                @block.sync
                def _(sp):
                    both_ways(sp, lambda nw: sync_program(sp, nw))

                @block.tensor
                def _(pe):
                    both_ways(pe, lambda nw: pe_program(pe, nw))

                @block.vector
                def _(dve):
                    both_ways(dve, lambda nw: dve_program(dve, nw))

    def norm_stats(dve, rows, stats, mean_var, var_eps, done, at):
        for k in range(K4):
            st = dve.bn_stats(stats[:, k, :], rows[:, k, :])
        st.then_inc(done, 1)
        dve.wait_ge(done, at + 1)
        dve.nop(nofuse=True)
        for k in range(K4):
            st = dve.bn_aggr(mean_var[:, k, :], stats[:, k, :])
        st.then_inc(done, 1)
        dve.wait_ge(done, at + 2)
        dve.tensor_scalar(var_eps[:, :], mean_var[:, :, 1], EPS, None, ALU.add).then_inc(done, 1)

    def norm_apply(dve, out_rows, rows, mean_var, root, inverse, done, at):
        dve.reciprocal(inverse[:, :], root[:, :]).then_inc(done, 1)
        dve.wait_ge(done, at + 1)
        for k in range(K4):
            st = dve.tensor_scalar(out_rows[:, k, :], rows[:, k, :], mean_var[:, k, 0:1], inverse[:, k:k + 1], ALU.subtract, ALU.mult)
        st.then_inc(done, 1)

    def rel_nodes(agg, share):
        with ExitStack() as ctx:
            tmp, psum, sem, pair = scope(ctx, "n0")
            wv, bv = tmp("wv", [P, R, D]), tmp("bv", [1, R, D])
            w_src, w_dst, b1 = tmp("w_src", [P, D]), tmp("w_dst", [P, D]), tmp("b1", [P, D])
            part, part_w = tmp("part", [P, GE * R]), tmp("part_w", [1, GE * R])
            xg, low, ex, h, y, x1, xt = (tmp(n, [P, K4, D]) for n in ("xg", "low", "ex", "h", "y", "x1", "xt"))
            src_rows, dst_rows = tmp("src_rows", [P, K4, D]), tmp("dst_rows", [P, K4, D])
            stats, mean_var = tmp("stats", [P, K4, 6]), tmp("mean_var", [P, K4, 2])
            var_eps, root, inverse = (tmp(n, [P, K4]) for n in ("var_eps", "root", "inverse"))
            ps_h, ps_x, ps_s, ps_d = (psum(n, [P, K4, D]) for n in ("ps_h", "ps_x", "ps_s", "ps_d"))
            weights_in, x_in, parts, h_mm, exped, rooted, vec, turned, xt_ready, tab_mm, src_out, dst_out, x_st, stored = (sem(n) for n in
                ("weights_in", "x_in", "parts", "h_mm", "exped", "rooted", "vec", "turned", "xt_ready", "tab_mm", "src_out", "dst_out", "x_st", "stored"))
            V = 8

            with nc.Block() as block:
                @block.sync
                def _(sp):
                    sp.dma_start(wv[:, :, :], L0_gnn_W_V.rearrange("r f g -> f r g")).then_inc(weights_in, 16)
                    sp.dma_start(bv[:, :, :].rearrange("a r f -> a (r f)"), across(L0_gnn_b_V.rearrange("r f -> (r f)"), R * D, 1)).then_inc(weights_in, 16)
                    sp.dma_start(w_src[:, :], L1_gnn_W1[0:D, :]).then_inc(weights_in, 16)
                    sp.dma_start(w_dst[:, :], L1_gnn_W1[D:2 * D, :]).then_inc(weights_in, 16)
                    sp.dma_start(b1[:, :], across(L1_gnn_b1, D)).then_inc(weights_in, 16)

                    def store_rows(g):
                        sp.wait_ge(src_out, g + 1)
                        sp.dma_start(rows_of(msg_table, g, D), src_rows[:, :, :]).then_inc(stored, 16)
                        sp.wait_ge(dst_out, g + 1)
                        sp.dma_start(rows_of(msg_window, g, D), dst_rows[:, :, :]).then_inc(stored, 16)

                    def group(g, last):
                        if not last:
                            sp.wait_ge(vec, V * g + 3)
                            sp.dma_start(xg[:, :, :], rows_of(xs[0], g + 1, D)).then_inc(x_in, 16)
                        sp.wait_ge(vec, V * g + 8)
                        sp.dma_start(rows_of(xs[1], g, D), x1[:, :, :]).then_inc(x_st, 16)
                        if not isinstance(g, int) or g > 0:
                            store_rows(g - 1)
                    sp.dma_start(xg[:, :, :], rows_of(xs[0], 0, D)).then_inc(x_in, 16)
                    over_groups(sp, group)
                    store_rows(NGRP - 1)
                    sp.wait_ge(x_st, 16 * NGRP)
                    sp.wait_ge(stored, 32 * NGRP)

                @block.tensor
                def _(pe):
                    pe.wait_ge(weights_in, 16 * 5)

                    def sums(g):
                        pe.wait_ge(parts, 2 * (g + 1))
                        by_node = part[:, :].rearrange("f (n k r) -> f n k r", k=K4, r=R)
                        by_node_w = part_w[:, :].rearrange("f (n k r) -> f n k r", k=K4, r=R)
                        for k in range(K4):
                            for r in range(R):
                                pe.matmul(ps_h[:, k, :], by_node[:, :, k, r], wv[:, r, :], start=(r == 0), stop=False, skip_group_check=True)
                                mm = pe.matmul(ps_h[:, k, :], by_node_w[:, :, k, r], bv[:, r, :], start=False, stop=(r == R - 1), skip_group_check=True)
                        mm.then_inc(h_mm, 1)

                    def group(g, last):
                        if not last:
                            pe.wait_ge(vec, V * g + 2)
                            sums(g + 1)
                        pe.wait_ge(vec, V * g + 8)
                        for k in range(K4):
                            mm = pe.transpose(ps_x[:, k, :], x1[:, k, :], ident[:, :])
                        mm.then_inc(turned, 1)
                        pe.wait_ge(xt_ready, g + 1)
                        hold(pe, src_out, g)
                        hold(pe, dst_out, g)
                        for k in range(K4):
                            pe.matmul(ps_s[:, k, :], xt[:, k, :], w_src[:, :], start=True, stop=True)
                            mm = pe.matmul(ps_d[:, k, :], xt[:, k, :], w_dst[:, :], start=True, stop=True)
                        mm.then_inc(tab_mm, 1)
                    sums(0)
                    over_groups(pe, group)

                @block.scalar
                def _(act):
                    def cut(g):
                        hold(act, h_mm, g)
                        act.copy(part[:, :], agg[:, bass.ds(g * (GE * R), GE * R)]).then_inc(parts, 1)
                        act.copy(part_w[:, :], share[0:1, bass.ds(g * (GE * R), GE * R)]).then_inc(parts, 1)

                    def source_rows(g):
                        act.wait_ge(tab_mm, g + 1)
                        hold(act, stored, 32 * g)
                        act.copy(src_rows[:, :, :], ps_s[:, :, :]).then_inc(src_out, 1)

                    def group(g, last):
                        act.wait_ge(vec, V * g + 1)
                        act.activation(ex[:, :, :], low[:, :, :], ACT.Exp).then_inc(exped, 1)
                        if not isinstance(g, int) or g > 0:
                            source_rows(g - 1)
                        if not last:
                            cut(g + 1)
                        act.wait_ge(vec, V * g + 6)
                        act.activation(root[:, :], var_eps[:, :], ACT.Sqrt).then_inc(rooted, 1)
                        act.wait_ge(turned, g + 1)
                        act.copy(xt[:, :, :], ps_x[:, :, :]).then_inc(xt_ready, 1)
                    cut(0)
                    over_groups(act, group)
                    source_rows(NGRP - 1)

                @block.vector
                def _(dve):
                    dve.wait_ge(weights_in, 16 * 5)

                    def dst_side(g):
                        dve.wait_ge(tab_mm, g + 1)
                        hold(dve, stored, 32 * g)
                        dve.tensor_tensor(dst_rows[:, :, :], ps_d[:, :, :], b1[:, :].unsqueeze(1).to_broadcast([P, K4, D]), ALU.add).then_inc(dst_out, 1)

                    def group(g, last):
                        dve.wait_ge(h_mm, g + 1)
                        dve.tensor_scalar(low[:, :, :], ps_h[:, :, :], 0.0, None, ALU.min).then_inc(vec, 1)
                        dve.wait_ge(exped, g + 1)
                        dve.scalar_tensor_tensor(out=h[:, :, :], in0=ps_h[:, :, :], scalar=0.0, in1=ex[:, :, :],
                                                 op0=ALU.max, op1=ALU.add).then_inc(vec, 1)
                        dve.wait_ge(vec, V * g + 2)
                        dve.wait_ge(x_in, 16 * (g + 1))
                        dve.scalar_tensor_tensor(out=y[:, :, :], in0=h[:, :, :], scalar=-1.0, in1=xg[:, :, :],
                                                 op0=ALU.add, op1=ALU.add).then_inc(vec, 1)
                        dve.wait_ge(vec, V * g + 3)
                        norm_stats(dve, y, stats, mean_var, var_eps, vec, V * g + 3)
                        if not isinstance(g, int) or g > 0:
                            dst_side(g - 1)
                        dve.wait_ge(rooted, g + 1)
                        hold(dve, x_st, 16 * g)
                        hold(dve, turned, g)
                        norm_apply(dve, x1, y, mean_var, root, inverse, vec, V * g + 6)
                    over_groups(dve, group)
                    dst_side(NGRP - 1)

    def mark_nodes(dve, onehot, s, q, nw):
        for w in range(nw):
            mk = dve.tensor_tensor(onehot[:, s, w, :, :], iota[:, w * WIN:(w + 1) * WIN].unsqueeze(1).to_broadcast([P, J, WIN]),
                                   dl_t[:, bass.ds(q * J, J)].unsqueeze(2).to_broadcast([P, J, WIN]), ALU.is_equal)
        return mk

    def spread_nodes(act, spread, ps_t, s, nw):
        for w in range(nw):
            for j in range(J):
                cp = act.copy(spread[j * WIN:(j + 1) * WIN, s, w, j, :], ps_t[j * WIN:(j + 1) * WIN, w, :])
        return cp

    def load_windows(sp, window, s, table, q, nw, loaded):
        for j in range(J):
            base = window_base([sp.engine], q, j)
            for w in range(nw):
                sp.dma_start(window[j * WIN:(j + 1) * WIN, s, w, :], table[bass.ds(base + w * WIN, WIN), :]).then_inc(loaded, 16)

    def add_windows(dve, sums, ps_a, s, q, nw, added):
        n = q * (J * nw)
        for j in range(J):
            base = window_base([dve.engine], q, j)
            for w in range(nw):
                to = bass.ds(base + w * WIN, WIN)
                dve.wait_ge(added, n + j * nw + w)
                dve.tensor_tensor(sums[:, to], sums[:, to], ps_a[s][:, w, j, :], ALU.add).then_inc(added, 1)

    def messages(agg1):
        with ExitStack() as ctx:
            tmp, psum, sem, pair = scope(ctx, "e1")
            S = 4
            NWM = P // WIN
            idx = tmp("idx", [P, S, J], I32)
            w_edge, w2 = tmp("w_edge", [P, 2, D]), tmp("w2", [P, D])
            b2 = tmp("b2", [P, J, D])
            gathered = tmp("gathered", [P, S, J, D])
            hidden, shifted, message = (tmp(n, [P, 2, J, D]) for n in ("hidden", "shifted", "message"))
            attr, attr_t = tmp("attr", [P, S, J, REL]), tmp("attr_t", [P, 2, 2, P])
            onehot, window = tmp("onehot", [P, S, NWM, J, WIN]), tmp("window", [P, S, NWM, D])
            spread = tmp("spread", [P, 2, NWM, J, P])
            ps_t, ps_e = psum("ps_t", [P, NWM, P]), psum("ps_e", [P, 2, P])
            ps_h, ps_m = ([psum(f"{n}{s}", [P, J, D]) for s in range(2)] for n in ("ps_h", "ps_m"))
            ps_a = [psum(f"ps_a{s}", [P, NWM, J, WIN]) for s in range(2)]
            cleared, weights_in, turned, copied, added, tail_in = (sem(n) for n in
                ("cleared", "weights_in", "turned", "copied", "added", "tail_in"))
            staged, src_in, win_in, attr_in, marked, h_mm = (pair(n, S) for n in ("staged", "src_in", "win_in", "attr_in", "marked", "h_mm"))
            h_out, m_mm, biased, m_out, a_mm = (pair(n) for n in ("h_out", "m_mm", "biased", "m_out", "a_mm"))
            full = (E - (Q - 1) * GE) // P
            rest = E - (Q - 1) * GE - full * P
            LOADS = Q // S

            def sync_program(sp, nw):
                sp.wait_ge(cleared, 1)
                for n in range(2):
                    sp.dma_start(w_edge[n * REL:(n + 1) * REL, n, :], L1_gnn_W1[2 * D:, :]).then_inc(weights_in, 16)
                sp.dma_start(w2[:, :], L1_gnn_W2).then_inc(weights_in, 16)
                for j in range(J):
                    sp.dma_start(b2[:, j, :], across(L1_gnn_b2, D)).then_inc(weights_in, 16)

                def load(q, s, c, last=False):
                    hold(sp, h_mm[s], c)
                    sp.nop(nofuse=True)
                    if last:
                        rows = edge_attr_64[(Q - 1) * GE:(Q - 1) * GE + full * P, :]
                        sp.dma_start(attr[0:rest, s, full, :], edge_attr_64[E - rest:E, :]).then_inc(tail_in, 16)
                        sp.wait_ge(tail_in, 16)
                        sp.dma_start(attr[:, s, 0:full, :], rows.rearrange("(j p) f -> p j f", p=P)).then_inc(attr_in[s], 16)
                    else:
                        rows = edge_attr_64[bass.ds(q * GE, GE), :]
                        sp.dma_start(attr[:, s, :, :], rows.rearrange("(j p) f -> p j f", p=P)).then_inc(attr_in[s], 16)
                    load_windows(sp, window, s, msg_window, q, nw, win_in[s])

                for u in range(U):
                    load(u, u, 0)
                with sp.Fori(1, LOADS - 1) as i:
                    for u in range(U):
                        load(U * i + u, u, i)
                for u in range(U):
                    load(Q - U + u, u, LOADS - 1, last=(u == U - 1))

            def pe_program(pe, nw):
                pe.wait_ge(weights_in, 16 * (3 + J))

                def turn(q, at):
                    s, c = at(S)
                    hold(pe, copied, 2 * q)
                    pe.wait_ge(attr_in[s], 16 * (c + 1))
                    pe.wait_ge(marked[s], c + 1)
                    for w in range(nw):
                        mm = pe.transpose(ps_t[:, w, :], onehot[:, s, w, :, :].rearrange("p j n -> p (j n)"), ident[:, :])
                    mm.then_inc(turned, 1)
                    for n in range(2):
                        mm = pe.transpose(ps_e[:, n, :], attr[:, s, 2 * n:2 * n + 2, :].rearrange("p j f -> p (j f)"), ident[:, :])
                    mm.then_inc(turned, 1)

                def hide(q, at):
                    s, c = at(S)
                    s2, c2 = at(2)
                    pe.wait_ge(win_in[s], 16 * J * nw * (c + 1))
                    pe.wait_ge(copied, 2 * (q + 1))
                    hold(pe, h_out[s2], c2)
                    pe.wait_ge(src_in[s], 16 * J * (c + 1))
                    for w in range(nw):
                        pe.matmul(ps_h[s2][:, :, :], window[:, s, w, :], spread[:, s2, w, :, :], start=(w == 0), stop=False, skip_group_check=True)
                    for j in range(J):
                        pe.matmul(ps_h[s2][:, j, :], w_edge[:, j % 2, :], attr_t[:, s2, j // 2, :], start=False, stop=False, skip_group_check=True)
                        mm = pe.matmul(ps_h[s2][:, j, :], gathered[:, s, j, :], ident[:, :], start=False, stop=True, skip_group_check=True)
                    mm.then_inc(h_mm[s], 1)

                def send(q, at):
                    s, c = at(2)
                    pe.wait_ge(h_out[s], c + 1)
                    hold(pe, biased[s], c)
                    for j in range(J):
                        mm = pe.matmul(ps_m[s][:, j, :], hidden[:, s, j, :], w2[:, :], start=True, stop=True)
                    mm.then_inc(m_mm[s], 1)

                def collect(q, at):
                    s, c = at(2)
                    s4, c4 = at(S)
                    pe.wait_ge(m_out[s], c + 1)
                    hold(pe, added, J * nw * (q - 1) if not isinstance(q, int) or q >= 2 else 0)
                    for w in range(nw):
                        for j in range(J):
                            mm = pe.matmul(ps_a[s][:, w, j, :], message[:, s, j, :], onehot[:, s4, w, j, :], start=True, stop=True)
                    mm.then_inc(a_mm[s], 1)
                pipeline(pe, (hide, 1), (turn, 0), (send, 2), (collect, 3))

            def act_program(act, nw):
                act.wait_ge(cleared, 2)

                def copy(q, at):
                    s, c = at(2)
                    if not isinstance(q, int) or q >= 2:
                        s4, c4 = at(S)
                        act.wait_ge(h_mm[(s4 + 2) % S], c4 + (1 if s4 >= 2 else 0))
                    act.wait_ge(turned, 2 * q + 1)
                    spread_nodes(act, spread, ps_t, s, nw).then_inc(copied, 1)
                    act.wait_ge(turned, 2 * q + 2)
                    act.copy(attr_t[:, s, :, :], ps_e[:, :, :]).then_inc(copied, 1)

                def hide(q, at):
                    s, c = at(2)
                    s4, c4 = at(S)
                    act.wait_ge(h_mm[s4], c4 + 1)
                    hold(act, m_mm[s], c)
                    act.activation(hidden[:, s, :, :], ps_h[s][:, :, :], ACT.Relu).then_inc(h_out[s], 1)

                def send(q, at):
                    s, c = at(2)
                    act.wait_ge(biased[s], c + 1)
                    hold(act, a_mm[s], c)
                    act.activation(message[:, s, :, :], shifted[:, s, :, :], ACT.Relu).then_inc(m_out[s], 1)
                pipeline(act, (hide, 1), (copy, 0), (send, 2))

            def dve_program(dve, nw):
                dve.memset(w_edge[:, :, :], 0.0).then_inc(cleared, 1)
                dve.memset(spread[:, :, :, :, :], 0.0).then_inc(cleared, 1)
                dve.memset(agg1[:, :], 0.0).then_inc(cleared, 1)
                dve.wait_ge(cleared, 3)
                dve.wait_ge(weights_in, 16 * (3 + J))

                def mark(q, at):
                    s, c = at(S)
                    s2, c2 = at(2)
                    hold(dve, a_mm[s2], c2 - 1 if not isinstance(c2, int) or c2 > 1 else 0)
                    mark_nodes(dve, onehot, s, q, nw).then_inc(marked[s], 1)

                def bias(q, at):
                    s, c = at(2)
                    dve.wait_ge(m_mm[s], c + 1)
                    hold(dve, m_out[s], c)
                    dve.tensor_tensor(shifted[:, s, :, :], ps_m[s][:, :, :], b2[:, :, :], ALU.add).then_inc(biased[s], 1)

                def add(q, at):
                    s, c = at(2)
                    dve.wait_ge(a_mm[s], c + 1)
                    dve.nop(nofuse=True)
                    add_windows(dve, agg1, ps_a, s, q, nw, added)
                pipeline(dve, (mark, 0), (add, 4), (bias, 2))

            with nc.Block() as block:
                @block.gpsimd
                def _(pool):
                    gathers(pool, S, idx, src_idx, staged, gathered, msg_table, src_in, [(h_mm, 1)])

                @block.sync
                def _(sp):
                    both_ways(sp, lambda nw: sync_program(sp, nw))

                @block.tensor
                def _(pe):
                    both_ways(pe, lambda nw: pe_program(pe, nw))

                @block.scalar
                def _(act):
                    both_ways(act, lambda nw: act_program(act, nw))

                @block.vector
                def _(dve):
                    both_ways(dve, lambda nw: dve_program(dve, nw))

    def message_nodes(agg1):
        with ExitStack() as ctx:
            tmp, psum, sem, pair = scope(ctx, "n1")
            C = 3 * D
            wn, bn, gamma, beta = tmp("wn", [P, D]), tmp("bn", [P, D]), tmp("gamma", [P, D]), tmp("beta", [P, D])
            wk, wv, wkt = tmp("wk", [P, NT, D]), tmp("wv", [P, NT, D]), tmp("wkt", [P, 2, NT, D])
            w_all = tmp("w_all", [P, NT, C])
            att, msg, pri = tmp("att", [P, H, DH]), tmp("msg", [P, H, DH]), tmp("pri", [P, H])
            types, mask = tmp("types", [P, NGRP, K4], I32), tmp("mask", [P, NT, NGRP * K4])
            part = tmp("part", [P, GE])
            xg, r1, y, z, v, x2 = (tmp(n, [P, K4, D]) for n in ("xg", "r1", "y", "z", "v", "x2"))
            masked, xt = tmp("masked", [P, NT, K4, D]), tmp("xt", [P, NT, K4, D])
            rows = tmp("rows", [P, K4, C])
            stats, mean_var = tmp("stats", [P, K4, 6]), tmp("mean_var", [P, K4, 2])
            var_eps, root, inverse = (tmp(n, [P, K4]) for n in ("var_eps", "root", "inverse"))
            ps_h = psum("ps_h", [P, K4, D])
            ps_x = [psum(f"ps_x{n}", [P, K4, D]) for n in range(NT)]
            ps_r = [psum(f"ps_r{k}", [P, 512]) for k in range(K4)]
            weights_in, x_in, parts, h_mm, rooted, vec, turned, xt_ready, tab_mm, rows_out, x_st, stored, ready, w_mm, w_out = (sem(n) for n in
                ("weights_in", "x_in", "parts", "h_mm", "rooted", "vec", "turned", "xt_ready", "tab_mm", "rows_out", "x_st", "stored", "ready", "w_mm", "w_out"))
            V = 17

            with nc.Block() as block:
                @block.gpsimd
                def _(pool):
                    pool.memset(att[:, :, :], 0.0).then_inc(ready, 1)
                    pool.memset(msg[:, :, :], 0.0).then_inc(ready, 1)

                @block.sync
                def _(sp):
                    sp.dma_start(wn[:, :], L1_gnn_Wn).then_inc(weights_in, 16)
                    for to, frm in ((bn, L1_gnn_bn), (gamma, L1_gnn_gamma), (beta, L1_gnn_beta)):
                        sp.dma_start(to[:, :], across(frm, D)).then_inc(weights_in, 16)
                    sp.dma_start(wk[:, :, :], L2_gnn_Wk.rearrange("t f c -> f t c")).then_inc(weights_in, 16)
                    sp.dma_start(wv[:, :, :], L2_gnn_Wv.rearrange("t f c -> f t c")).then_inc(weights_in, 16)
                    sp.dma_start(w_all[:, :, 2 * D:3 * D], L2_gnn_Wq.rearrange("t f c -> f t c")).then_inc(weights_in, 16)
                    sp.dma_start(pri[:, :], across(L2_gnn_rel_pri, H)).then_inc(weights_in, 16)
                    sp.dma_start(types[:, :, :], type_pad.rearrange("(g p k) -> p g k", p=P, k=K4)).then_inc(weights_in, 16)
                    sp.wait_ge(ready, 2)
                    for h in range(H):
                        sp.dma_start(att[h * DH:(h + 1) * DH, h, :], L2_gnn_rel_att[h, :, :]).then_inc(weights_in, 16)
                        sp.dma_start(msg[h * DH:(h + 1) * DH, h, :], L2_gnn_rel_msg[h, :, :]).then_inc(weights_in, 16)

                    def store_rows(g):
                        sp.wait_ge(rows_out, K4 * (g + 1))
                        sp.dma_start(rows_of(kv_table, g, 2 * D), rows[:, :, 0:2 * D]).then_inc(stored, 16)
                        sp.dma_start(rows_of(q_window, g, D), rows[:, :, 2 * D:3 * D]).then_inc(stored, 16)

                    def group(g, last):
                        if not last:
                            sp.wait_ge(vec, 7 + V * g + 11)
                            sp.dma_start(xg[:, :, :], rows_of(xs[1], g + 1, D)).then_inc(x_in, 16)
                        sp.wait_ge(vec, 7 + V * g + 16)
                        sp.dma_start(rows_of(xs[2], g, D), x2[:, :, :]).then_inc(x_st, 16)
                        if not isinstance(g, int) or g > 0:
                            store_rows(g - 1)
                    sp.dma_start(xg[:, :, :], rows_of(xs[1], 0, D)).then_inc(x_in, 16)
                    over_groups(sp, group)
                    store_rows(NGRP - 1)
                    sp.wait_ge(x_st, 16 * NGRP)
                    sp.wait_ge(stored, 32 * NGRP)

                @block.tensor
                def _(pe):
                    pe.wait_ge(weights_in, 16 * (9 + 2 * H))
                    for n, w in enumerate((wk, wv)):
                        for t in range(NT):
                            mm = pe.transpose(ps_x[n][:, t, :], w[:, t, :], ident[:, :])
                        mm.then_inc(w_mm, 1)
                    pe.wait_ge(w_out, 2)
                    pe.wait_ge(vec, 1)
                    for t in range(NT):
                        pe.matmul(ps_r[t][:, 0:D], wkt[:, 0, t, :], att[:, :, :].rearrange("c h o -> c (h o)"), start=True, stop=True)
                        mm = pe.matmul(ps_r[t][:, D:2 * D], wkt[:, 1, t, :], msg[:, :, :].rearrange("c h o -> c (h o)"), start=True, stop=True)
                    mm.then_inc(w_mm, 1)
                    pe.wait_ge(w_out, 3)

                    def hidden(g):
                        pe.wait_ge(parts, g + 1)
                        for k in range(K4):
                            mm = pe.matmul(ps_h[:, k, :], part[:, k::K4], wn[:, :], start=True, stop=True)
                        mm.then_inc(h_mm, 1)

                    def group(g, last):
                        if not last:
                            pe.wait_ge(vec, 7 + V * g + 1)
                            hidden(g + 1)
                        pe.wait_ge(vec, 7 + V * g + 17)
                        for t in range(NT):
                            for k in range(K4):
                                mm = pe.transpose(ps_x[t][:, k, :], masked[:, t, k, :], ident[:, :])
                            mm.then_inc(turned, 1)
                        pe.wait_ge(xt_ready, NT * (g + 1))
                        hold(pe, rows_out, K4 * g)
                        for k in range(K4):
                            for t in range(NT):
                                mm = pe.matmul(ps_r[k][:, 0:C], xt[:, t, k, :], w_all[:, t, :], start=(t == 0), stop=(t == NT - 1))
                            mm.then_inc(tab_mm, 1)
                    hidden(0)
                    over_groups(pe, group)

                @block.scalar
                def _(act):
                    for n in range(2):
                        act.wait_ge(w_mm, n + 1)
                        act.copy(wkt[:, n, :, :], ps_x[n][:, 0:NT, :]).then_inc(w_out, 1)
                    act.wait_ge(w_mm, 3)
                    act.wait_ge(weights_in, 16 * (9 + 2 * H))
                    for t in range(NT):
                        cp = act.copy(w_all[:, t, 0:2 * D], ps_r[t][:, 0:2 * D])
                    cp.then_inc(w_out, 1)

                    def cut(g):
                        hold(act, h_mm, g)
                        act.copy(part[:, :], agg1[:, bass.ds(g * GE, GE)]).then_inc(parts, 1)

                    def table_rows(g):
                        hold(act, stored, 32 * g)
                        for k in range(K4):
                            act.wait_ge(tab_mm, K4 * g + k + 1)
                            act.copy(rows[:, k, :], ps_r[k][:, 0:C]).then_inc(rows_out, 1)

                    def group(g, last):
                        if not last:
                            cut(g + 1)
                        act.wait_ge(vec, 7 + V * g + 6)
                        act.activation(root[:, :], var_eps[:, :], ACT.Sqrt).then_inc(rooted, 1)
                        if not isinstance(g, int) or g > 0:
                            table_rows(g - 1)
                        act.wait_ge(vec, 7 + V * g + 14)
                        act.activation(root[:, :], var_eps[:, :], ACT.Sqrt).then_inc(rooted, 1)
                        for t in range(NT):
                            act.wait_ge(turned, NT * g + t + 1)
                            act.copy(xt[:, t, :, :], ps_x[t][:, :, :]).then_inc(xt_ready, 1)
                    cut(0)
                    over_groups(act, group)
                    table_rows(NGRP - 1)

                @block.vector
                def _(dve):
                    dve.wait_ge(weights_in, 16 * (9 + 2 * H))
                    dve.tensor_scalar(pri[:, :], pri[:, :], DH ** -0.5, None, ALU.mult).then_inc(ready, 1)
                    dve.wait_ge(ready, 3)
                    dve.tensor_tensor(att[:, :, :], att[:, :, :], pri[:, :].unsqueeze(2).to_broadcast([P, H, DH]), ALU.mult).then_inc(vec, 1)
                    for t in range(NT):
                        dve.tensor_scalar(mask[:, t, :], types[:, :, :].rearrange("p g k -> p (g k)"), float(t), None, ALU.is_equal).then_inc(vec, 2)
                    dve.wait_ge(vec, 7)
                    wide_b = lambda a: a[:, :].unsqueeze(1).to_broadcast([P, K4, D])

                    def group(g, last):
                        at = 7 + V * g
                        dve.wait_ge(h_mm, g + 1)
                        dve.tensor_tensor(r1[:, :, :], ps_h[:, :, :], wide_b(bn), ALU.add).then_inc(vec, 1)
                        dve.wait_ge(vec, at + 1)
                        dve.wait_ge(x_in, 16 * (g + 1))
                        dve.scalar_tensor_tensor(out=y[:, :, :], in0=r1[:, :, :], scalar=0.0, in1=xg[:, :, :],
                                                 op0=ALU.max, op1=ALU.add).then_inc(vec, 2)
                        dve.wait_ge(vec, at + 3)
                        norm_stats(dve, y, stats, mean_var, var_eps, vec, at + 3)
                        dve.wait_ge(rooted, 2 * g + 1)
                        norm_apply(dve, z, y, mean_var, root, inverse, vec, at + 6)
                        dve.wait_ge(vec, at + 8)
                        dve.tensor_tensor(v[:, :, :], z[:, :, :], wide_b(gamma), ALU.mult).then_inc(vec, 1)
                        dve.wait_ge(vec, at + 9)
                        dve.tensor_tensor(z[:, :, :], v[:, :, :], wide_b(beta), ALU.add).then_inc(vec, 1)
                        dve.wait_ge(vec, at + 10)
                        dve.tensor_tensor(y[:, :, :], z[:, :, :], xg[:, :, :], ALU.add).then_inc(vec, 1)
                        dve.wait_ge(vec, at + 11)
                        norm_stats(dve, y, stats, mean_var, var_eps, vec, at + 11)
                        dve.wait_ge(rooted, 2 * g + 2)
                        hold(dve, x_st, 16 * g)
                        norm_apply(dve, x2, y, mean_var, root, inverse, vec, at + 14)
                        dve.wait_ge(vec, at + 16)
                        hold(dve, turned, NT * g)
                        for t in range(NT):
                            for k in range(K4):
                                mk = dve.tensor_scalar(masked[:, t, k, :], x2[:, k, :], mask[:, t, bass.ds(g * K4 + k, 1)], None, ALU.mult)
                        mk.then_inc(vec, 1)
                    over_groups(dve, group)

    def head_scores(a_t):
        with ExitStack() as ctx:
            tmp, psum, sem, pair = scope(ctx, "e2")
            NWM = P // WIN
            idx = tmp("idx", [P, 2, J], I32)
            gathered = tmp("gathered", [P, 2, J, 2 * D])
            product = tmp("product", [P, J, D])
            onehot = tmp("onehot", [P, 2, NWM, J, WIN])
            spread, window = tmp("spread", [P, 2, NWM, J, P]), tmp("window", [P, 2, NWM, D])
            ps_t = [psum(f"ps_t{s}", [P, NWM, P]) for s in range(2)]
            ps_q = [psum(f"ps_q{s}", [P, J, D]) for s in range(2)]
            cleared = sem("cleared")
            staged, src_in, win_in, marked, turned, copied, q_mm, multiplied, reduced, v_st = (pair(n) for n in
                ("staged", "src_in", "win_in", "marked", "turned", "copied", "q_mm", "multiplied", "reduced", "v_st"))

            def sync_program(sp, nw):
                def store(q, i, s):
                    sp.wait_ge(src_in[s], 16 * J * (i + 1))
                    sp.dma_start(v_edges[bass.ds(q, 1), :, :].rearrange("a p (j f) -> (a p) j f", f=D), gathered[:, s, :, D:2 * D]).then_inc(v_st[s], 16)

                def body(i, first):
                    for s in range(2):
                        sp.wait_ge(q_mm[s], i)
                        sp.nop(nofuse=True)
                        load_windows(sp, window, s, q_window, 2 * i + s, nw, win_in[s])
                        if not (first and s == 0):
                            store(2 * i + s - 1, i - 1 + s, 1 - s)
                pairs(sp, body)
                store(Q - 1, Q // 2 - 1, 1)
                for s in range(2):
                    sp.wait_ge(v_st[s], 16 * (Q // 2))

            def pe_program(pe, nw):
                def expand(i, s):
                    pe.wait_ge(win_in[s], 16 * J * nw * (i + 1))
                    pe.wait_ge(copied[s], i + 1)
                    pe.wait_ge(multiplied[s], i)
                    for j in range(J):
                        for w in range(nw):
                            mm = pe.matmul(ps_q[s][:, j, :], spread[:, s, w, j, :], window[:, s, w, :], start=(w == 0), stop=(w == nw - 1))
                    mm.then_inc(q_mm[s], 1)

                def body(i, first):
                    for s in range(2):
                        pe.wait_ge(marked[s], i + 1)
                        pe.wait_ge(copied[s], i)
                        for w in range(nw):
                            mm = pe.transpose(ps_t[s][:, w, :], onehot[:, s, w, :, :].rearrange("p j n -> p (j n)"), ident[:, :])
                        mm.then_inc(turned[s], 1)
                        if not (first and s == 0):
                            expand(i - 1 + s, 1 - s)
                pairs(pe, body)
                expand(Q // 2 - 1, 1)

            def act_program(act, nw):
                act.wait_ge(cleared, 1)
                with act.Fori(0, Q // 2) as i:
                    for s in range(2):
                        act.wait_ge(src_in[s], 16 * J * i)
                        act.copy(idx[:, s, :], src_idx[:, bass.ds((2 * i + s) * J, J)]).then_inc(staged[s], 1)
                        act.wait_ge(turned[s], i + 1)
                        act.wait_ge(q_mm[s], i)
                        spread_nodes(act, spread, ps_t[s], s, nw).then_inc(copied[s], 1)

            def dve_program(dve, nw):
                dve.memset(spread[:, :, :, :, :], 0.0).then_inc(cleared, 1)

                def score(i, s, first):
                    dve.wait_ge(q_mm[s], i + 1)
                    dve.wait_ge(src_in[s], 16 * J * (i + 1))
                    if s == 1 or not first:
                        dve.wait_ge(reduced[1 - s], i + s)
                    dve.tensor_tensor(product[:, :, :], gathered[:, s, :, 0:D], ps_q[s][:, :, :], ALU.mult).then_inc(multiplied[s], 1)
                    dve.wait_ge(multiplied[s], i + 1)
                    dve.tensor_reduce(a_t[:, bass.ds((2 * i + s) * J * H, J * H)], product[:, :, :].rearrange("p j (h o) -> p (j h) o", o=DH),
                                      AX.X, ALU.add).then_inc(reduced[s], 1)

                def body(i, first):
                    for s in range(2):
                        dve.wait_ge(turned[s], i)
                        mark_nodes(dve, onehot, s, 2 * i + s, nw).then_inc(marked[s], 1)
                        if not (first and s == 0):
                            score(i - 1 + s, 1 - s, first)
                pairs(dve, body)
                score(Q // 2 - 1, 1, False)

            with nc.Block() as block:
                @block.gpsimd
                def _(pool):
                    with pool.Fori(0, Q // 2) as i:
                        for s in range(2):
                            pool.wait_ge(staged[s], i + 1)
                            pool.wait_ge(multiplied[s], i)
                            pool.wait_ge(v_st[s], 16 * i)
                            pool.nop(nofuse=True)
                            for j in range(J):
                                pool.indirect_dma_start(gathered[:, s, j, :], None, kv_table,
                                                        bass.IndirectOffsetOnAxis(ap=idx[:, s, j:j + 1], axis=0)).then_inc(src_in[s], 16)

                @block.sync
                def _(sp):
                    both_ways(sp, lambda nw: sync_program(sp, nw))

                @block.tensor
                def _(pe):
                    both_ways(pe, lambda nw: pe_program(pe, nw))

                @block.scalar
                def _(act):
                    both_ways(act, lambda nw: act_program(act, nw))

                @block.vector
                def _(dve):
                    both_ways(dve, lambda nw: dve_program(dve, nw))

    def head_softmax(a_t):
        with ExitStack() as ctx:
            tmp, psum, sem, pair = scope(ctx, "s2")
            val, ex, scratch = (tmp(n, [Q, H, GE]) for n in ("val", "ex", "scratch"))
            ps_s = [psum(f"ps_s{n}", [Q, J, P]) for n in range(2)]
            ps_b = [psum(f"ps_b{n}", [P, J, Q]) for n in range(2)]
            turned, moved, step, exped, back, placed = (sem(n) for n in ("turned", "moved", "step", "exped", "back", "placed"))
            totals_v, totals_t = segment_totals(ctx, "s2t", H)
            heads = lambda a: [a[:, h, :] for h in range(H)]
            scores = a_t[:, :].rearrange("p (q j h) -> p q j h", j=J, h=H)

            with nc.Block() as block:
                @block.tensor
                def _(pe):
                    for h in range(H):
                        if h >= 2:
                            pe.wait_ge(moved, h - 1)
                        for j in range(J):
                            mm = pe.transpose(ps_s[h % 2][:, j, :], scores[:, :, j, h], ident[:, :])
                        mm.then_inc(turned, 1)
                    totals_t(pe, 0)
                    totals_t(pe, 1)
                    for h in range(H):
                        pe.wait_ge(step, 2 * H + h + 1)
                        if h >= 2:
                            pe.wait_ge(placed, 2 * H + h - 1)
                        for j in range(J):
                            mm = pe.transpose(ps_b[h % 2][:, j, :], val[:, h, j * P:(j + 1) * P], ident[0:Q, 0:Q])
                        mm.then_inc(back, 1)

                @block.scalar
                def _(act):
                    for h in range(H):
                        act.wait_ge(turned, h + 1)
                        act.copy(ex[:, h, :], ps_s[h % 2][:, :, :].rearrange("q j e -> q (j e)")).then_inc(moved, 1)
                    for h in range(H):
                        act.wait_ge(step, H + h + 1)
                        act.activation(ex[:, h, :], ex[:, h, :], ACT.Exp).then_inc(exped, 1)

                @block.vector
                def _(dve):
                    for h in range(H):
                        dve.wait_ge(moved, h + 1)
                        dve.tensor_copy(val[:, h, :], ex[:, h, :]).then_inc(step, 1)
                    dve.wait_ge(step, H)
                    totals_v(dve, 0, True, heads(val), heads(scratch))
                    for h in range(H):
                        dve.tensor_tensor(ex[:, h, :], ex[:, h, :], val[:, h, :], ALU.subtract).then_inc(step, 1)
                    dve.wait_ge(exped, H)
                    for h in range(H):
                        cp = dve.tensor_copy(val[:, h, :], ex[:, h, :]).then_inc(placed, 1)
                    dve.wait_ge(placed, H)
                    totals_v(dve, 1, False, heads(val), heads(scratch))
                    for h in range(H):
                        dve.reciprocal(scratch[:, h, :], val[:, h, :]).then_inc(placed, 1)
                    for h in range(H):
                        dve.wait_ge(placed, H + h + 1)
                        dve.tensor_tensor(val[:, h, :], ex[:, h, :], scratch[:, h, :], ALU.mult).then_inc(step, 1)
                    for h in range(H):
                        dve.wait_ge(back, h + 1)
                        dve.tensor_copy(scores[:, :, :, h].rearrange("p q j -> p j q"), ps_b[h % 2][:, :, :]).then_inc(placed, 1)

    def head_sums(a_t, agg2):
        with ExitStack() as ctx:
            tmp, psum, sem, pair = scope(ctx, "g2")
            NWM = P // WIN
            v, weighted = tmp("v", [P, 2, J, D]), tmp("weighted", [P, 2, J, D])
            onehot = tmp("onehot", [P, 2, NWM, J, WIN])
            ps_a = [psum(f"ps_a{s}", [P, NWM, J, WIN]) for s in range(2)]
            cleared, added = sem("cleared"), sem("added")
            v_in, made, a_mm = pair("v_in"), pair("made"), pair("a_mm")

            def pe_program(pe, nw):
                def body(i, first):
                    for s in range(2):
                        pe.wait_ge(made[s], i + 1)
                        if not first:
                            pe.wait_ge(added, J * nw * (2 * i + s - 1))
                        for w in range(nw):
                            for j in range(J):
                                mm = pe.matmul(ps_a[s][:, w, j, :], weighted[:, s, j, :], onehot[:, s, w, j, :], start=True, stop=True)
                        mm.then_inc(a_mm[s], 1)
                pairs(pe, body)

            def dve_program(dve, nw):
                dve.memset(agg2[:, :], 0.0).then_inc(cleared, 1)
                dve.wait_ge(cleared, 1)

                def add(i, s):
                    dve.wait_ge(a_mm[s], i + 1)
                    dve.nop(nofuse=True)
                    add_windows(dve, agg2, ps_a, s, 2 * i + s, nw, added)

                def body(i, first):
                    for s in range(2):
                        dve.wait_ge(a_mm[s], i)
                        dve.wait_ge(v_in[s], 16 * (i + 1))
                        mark_nodes(dve, onehot, s, 2 * i + s, nw)
                        dve.tensor_tensor(weighted[:, s, :, :].rearrange("p j (h o) -> p (j h) o", o=DH),
                                          v[:, s, :, :].rearrange("p j (h o) -> p (j h) o", o=DH),
                                          a_t[:, bass.ds((2 * i + s) * J * H, J * H)].unsqueeze(2).to_broadcast([P, J * H, DH]), ALU.mult).then_inc(made[s], 1)
                        if not (first and s == 0):
                            add(i - 1 + s, 1 - s)
                pairs(dve, body)
                add(Q // 2 - 1, 1)

            with nc.Block() as block:
                @block.sync
                def _(sp):
                    with sp.Fori(0, Q // 2) as i:
                        for s in range(2):
                            sp.wait_ge(made[s], i)
                            sp.dma_start(v[:, s, :, :].rearrange("p j f -> p (j f)"),
                                         v_edges[bass.ds(2 * i + s, 1), :, :].rearrange("a p f -> (a p) f")).then_inc(v_in[s], 16)

                @block.tensor
                def _(pe):
                    both_ways(pe, lambda nw: pe_program(pe, nw))

                @block.vector
                def _(dve):
                    both_ways(dve, lambda nw: dve_program(dve, nw))

    def head_nodes(agg2):
        with ExitStack() as ctx:
            tmp, psum, sem, pair = scope(ctx, "n2")
            wa = tmp("wa", [P, NT, D])
            ln_g, ln_b, film_b, film = tmp("ln_g", [P, D]), tmp("ln_b", [P, D]), tmp("film_b", [P, 2 * D]), tmp("film", [P, 2 * D])
            film_w, context, context_all = tmp("film_w", [CTX, 2 * D]), tmp("context", [CTX, 1]), tmp("context_all", [CTX, P])
            skip, alpha = tmp("skip", [P, NT]), tmp("alpha", [P, NT])
            types, mask = tmp("types", [P, NGRP, K4], I32), tmp("mask", [P, NT, NGRP * K4])
            keep = tmp("keep", [P, NGRP * K4])
            part = tmp("part", [P, GE])
            xg, y, z, v, x3 = (tmp(n, [P, K4, D]) for n in ("xg", "y", "z", "v", "x3"))
            stats, mean_var = tmp("stats", [P, K4, 6]), tmp("mean_var", [P, K4, 2])
            var_eps, root, inverse = (tmp(n, [P, K4]) for n in ("var_eps", "root", "inverse"))
            ps_h = [psum(f"ps_h{k}", [P, 512]) for k in range(K4)]
            ps_f = psum("ps_f", [P, 2 * D])
            weights_in, x_in, parts, h_mm, rooted, vec, pre, stored, film_mm, sig = (sem(n) for n in
                ("weights_in", "x_in", "parts", "h_mm", "rooted", "vec", "pre", "stored", "film_mm", "sig"))
            V = 20
            n_pre = 1 + NT + NT + 2 + NT

            with nc.Block() as block:
                @block.sync
                def _(sp):
                    sp.dma_start(wa[:, :, :], L2_gnn_Wa.rearrange("t f c -> f t c")).then_inc(weights_in, 16)
                    for to, frm, n in ((ln_g, L2_gnn_ln_g, D), (ln_b, L2_gnn_ln_b, D), (film_b, L2_gnn_film_b, 2 * D), (skip, L2_gnn_skip, NT)):
                        sp.dma_start(to[:, :], across(frm, n)).then_inc(weights_in, 16)
                    sp.dma_start(film_w[:, :], L2_gnn_film_w).then_inc(weights_in, 16)
                    sp.dma_start(context[:, :], L2_gnn_global_context.rearrange("(c a) -> c a", a=1)).then_inc(weights_in, 16)
                    sp.dma_start(types[:, :, :], type_pad.rearrange("(g p k) -> p g k", p=P, k=K4)).then_inc(weights_in, 16)

                    def group(g, last):
                        if not last:
                            sp.wait_ge(vec, V * g + 15)
                            sp.dma_start(xg[:, :, :], rows_of(xs[2], g + 1, D)).then_inc(x_in, 16)
                        sp.wait_ge(vec, V * g + V)
                        sp.dma_start(rows_of(xs[3], g, D), x3[:, :, :]).then_inc(stored, 16)
                    sp.dma_start(xg[:, :, :], rows_of(xs[2], 0, D)).then_inc(x_in, 16)
                    over_groups(sp, group)
                    sp.wait_ge(stored, 16 * NGRP)

                @block.tensor
                def _(pe):
                    pe.wait_ge(weights_in, 16 * 8)
                    pe.wait_ge(pre, 1)
                    pe.matmul(ps_f[:, :], context_all[:, :], film_w[:, :], start=True, stop=True).then_inc(film_mm, 1)

                    def hidden(g):
                        pe.wait_ge(parts, g + 1)
                        for k in range(K4):
                            mm = pe.matmul(ps_h[k][:, 0:NT * D], part[:, k::K4], wa[:, :, :].rearrange("f t c -> f (t c)"), start=True, stop=True)
                        mm.then_inc(h_mm, 1)

                    def group(g, last):
                        if not last:
                            pe.wait_ge(vec, V * g + 4)
                            hidden(g + 1)
                    hidden(0)
                    over_groups(pe, group)

                @block.scalar
                def _(act):
                    act.wait_ge(weights_in, 16 * 8)
                    act.activation(alpha[:, :], skip[:, :], ACT.Sigmoid).then_inc(sig, 1)

                    def cut(g):
                        hold(act, h_mm, g)
                        act.copy(part[:, :], agg2[:, bass.ds(g * GE, GE)]).then_inc(parts, 1)

                    def group(g, last):
                        if not last:
                            cut(g + 1)
                        act.wait_ge(vec, V * g + 7)
                        act.activation(root[:, :], var_eps[:, :], ACT.Sqrt).then_inc(rooted, 1)
                        act.wait_ge(vec, V * g + 18)
                        act.activation(root[:, :], var_eps[:, :], ACT.Sqrt).then_inc(rooted, 1)
                    cut(0)
                    over_groups(act, group)

                @block.vector
                def _(dve):
                    dve.wait_ge(weights_in, 16 * 8)
                    dve.tensor_copy(context_all[:, :], context[:, 0:1].to_broadcast([CTX, P])).then_inc(pre, 1)
                    for t in range(NT):
                        dve.tensor_scalar(mask[:, t, :], types[:, :, :].rearrange("p g k -> p (g k)"), float(t), None, ALU.is_equal).then_inc(pre, 1)
                    dve.wait_ge(pre, 1 + NT)
                    dve.wait_ge(sig, 1)
                    for t in range(NT):
                        dve.tensor_scalar(mask[:, t, :], mask[:, t, :], alpha[:, t:t + 1], None, ALU.mult).then_inc(pre, 1)
                    dve.wait_ge(film_mm, 1)
                    dve.tensor_tensor(film[:, :], ps_f[:, :], film_b[:, :], ALU.add).then_inc(pre, 1)
                    dve.memset(keep[:, :], 1.0).then_inc(pre, 1)
                    for t in range(NT):
                        dve.wait_ge(pre, 1 + 2 * NT + 2 + t)
                        dve.tensor_tensor(keep[:, :], keep[:, :], mask[:, t, :], ALU.subtract).then_inc(pre, 1)
                    dve.wait_ge(pre, n_pre)
                    wide_b = lambda a: a.unsqueeze(1).to_broadcast([P, K4, D])

                    def group(g, last):
                        at = V * g
                        dve.wait_ge(h_mm, g + 1)
                        dve.wait_ge(x_in, 16 * (g + 1))
                        for k in range(K4):
                            st = dve.tensor_scalar(y[:, k, :], xg[:, k, :], keep[:, bass.ds(g * K4 + k, 1)], None, ALU.mult)
                        st.then_inc(vec, 1)
                        for t in range(NT):
                            dve.wait_ge(vec, at + 1 + t)
                            to, frm = ((z, y), (y, z), (z, y))[t]
                            for k in range(K4):
                                st = dve.scalar_tensor_tensor(out=to[:, k, :], in0=ps_h[k][:, t * D:(t + 1) * D], scalar=mask[:, t, bass.ds(g * K4 + k, 1)],
                                                              in1=frm[:, k, :], op0=ALU.mult, op1=ALU.add)
                            st.then_inc(vec, 1)
                        dve.wait_ge(vec, at + 4)
                        norm_stats(dve, z, stats, mean_var, var_eps, vec, at + 4)
                        dve.wait_ge(rooted, 2 * g + 1)
                        norm_apply(dve, y, z, mean_var, root, inverse, vec, at + 7)
                        at = at + 9
                        dve.wait_ge(vec, at)
                        dve.tensor_tensor(v[:, :, :], y[:, :, :], wide_b(ln_g[:, :]), ALU.mult).then_inc(vec, 1)
                        dve.wait_ge(vec, at + 1)
                        dve.tensor_tensor(y[:, :, :], v[:, :, :], wide_b(ln_b[:, :]), ALU.add).then_inc(vec, 1)
                        dve.wait_ge(vec, at + 2)
                        dve.tensor_tensor(v[:, :, :], y[:, :, :], xg[:, :, :], ALU.add).then_inc(vec, 1)
                        dve.wait_ge(vec, at + 3)
                        dve.tensor_tensor(y[:, :, :], v[:, :, :], wide_b(film[:, 0:D]), ALU.mult).then_inc(vec, 1)
                        dve.wait_ge(vec, at + 4)
                        dve.tensor_tensor(v[:, :, :], y[:, :, :], wide_b(film[:, D:2 * D]), ALU.add).then_inc(vec, 1)
                        at = at + 5
                        dve.wait_ge(vec, at)
                        dve.tensor_tensor(z[:, :, :], v[:, :, :], xg[:, :, :], ALU.add).then_inc(vec, 1)
                        dve.wait_ge(vec, at + 1)
                        norm_stats(dve, z, stats, mean_var, var_eps, vec, at + 1)
                        dve.wait_ge(rooted, 2 * g + 2)
                        hold(dve, stored, 16 * g)
                        norm_apply(dve, x3, z, mean_var, root, inverse, vec, at + 4)
                    over_groups(dve, group)

    def propagate():
        with ExitStack() as ctx:
            tmp, psum, sem, pair = scope(ctx, "e3")
            NWM = P // WIN
            src_all = tmp("src_all", [P, 2, J, P])
            equal = tmp("equal", [P, 2, J, P])
            junk, below, spare = tmp("junk", [P, J, P]), tmp("below", [P, P]), tmp("spare", [P, 1])
            earlier, again, shift = tmp("earlier", [P, 2, J]), tmp("again", [P, 2, J]), tmp("shift", [P, 2, J])
            row = tmp("row", [P, 2, J], I32)
            weighted, merged = tmp("weighted", [P, 2, J, D]), tmp("merged", [P, 2, J, D])
            onehot = tmp("onehot", [P, 2, NWM, J, WIN])
            spread, window = tmp("spread", [P, 2, NWM, J, P]), tmp("window", [P, 2, NWM, D])
            ps_t = [psum(f"ps_t{s}", [P, NWM, P]) for s in range(2)]
            ps_y = [psum(f"ps_y{s}", [P, J, D]) for s in range(2)]
            ps_z = [psum(f"ps_z{s}", [P, J, D]) for s in range(2)]
            cleared = sem("cleared")
            src_in, win_in, marked, turned, copied, y_mm, y_out, compared, z_mm, z_out, placed, counted = (pair(n) for n in
                ("src_in", "win_in", "marked", "turned", "copied", "y_mm", "y_out", "compared", "z_mm", "z_out", "placed", "counted"))
            sent = [sem(f"sent{c}") for c in range(COPIES)]

            def sync_program(sp, nw):
                with sp.Fori(0, Q // 2) as i:
                    for s in range(2):
                        sp.wait_ge(counted[s], i)
                        sp.dma_start(src_all[:, s, :, :].rearrange("p j e -> p (j e)"),
                                     src_row.rearrange("(q e) -> q e", e=GE)[bass.ds(2 * i + s, 1), :].broadcast_to([P, GE])).then_inc(src_in[s], 16)
                        sp.wait_ge(y_mm[s], i)
                        sp.nop(nofuse=True)
                        load_windows(sp, window, s, xs[3], 2 * i + s, nw, win_in[s])

            def pe_program(pe, nw):
                def expand(i, s):
                    pe.wait_ge(win_in[s], 16 * J * nw * (i + 1))
                    pe.wait_ge(copied[s], i + 1)
                    pe.wait_ge(y_out[s], i)
                    for j in range(J):
                        for w in range(nw):
                            mm = pe.matmul(ps_y[s][:, j, :], spread[:, s, w, j, :], window[:, s, w, :], start=(w == 0), stop=(w == nw - 1))
                    mm.then_inc(y_mm[s], 1)

                def merge(i, s):
                    pe.wait_ge(compared[s], i + 1)
                    pe.wait_ge(y_out[s], i + 1)
                    pe.wait_ge(z_out[s], i)
                    for j in range(J):
                        mm = pe.matmul(ps_z[s][:, j, :], equal[:, s, j, :], weighted[:, s, j, :], start=True, stop=True)
                    mm.then_inc(z_mm[s], 1)

                def body(i, first):
                    for s in range(2):
                        pe.wait_ge(marked[s], i + 1)
                        pe.wait_ge(copied[s], i)
                        for w in range(nw):
                            mm = pe.transpose(ps_t[s][:, w, :], onehot[:, s, w, :, :].rearrange("p j n -> p (j n)"), ident[:, :])
                        mm.then_inc(turned[s], 1)
                        if not (first and s == 0):
                            merge(i - 1 + s, 1 - s)
                        expand(i, s)
                pairs(pe, body)
                merge(Q // 2 - 1, 1)

            def act_program(act, nw):
                act.wait_ge(cleared, 3)

                def body(i, first):
                    for s in range(2):
                        act.wait_ge(turned[s], i + 1)
                        act.wait_ge(y_mm[s], i)
                        spread_nodes(act, spread, ps_t[s], s, nw).then_inc(copied[s], 1)
                        if not (first and s == 0):
                            merged_out(i - 1 + s, 1 - s, s)

                def merged_out(i, s, turn):
                    act.wait_ge(z_mm[s], i + 1)
                    for j in range(J):
                        act.wait_ge(sent[s * J + j], 16 * i)
                    act.copy(merged[:, s, :, :], ps_z[s][:, :, :]).then_inc(z_out[s], 1)
                pairs(act, body)
                merged_out(Q // 2 - 1, 1, 0)

            def dve_program(dve, nw):
                dve.memset(spread[:, :, :, :, :], 0.0).then_inc(cleared, 1)
                dve.tensor_scalar(spare[:, :], ident[:, 0:1], 0.0, None, ALU.mult).then_inc(cleared, 1)
                dve.wait_ge(cleared, 3)
                dve.tensor_tensor_reduce(junk[:, 0, :], ident[:, :], iota[:, 0:P], 1.0, 0.0, ALU.mult, ALU.add, spare[:, :]).then_inc(cleared, 1)
                dve.wait_ge(cleared, 4)
                dve.tensor_scalar(below[:, :], iota[:, 0:P], spare[:, 0:1], None, ALU.is_lt).then_inc(cleared, 1)
                dve.wait_ge(cleared, 5)
                dve.tensor_scalar(spare[:, :], spare[:, :], float(N), None, ALU.add).then_inc(cleared, 1)
                dve.wait_ge(cleared, 6)

                def weigh(i, s):
                    dve.wait_ge(y_mm[s], i + 1)
                    dve.wait_ge(z_mm[s], i)
                    dve.tensor_tensor(weighted[:, s, :, :], ps_y[s][:, :, :],
                                      w_t[:, bass.ds((2 * i + s) * J, J)].unsqueeze(2).to_broadcast([P, J, D]), ALU.mult).then_inc(y_out[s], 1)

                def compare(i, s):
                    q = 2 * i + s
                    dve.wait_ge(src_in[s], 16 * (i + 1))
                    dve.wait_ge(z_mm[s], i)
                    for j in range(J):
                        eq = dve.tensor_scalar(equal[:, s, j, :], src_all[:, s, j, :], src_t[:, bass.ds(q * J + j, 1)], None, ALU.is_equal)
                    eq.then_inc(compared[s], 1)
                    dve.wait_ge(compared[s], i + 1)
                    for j in range(J):
                        cnt = dve.tensor_tensor_reduce(junk[:, j, :], equal[:, s, j, :], below[:, :], 1.0, 0.0, ALU.mult, ALU.add, earlier[:, s, j:j + 1])
                    cnt.then_inc(counted[s], 1)
                    dve.wait_ge(counted[s], i + 1)
                    dve.tensor_scalar(again[:, s, :], earlier[:, s, :], 0.0, None, ALU.is_gt)
                    dve.tensor_scalar(shift[:, s, :], src_t[:, bass.ds(q * J, J)], spare[:, 0:1], -1.0, ALU.subtract, ALU.mult).then_inc(placed[s], 1)
                    dve.wait_ge(placed[s], 3 * i + 1)
                    dve.tensor_tensor(shift[:, s, :], shift[:, s, :], again[:, s, :], ALU.mult).then_inc(placed[s], 1)
                    dve.wait_ge(placed[s], 3 * i + 2)
                    for j in range(J):
                        dve.wait_ge(sent[s * J + j], 16 * i)
                    dve.tensor_tensor(row[:, s, :], shift[:, s, :], src_t[:, bass.ds(q * J, J)], ALU.add).then_inc(placed[s], 1)

                def body(i, first):
                    for s in range(2):
                        dve.wait_ge(turned[s], i)
                        mark_nodes(dve, onehot, s, 2 * i + s, nw).then_inc(marked[s], 1)
                        if s == 1 or not first:
                            dve.wait_ge(counted[1 - s], i + s)
                        compare(i, s)
                        weigh(i, s)
                pairs(dve, body)

            with nc.Block() as block:
                @block.gpsimd
                def _(pool):
                    pool.memset(junk[:, 1, 0:1], 0.0).then_inc(cleared, 1)
                    with pool.Fori(0, Q // 2) as i:
                        for s in range(2):
                            pool.wait_ge(z_out[s], i + 1)
                            pool.wait_ge(placed[s], 3 * (i + 1))
                            for j in range(J):
                                c = s * J + j
                                pool.wait_ge(sent[c], 16 * i)
                                pool.nop(nofuse=True)
                                pool.indirect_dma_start(side[c], bass.IndirectOffsetOnAxis(ap=row[:, s, j:j + 1], axis=0),
                                                        merged[:, s, j, :], None, compute_op=ALU.add).then_inc(sent[c], 16)
                    for c in range(COPIES):
                        pool.wait_ge(sent[c], 16 * (Q // 2))

                @block.sync
                def _(sp):
                    both_ways(sp, lambda nw: sync_program(sp, nw))

                @block.tensor
                def _(pe):
                    both_ways(pe, lambda nw: pe_program(pe, nw))

                @block.scalar
                def _(act):
                    both_ways(act, lambda nw: act_program(act, nw))

                @block.vector
                def _(dve):
                    both_ways(dve, lambda nw: dve_program(dve, nw))

    def last_nodes():
        with ExitStack() as ctx:
            tmp, psum, sem, pair = scope(ctx, "n3")
            xg, total, y, z = (tmp(n, [P, K4, D]) for n in ("xg", "total", "y", "z"))
            parts = tmp("parts", [P, COPIES, K4, D])
            stats, mean_var = tmp("stats", [P, K4, 6]), tmp("mean_var", [P, K4, 2])
            var_eps, root, inverse = (tmp(n, [P, K4]) for n in ("var_eps", "root", "inverse"))
            x_in, rooted, vec, stored = sem("x_in"), sem("rooted"), sem("vec"), sem("stored")
            V = COPIES + 7
            whole = N // GE
            rest = N - whole * GE

            with nc.Block() as block:
                @block.sync
                def _(sp):
                    def body(g, rows):
                        parts_n = rows // K4
                        sp.wait_ge(vec, V * g)
                        if rows == GE:
                            sp.dma_start(xg[:, :, :], rows_of(xs[3], g, D)).then_inc(x_in, 16)
                            for c in range(COPIES):
                                flat = side[c][0:whole * GE, :].rearrange("(a k) f -> a (k f)", k=K4)
                                sp.dma_start(parts[:, c, :, :].rearrange("p k f -> p (k f)"), flat[bass.ds(g * P, P), :]).then_inc(x_in, 16)
                        else:
                            sp.dma_start(xg[:, :, :], rows_of(xs[3], g, D)).then_inc(x_in, 16)
                            for c in range(COPIES):
                                flat = side[c][whole * GE:whole * GE + parts_n * K4, :].rearrange("(a k) f -> a (k f)", k=K4)
                                sp.dma_start(parts[0:parts_n, c, :, :].rearrange("p k f -> p (k f)"), flat).then_inc(x_in, 16)
                        sp.wait_ge(vec, V * (g + 1))
                        if rows == GE:
                            flat = out[0:whole * GE, :].rearrange("(a k) f -> a (k f)", k=K4)
                            sp.dma_start(flat[bass.ds(g * P, P), :], z[:, :, :].rearrange("p k f -> p (k f)")).then_inc(stored, 16)
                        else:
                            n = rest // K4
                            sp.dma_start(out[whole * GE:whole * GE + n * K4, :].rearrange("(a k) f -> a (k f)", k=K4),
                                         z[0:n, :, :].rearrange("p k f -> p (k f)")).then_inc(stored, 16)
                            left = rest - n * K4
                            sp.dma_start(out[N - left:N, :].rearrange("(a k) f -> a (k f)", k=left),
                                         z[n:n + 1, 0:left, :].rearrange("p k f -> p (k f)")).then_inc(stored, 16)
                    with sp.Fori(0, whole) as g:
                        body(g, GE)
                    body(whole, -(-rest // K4) * K4)
                    sp.wait_ge(stored, 16 * (whole + 2))

                @block.scalar
                def _(act):
                    with act.Fori(0, whole + 1) as g:
                        act.wait_ge(vec, V * g + V - 2)
                        act.activation(root[:, :], var_eps[:, :], ACT.Sqrt).then_inc(rooted, 1)

                @block.vector
                def _(dve):
                    with dve.Fori(0, whole + 1) as g:
                        at = V * g
                        dve.wait_ge(x_in, 16 * (COPIES + 1) * (g + 1))
                        dve.tensor_tensor(total[:, :, :], parts[:, 0, :, :], parts[:, 1, :, :], ALU.add).then_inc(vec, 1)
                        for c in range(2, COPIES):
                            dve.wait_ge(vec, at + c - 1)
                            dve.tensor_tensor(total[:, :, :], total[:, :, :], parts[:, c, :, :], ALU.add).then_inc(vec, 1)
                        at = at + COPIES - 1
                        dve.wait_ge(vec, at)
                        dve.scalar_tensor_tensor(out=y[:, :, :], in0=total[:, :, :], scalar=3.0, in1=xg[:, :, :],
                                                 op0=ALU.mult, op1=ALU.add).then_inc(vec, 1)
                        dve.wait_ge(vec, at + 1)
                        dve.tensor_scalar(y[:, :, :], y[:, :, :], 0.25, None, ALU.mult).then_inc(vec, 1)
                        dve.wait_ge(vec, at + 2)
                        dve.tensor_tensor(total[:, :, :], y[:, :, :], xg[:, :, :], ALU.add).then_inc(vec, 1)
                        dve.wait_ge(vec, at + 3)
                        norm_stats(dve, total, stats, mean_var, var_eps, vec, at + 3)
                        dve.wait_ge(rooted, g + 1)
                        dve.wait_ge(stored, 16 * g)
                        norm_apply(dve, z, total, mean_var, root, inverse, vec, at + 6)

    lay_out()
    with ExitStack() as layer0:
        agg = layer0.enter_context(nc.sbuf_tensor("agg0", [P, NP * R], F32))
        share = layer0.enter_context(nc.sbuf_tensor("share", [1, NP * R], F32))
        with ExitStack() as edges0:
            u_keys = edges0.enter_context(nc.sbuf_tensor("u_keys", [P, D], F32))
            e_bias = edges0.enter_context(nc.sbuf_tensor("e_bias", [Q, R], F32))
            e_t = edges0.enter_context(nc.sbuf_tensor("e_t", [P, T], F32))
            rel_tables(u_keys, e_bias, agg, share)
            rel_scores(u_keys, e_t)
            rel_softmax(e_t, e_bias)
        rel_sums(agg, share)
        rel_nodes(agg, share)
    layer1 = top.enter_context(ExitStack())
    agg1 = layer1.enter_context(nc.sbuf_tensor("agg1", [P, NP], F32))
    messages(agg1)
    message_nodes(agg1)
    layer1.close()
    with ExitStack() as layer2:
        a_t = layer2.enter_context(nc.sbuf_tensor("a_t", [P, T * H], F32))
        agg2 = layer2.enter_context(nc.sbuf_tensor("agg2", [P, NP], F32))
        head_scores(a_t)
        head_softmax(a_t)
        head_sums(a_t, agg2)
        head_nodes(agg2)
    propagate()
    last_nodes()
    top.close()


OUT = ((N, D), "float32")


def kernel(**inputs):
    import numpy as np
    import concourse.bacc as bacc
    from concourse.bass_utils import run_bass_kernel_spmd

    nc = bacc.Bacc("TRN2", target_bir_lowering=False, num_devices=1)
    arrays, args = {}, {}
    for name, value in inputs.items():
        a = np.ascontiguousarray(value)
        arrays[f"in_{name}_dram"] = a
        args[name] = nc.dram_tensor(f"in_{name}_dram", a.shape, mybir.dt.from_np(a.dtype), kind="ExternalInput").ap()
    args["out"] = nc.dram_tensor("out_0_dram", OUT[0], mybir.dt.from_np(np.dtype(OUT[1])), kind="ExternalOutput").ap()
    build(nc, **args)
    result = run_bass_kernel_spmd(nc, [arrays], core_ids=[0])
    return result.results[0]["out_0_dram"]
```

```python
from contextlib import ExitStack

import concourse.bass as bass
from concourse import mybir
from concourse.alu_op_type import AluOpType as ALU

ACT = mybir.ActivationFunctionType
AX = mybir.AxisListType
F32 = mybir.dt.float32
I32 = mybir.dt.int32

P = 128
N = 3125
D = 128
E = 53125
J = 4
GE = J * P
Q = -(-E // GE)
T = Q * J
R = 4
H, DH = 8, 16
NT = 3
REL = 64
CTX = 64
K4 = 4
NGRP = -(-(N + 1 + P) // GE)
NP = NGRP * GE
WIN = 32
KEYS = WIN * R
EPS = 1e-5
BIG = 3e30
NEG = 1e30
COPIES = 8
U = 4


def build(nc, x, src, dst, edge_attr_64, edge_type_4, edge_weight, node_type_3,
          L0_gnn_W_R, L0_gnn_b_R, L0_gnn_W_Q, L0_gnn_b_Q, L0_gnn_W_K, L0_gnn_b_K, L0_gnn_W_V, L0_gnn_b_V,
          L0_gnn_a_w, L0_gnn_a_b, L1_gnn_W1, L1_gnn_b1, L1_gnn_W2, L1_gnn_b2, L1_gnn_Wn, L1_gnn_bn,
          L1_gnn_gamma, L1_gnn_beta, L2_gnn_global_context, L2_gnn_Wk, L2_gnn_Wq, L2_gnn_Wv,
          L2_gnn_rel_att, L2_gnn_rel_msg, L2_gnn_rel_pri, L2_gnn_Wa, L2_gnn_skip, L2_gnn_ln_g,
          L2_gnn_ln_b, L2_gnn_film_w, L2_gnn_film_b, out):
    top = ExitStack()

    def dram(name, shape, dt=F32):
        return nc.dram_tensor(name, shape, dt, kind="Internal").ap()

    xs = [dram(f"x_layer{n}", [NP, D]) for n in range(4)]
    type_pad = dram("node_type_padded", [NP], I32)
    base_row = dram("tile_base", [T], I32)
    src_row = dram("src_padded", [T * P])
    rel_table = dram("rel_src_table", [NP * R, D])
    rel_window = dram("rel_dst_table", [NP * R, D])
    rel_edges = dram("rel_edges", [Q, P, J * D])
    msg_table = dram("msg_src_table", [NP, D])
    msg_window = dram("msg_dst_table", [NP, D])
    kv_table = dram("kv_table", [NP, 2 * D])
    q_window = dram("q_table", [NP, D])
    v_edges = dram("v_edges", [Q, P, J * D])
    side = [dram(f"side_{c}", [N + P, D]) for c in range(COPIES)]

    def sb(name, shape, dt=F32):
        return top.enter_context(nc.sbuf_tensor(name, shape, dt))

    ident = sb("ident", [P, P])
    iota = sb("iota", [P, R * P])
    ones = sb("ones", [P, P])
    key_t = sb("key_t", [P, T])
    dl_t = sb("dl_t", [P, T])
    rel_idx = sb("rel_idx", [P, T], I32)
    src_idx = sb("src_idx", [P, T], I32)
    src_t = sb("src_t", [P, T])
    w_t = sb("w_t", [P, T])
    attn_t = sb("attn_t", [P, T])
    base_sb = sb("base_sb", [1, T], I32)
    typ_s = sb("typ_s", [Q, GE])
    pen = sb("pen", [Q, GE + 1])
    same = sb("same", [Q, GE + 1])
    in_first = sb("in_first", [Q, GE])
    in_last = sb("in_last", [Q, GE])
    pen_first = sb("pen_first", [Q, GE])
    pen_last = sb("pen_last", [Q, GE])
    cont = sb("cont", [H, Q + 1])
    through = sb("through", [H, Q + 2])
    wide = sb("wide", [1, 1], I32)

    def window_bases(engines, q):
        _, bases = nc.values_load_multi_w_load_instructions(base_sb[0:1, bass.ds(q * J, J)], engines=engines, min_val=0, max_val=N,
                                                            skip_runtime_bounds_check_because="dst is a node")
        return bases

    def lay_out():
        with ExitStack() as ctx:
            def tmp(name, shape, dt=F32):
                return ctx.enter_context(nc.sbuf_tensor(name, shape, dt))

            def sem(name):
                return ctx.enter_context(nc.semaphore(name))

            src_i, dst_i, typ_i = (tmp(n, [Q, GE], I32) for n in ("src_i", "dst_i", "typ_i"))
            w_s, src_s, dst_s, dl_s, key_s, idx_s = (tmp(n, [Q, GE]) for n in
                                                      ("w_s", "src_s", "dst_s", "dl_s", "key_s", "idx_s"))
            base_i = tmp("base_i", [Q, J], I32)
            top_s = tmp("top_s", [Q, 1])
            ends = tmp("ends", [Q, 2, H])
            rows = tmp("rows", [H, 2, Q])
            zero_x = tmp("zero_x", [P, D])
            zero_i = tmp("zero_i", [NP - N, 1], I32) if NP - N <= P else tmp("zero_i", [1, NP - N], I32)
            zeros_set, edges_in, pads_in, made, moved, turned, stored = (sem(n) for n in
                ("zeros_set", "edges_in", "pads_in", "made", "moved", "turned", "stored"))
            ps = [ctx.enter_context(nc.psum_tensor(f"lay_ps{i}", [P, J, Q], F32)) for i in range(5)]
            ps_row = ctx.enter_context(nc.psum_tensor("lay_row", [H, 2, P], F32))
            ps_top = ctx.enter_context(nc.psum_tensor("lay_top", [1, P], F32))
            last = E - (Q - 1) * GE

            with nc.Block() as block:
                @block.gpsimd
                def _(pool):
                    pool.memset(src_i[:, :], 0).then_inc(zeros_set, 1)
                    pool.memset(dst_i[:, :], N).then_inc(zeros_set, 1)
                    pool.memset(typ_i[:, :], 0).then_inc(zeros_set, 1)
                    pool.memset(w_s[:, :], 0.0).then_inc(zeros_set, 1)
                    pool.memset(zero_x[:, :], 0.0).then_inc(zeros_set, 1)
                    pool.memset(zero_i[:, :], 0).then_inc(zeros_set, 1)
                    pool.memset(ones[:, :], 1.0).then_inc(zeros_set, 1)
                    pool.memset(ident[:, :], 0.0).then_inc(made, 1)
                    pool.wait_ge(made, 1)
                    pool.affine_select(out=ident[:, :], in_=ident[:, :], compare_op=ALU.not_equal, fill=1.0,
                                       base=0, pattern=[[-1, P]], channel_multiplier=1).then_inc(made, 1)
                    pool.iota(iota[:, :], [[1, R * P]], base=0, channel_multiplier=0,
                              allow_small_or_imprecise_dtypes=True).then_inc(made, 1)

                @block.sync
                def _(sp):
                    sp.wait_ge(zeros_set, 7)
                    for to, frm in ((src_i, src), (dst_i, dst), (typ_i, edge_type_4), (w_s, edge_weight)):
                        sp.dma_start(to[0:Q - 1, :], frm[0:(Q - 1) * GE].rearrange("(q e) -> q e", e=GE)).then_inc(edges_in, 16)
                        sp.dma_start(to[Q - 1:Q, 0:last], frm[(Q - 1) * GE:E].rearrange("(q e) -> q e", q=1)).then_inc(edges_in, 16)
                    sp.dma_start(xs[0][0:N, :], x).then_inc(pads_in, 16)
                    a = N
                    while a < NP:
                        n = min(P, NP - a)
                        sp.dma_start(xs[0][a:a + n, :], zero_x[0:n, 0:D]).then_inc(pads_in, 16)
                        a += n
                    sp.dma_start(type_pad[0:N].rearrange("(a n) -> a n", a=5), node_type_3.rearrange("(a n) -> a n", a=5)).then_inc(pads_in, 16)
                    sp.dma_start(type_pad[N:NP].rearrange("(a n) -> a n", a=1), zero_i[:, :]).then_inc(pads_in, 16)
                    n_pads = 3 + -(-(NP - N) // P)
                    sp.wait_ge(moved, 2)
                    sp.dma_start(base_row.rearrange("(q j) -> q j", j=J), base_i[:, :]).then_inc(stored, 16)
                    sp.dma_start(src_row.rearrange("(q e) -> q e", e=GE), src_s[:, :]).then_inc(stored, 16)
                    sp.wait_ge(stored, 32)
                    sp.dma_start(base_sb[:, :], base_row.rearrange("(a t) -> a t", a=1)).then_inc(stored, 16)
                    sp.wait_ge(stored, 48)
                    sp.wait_ge(pads_in, 16 * n_pads)

                @block.vector
                def _(dve):
                    dve.wait_ge(edges_in, 16 * 8)
                    dve.tensor_copy(src_s[:, :], src_i[:, :]).then_inc(moved, 1)
                    dve.tensor_copy(base_i[:, :], dst_i[:, ::P]).then_inc(moved, 1)
                    dve.tensor_copy(dst_s[:, :], dst_i[:, :]).then_inc(moved, 1)
                    dve.tensor_copy(typ_s[:, :], typ_i[:, :]).then_inc(moved, 1)
                    dve.wait_ge(moved, 4)
                    tiles = lambda a: a[:, :].rearrange("q (j e) -> q j e", e=P)
                    dve.tensor_tensor(tiles(dl_s), tiles(dst_s), tiles(dst_s)[:, :, 0:1].to_broadcast([Q, J, P]),
                                      ALU.subtract).then_inc(moved, 1)
                    dve.scalar_tensor_tensor(out=idx_s[:, :], in0=src_s[:, :], scalar=float(R), in1=typ_s[:, :],
                                             op0=ALU.mult, op1=ALU.add).then_inc(moved, 1)
                    dve.wait_ge(moved, 5)
                    dve.scalar_tensor_tensor(out=key_s[:, :], in0=dl_s[:, :], scalar=float(R), in1=typ_s[:, :],
                                             op0=ALU.mult, op1=ALU.add).then_inc(moved, 1)
                    dve.tensor_reduce(top_s[:, :], dl_s[:, :], AX.X, ALU.max).then_inc(moved, 1)
                    dve.memset(same[:, :], 0.0).then_inc(moved, 1)
                    dve.wait_ge(moved, 9)
                    dve.tensor_tensor(same[:, 1:GE], dst_s[:, 1:GE], dst_s[:, 0:GE - 1], ALU.is_equal).then_inc(moved, 1)
                    dve.tensor_scalar(in_first[:, :], dst_s[:, :], dst_s[:, 0:1], None, ALU.is_equal).then_inc(moved, 1)
                    dve.tensor_scalar(in_last[:, :], dst_s[:, :], dst_s[:, GE - 1:GE], None, ALU.is_equal).then_inc(moved, 1)
                    dve.tensor_copy(ends[:, 0, :], dst_s[:, 0:1].to_broadcast([Q, H])).then_inc(moved, 1)
                    dve.tensor_copy(ends[:, 1, :], dst_s[:, GE - 1:GE].to_broadcast([Q, H])).then_inc(moved, 1)
                    dve.wait_ge(moved, 14)
                    for to, frm in ((pen, same), (pen_first, in_first), (pen_last, in_last)):
                        dve.tensor_scalar(to[:, :], frm[:, :], 1.0, BIG, ALU.subtract, ALU.mult).then_inc(moved, 1)
                    for n, to in enumerate((dl_t, key_t, src_t, rel_idx, w_t)):
                        dve.wait_ge(turned, n + 1)
                        dve.tensor_copy(to[:, :].rearrange("p (q j) -> p j q", j=J), ps[n][:, :, :]).then_inc(moved, 1)
                    dve.wait_ge(turned, 6)
                    dve.tensor_copy(rows[:, :, :], ps_row[:, :, 0:Q]).then_inc(moved, 1)
                    dve.memset(cont[:, :], 0.0).then_inc(moved, 1)
                    dve.memset(through[:, :], 0.0).then_inc(moved, 1)
                    dve.wait_ge(moved, 25)
                    dve.tensor_copy(src_idx[:, :], src_t[:, :]).then_inc(moved, 1)
                    dve.tensor_tensor(cont[:, 1:Q], rows[:, 0, 1:Q], rows[:, 1, 0:Q - 1], ALU.is_equal).then_inc(moved, 1)
                    dve.tensor_tensor(through[:, 1:Q + 1], rows[:, 0, :], rows[:, 1, :], ALU.is_equal).then_inc(moved, 1)
                    dve.wait_ge(turned, 7)
                    dve.tensor_reduce(wide[:, :], ps_top[:, 0:Q], AX.X, ALU.max).then_inc(moved, 1)

                @block.tensor
                def _(pe):
                    pe.wait_ge(made, 2)
                    for n, (frm, ready) in enumerate(((dl_s, 5), (key_s, 7), (src_s, 7), (idx_s, 7), (w_s, 7))):
                        pe.wait_ge(moved, ready)
                        for j in range(J):
                            turn = pe.transpose(ps[n][:, j, :], frm[:, j * P:(j + 1) * P], ident[0:Q, 0:Q])
                        turn.then_inc(turned, 1)
                    pe.wait_ge(moved, 14)
                    for n in range(2):
                        turn = pe.transpose(ps_row[:, n, 0:Q], ends[:, n, :], ident[0:Q, 0:Q])
                    turn.then_inc(turned, 1)
                    pe.transpose(ps_top[:, 0:Q], top_s[:, :], ident[0:Q, 0:Q]).then_inc(turned, 1)


    def rows_of(table, g, width):
        flat = table.rearrange("(a k) f -> a (k f)", k=K4)
        return flat[bass.ds(g * P, P), :].rearrange("p (k f) -> p k f", f=width)

    def across(vector, n, parts=P):
        return vector.rearrange("(a n) -> a n", a=1).broadcast_to([parts, n])

    def scope(ctx, tag, slots=2):
        taken = []

        def sem(name):
            taken.append(nc.alloc_semaphore(f"{tag}_{name}"))
            return taken[-1]

        def give_back():
            nc.clear_and_free_semaphores(taken)
            nc.all_engine_barrier()

        ctx.callback(give_back)
        return (lambda name, shape, dt=F32: ctx.enter_context(nc.sbuf_tensor(f"{tag}_{name}", shape, dt)),
                lambda name, shape: ctx.enter_context(nc.psum_tensor(f"{tag}_{name}", shape, F32)),
                sem,
                lambda name, n=slots: [sem(f"{name}{s}") for s in range(n)])

    def both_ways(eng, program):
        reach = nc.values_load(wide[0:1, 0:1], engines=[eng.engine], min_val=0, max_val=P - 1,
                               skip_runtime_bounds_check_because="every node has an edge of its own")
        with eng.If(reach < WIN):
            program(1)
        with eng.Else():
            program(P // WIN)

    def pipeline(eng, *stages):
        def turn(i, first=False, last=False):
            for u in range(U):
                for work, lag in stages:
                    if not (first and u < lag) and not (last and u >= lag):
                        work(U * i + (u - lag), lambda slots, n=u - lag: (n % slots, (U // slots) * i + n // slots))
        turn(0, first=True)
        with eng.Fori(1, Q // U) as i:
            turn(i)
        turn(Q // U, last=True)

    def hold(eng, semaphore, count):
        if not (isinstance(count, int) and count <= 0):
            eng.wait_ge(semaphore, count)

    def over_groups(eng, work):
        work(0, False)
        with eng.Fori(1, NGRP - 1) as g:
            work(g, False)
        work(NGRP - 1, True)

    def gathers(pool, slots, numbers, all_numbers, staged, to, table, src_in, freed):
        def gather(q, at):
            s, c = at(slots)
            for semaphore, adds in freed:
                hold(pool, semaphore[s], adds * c)
            pool.nop(nofuse=True)
            pool.tensor_copy(numbers[:, s, :], all_numbers[:, bass.ds(q * J, J)]).then_inc(staged[s], 1)
            pool.wait_ge(staged[s], c + 1)
            pool.nop(nofuse=True)
            for j in range(J):
                pool.indirect_dma_start(to[:, s, j, :], None, table,
                                        bass.IndirectOffsetOnAxis(ap=numbers[:, s, j:j + 1], axis=0)).then_inc(src_in[s], 16)
        pipeline(pool, (gather, 0))

    def rel_tables(u_keys, e_bias, agg, share):
        with ExitStack() as ctx:
            tmp, psum, sem, pair = scope(ctx, "t0")
            w_up, w_low = tmp("w_up", [P, R, D]), tmp("w_low", [P, R, D])
            b_all = tmp("b_all", [P, R * D])
            wq, wk = tmp("wq", [P, R, D]), tmp("wk", [P, R, D])
            a_all = tmp("a_all", [P, 2 * D])
            bq, bk = tmp("bq", [Q, R, D]), tmp("bk", [Q, R, D])
            ab = tmp("ab", [Q, 1])
            junk = tmp("junk", [P, 4 * R, D])
            u_part, u_col = tmp("u_part", [P, 2, R]), tmp("u_col", [P, R])
            c_part = tmp("c_part", [Q, 2, R])
            u_rows, spread = tmp("u_rows", [R, D]), tmp("spread", [R, P])
            xg, xt = tmp("xg", [P, K4, D]), tmp("xt", [P, K4, D])
            up, low = tmp("up", [P, K4, R * D]), tmp("low", [P, K4, R * D])
            ps_x, ps_u = psum("ps_x", [P, K4, D]), psum("ps_u", [P, D])
            ps_up = [psum(f"ps_up{n}", [P, R * D]) for n in range(2)]
            ps_low = [psum(f"ps_low{n}", [P, R * D]) for n in range(2)]
            weights_in, dots, u_mm, u_copied, x_in, turned, xt_ready, up_mm, low_mm, up_out, low_out, up_st, low_st, cleared = (
                sem(n) for n in ("weights_in", "dots", "u_mm", "u_copied", "x_in", "turned", "xt_ready", "up_mm", "low_mm",
                                 "up_out", "low_out", "up_st", "low_st", "cleared"))

            with nc.Block() as block:
                @block.sync
                def _(sp):
                    for to, frm in ((w_up, L0_gnn_W_R[:, 0:D, :]), (w_low, L0_gnn_W_R[:, D:2 * D, :]), (wq, L0_gnn_W_Q), (wk, L0_gnn_W_K)):
                        sp.dma_start(to[:, :, :], frm.rearrange("r f g -> f r g")).then_inc(weights_in, 16)
                    sp.dma_start(b_all[:, :], across(L0_gnn_b_R.rearrange("r f -> (r f)"), R * D)).then_inc(weights_in, 16)
                    sp.dma_start(a_all[:, :], across(L0_gnn_a_w.rearrange("f a -> (f a)"), 2 * D)).then_inc(weights_in, 16)
                    for to, frm in ((bq, L0_gnn_b_Q), (bk, L0_gnn_b_K)):
                        sp.dma_start(to[:, :, :].rearrange("q r f -> q (r f)"), across(frm.rearrange("r f -> (r f)"), R * D, Q)).then_inc(weights_in, 16)
                    sp.dma_start(ab[:, :], across(L0_gnn_a_b, 1, Q)).then_inc(weights_in, 16)
                    sp.dma_start(xg[:, :, :], rows_of(xs[0], 0, D)).then_inc(x_in, 16)

                    def store(g):
                        sp.wait_ge(up_out, 4 * (g + 1))
                        sp.dma_start(rows_of(rel_table.rearrange("(n r) f -> n (r f)", r=R), g, R * D), up[:, :, :]).then_inc(up_st, 16)
                        sp.wait_ge(low_out, 4 * (g + 1))
                        sp.dma_start(rows_of(rel_window.rearrange("(n r) f -> n (r f)", r=R), g, R * D), low[:, :, :]).then_inc(low_st, 16)

                    with sp.Fori(0, NGRP - 1) as g:
                        sp.wait_ge(turned, g + 1)
                        sp.dma_start(xg[:, :, :], rows_of(xs[0], g + 1, D)).then_inc(x_in, 16)
                        store(g)
                    store(NGRP - 1)
                    sp.wait_ge(up_st, 16 * NGRP)
                    sp.wait_ge(low_st, 16 * NGRP)

                @block.gpsimd
                def _(pool):
                    pool.memset(agg[:, :], 0.0).then_inc(cleared, 1)
                    pool.memset(share[:, :], 0.0).then_inc(cleared, 1)

                @block.tensor
                def _(pe):
                    pe.wait_ge(dots, 1)
                    pe.transpose(ps_u[0:R, :], u_col[:, :], ident[:, :]).then_inc(u_mm, 1)
                    pe.wait_ge(u_copied, 2)
                    pe.matmul(ps_u[:, :], spread[:, :], u_rows[:, :], start=True, stop=True).then_inc(u_mm, 1)
                    pe.wait_ge(weights_in, 16 * 9)
                    with pe.Fori(0, NGRP) as g:
                        pe.wait_ge(x_in, 16 * (g + 1))
                        pe.wait_ge(xt_ready, g)
                        for k in range(K4):
                            turn = pe.transpose(ps_x[:, k, :], xg[:, k, :], ident[:, :])
                        turn.then_inc(turned, 1)
                        pe.wait_ge(xt_ready, g + 1)
                        for k in range(K4):
                            pe.wait_ge(up_out, 4 * g + max(k - 1, 0))
                            pe.matmul(ps_up[k % 2][:, :], xt[:, k, :], w_up[:, :, :].rearrange("f r g -> f (r g)"), start=True, stop=True).then_inc(up_mm, 1)
                            pe.wait_ge(low_out, 4 * g + max(k - 1, 0))
                            pe.matmul(ps_low[k % 2][:, :], xt[:, k, :], w_low[:, :, :].rearrange("f r g -> f (r g)"), start=True, stop=True).then_inc(low_mm, 1)

                @block.scalar
                def _(act):
                    with act.Fori(0, NGRP) as g:
                        act.wait_ge(turned, g + 1)
                        act.wait_ge(low_mm, 4 * g)
                        act.copy(xt[:, :, :], ps_x[:, :, :]).then_inc(xt_ready, 1)
                        act.wait_ge(up_st, 16 * g)
                        for k in range(K4):
                            act.wait_ge(up_mm, 4 * g + k + 1)
                            act.copy(up[:, k, :], ps_up[k % 2][:, :]).then_inc(up_out, 1)

                @block.vector
                def _(dve):
                    dve.wait_ge(weights_in, 16 * 9)
                    for n, (w, b) in enumerate(((wq, bq), (wk, bk))):
                        for r in range(R):
                            dve.tensor_tensor_reduce(junk[:, 2 * R * n + r, :], w[:, r, :], a_all[:, n * D:(n + 1) * D], 1.0, 0.0,
                                                     ALU.mult, ALU.add, u_part[:, n, r:r + 1]).then_inc(cleared, 1)
                            dve.tensor_tensor_reduce(junk[0:Q, 2 * R * n + R + r, :], b[:, r, :], a_all[0:Q, n * D:(n + 1) * D], 1.0, 0.0,
                                                     ALU.mult, ALU.add, c_part[:, n, r:r + 1]).then_inc(cleared, 1)
                    dve.wait_ge(cleared, 2 + 4 * R)
                    dve.tensor_tensor(u_col[:, :], u_part[:, 0, :], u_part[:, 1, :], ALU.add).then_inc(dots, 1)
                    dve.tensor_tensor(e_bias[:, :], c_part[:, 0, :], c_part[:, 1, :], ALU.add).then_inc(dots, 1)
                    dve.wait_ge(dots, 2)
                    dve.tensor_scalar(e_bias[:, :], e_bias[:, :], ab[:, 0:1], None, ALU.add).then_inc(dots, 1)
                    dve.wait_ge(u_mm, 1)
                    dve.tensor_copy(u_rows[:, :], ps_u[0:R, :]).then_inc(u_copied, 1)
                    dve.tensor_copy(spread[:, :].rearrange("r (n c) -> r n c", c=R),
                                    ident[0:R, 0:R].unsqueeze(1).to_broadcast([R, WIN, R])).then_inc(u_copied, 1)
                    dve.wait_ge(u_mm, 2)
                    dve.tensor_copy(u_keys[:, :], ps_u[:, :]).then_inc(u_copied, 1)
                    with dve.Fori(0, NGRP) as g:
                        dve.wait_ge(low_st, 16 * g)
                        for k in range(K4):
                            dve.wait_ge(low_mm, 4 * g + k + 1)
                            dve.tensor_tensor(low[:, k, :], ps_low[k % 2][:, :], b_all[:, :], ALU.add).then_inc(low_out, 1)

    def rel_scores(u_keys, e_t):
        with ExitStack() as ctx:
            tmp, psum, sem, pair = scope(ctx, "e0")
            S = 4
            idx = tmp("idx", [P, S, J], I32)
            gathered, window, rel = (tmp(n, [P, S, J, D]) for n in ("gathered", "window", "rel"))
            onehot, spread = tmp("onehot", [P, 2, J, KEYS]), tmp("spread", [P, 2, J, P])
            low, junk = tmp("low", [P, 2, J, D]), tmp("junk", [P, 2, J, D])
            e_now = tmp("e_now", [P, 2, J])
            ps_t, ps_r, ps_u = ([psum(f"{n}{s}", [P, J, D]) for s in range(2)] for n in ("ps_t", "ps_r", "ps_u"))
            staged, src_in, win_in, rel_made, rel_st = (pair(n, S) for n in ("staged", "src_in", "win_in", "rel_made", "rel_st"))
            used = pair("used", S)
            marked, turned, copied, added, dotted, e_made = (pair(n) for n in ("marked", "turned", "copied", "added", "dotted", "e_made"))

            def lags(nw, narrow):
                return narrow if nw == 1 else 0

            def sync_program(sp, nw):
                def load(q, at):
                    s, c = at(S)
                    for w in range(nw):
                        hold(sp, used[s], c * nw + w)
                        sp.nop(nofuse=True)
                        for j, base in enumerate(window_bases([sp.engine], q)):
                            sp.dma_start(window[:, s, j, :], rel_window[bass.ds(base * R + w * KEYS, KEYS), :]).then_inc(win_in[s], 16)

                def store(q, at):
                    s, c = at(S)
                    sp.wait_ge(rel_made[s], c + 1)
                    sp.dma_start(rel_edges[bass.ds(q, 1), :, :].rearrange("a p f -> (a p) f"),
                                 rel[:, s, :, :].rearrange("p j f -> p (j f)")).then_inc(rel_st[s], 16)

                pipeline(sp, (load, 0), (store, lags(nw, 3)))
                for s in range(S):
                    sp.wait_ge(rel_st[s], 16 * (Q // S))

            def pe_program(pe, nw):
                def turn(q, at, w=0):
                    s, c = at(2)
                    pe.wait_ge(marked[s], c * nw + w + 1)
                    hold(pe, copied[s], c * nw + w)
                    for j in range(J):
                        mm = pe.transpose(ps_t[s][:, j, :], onehot[:, s, j, :], ident[:, :])
                    mm.then_inc(turned[s], 1)

                def expand(q, at):
                    s, c = at(2)
                    s4, c4 = at(S)
                    hold(pe, dotted[s], c)
                    for w in range(nw):
                        if w > 0:
                            turn(q, at, w)
                        pe.wait_ge(win_in[s4], 16 * J * (c4 * nw + w + 1))
                        pe.wait_ge(copied[s], c * nw + w + 1)
                        for j in range(J):
                            pe.matmul(ps_r[s][:, j, :], spread[:, s, j, :], window[:, s4, j, :], start=(w == 0 and (nw == 1 or j == 0)), stop=(w == nw - 1), skip_group_check=True)
                            mm = pe.matmul(ps_u[s][:, j, :], spread[:, s, j, :], u_keys[:, :], start=(w == 0 and (nw == 1 or j == 0)), stop=(w == nw - 1), skip_group_check=True)
                        mm.then_inc(used[s4], 1)
                pipeline(pe, (turn, 0), (expand, lags(nw, 1)))

            def act_program(act, nw):
                def copy(q, at):
                    s, c = at(2)
                    for w in range(nw):
                        act.wait_ge(turned[s], c * nw + w + 1)
                        if w > 0:
                            s4, c4 = at(S)
                            act.wait_ge(used[s4], c4 * nw + w)
                        else:
                            s4, c4 = at(S)
                            before = (s4 + 2) % S
                            hold(act, used[before], (c4 + (1 if s4 >= 2 else 0)) * nw)
                        act.copy(spread[:, s, :, :], ps_t[s][:, :, :]).then_inc(copied[s], 1)
                pipeline(act, (copy, 0))

            def dve_program(dve, nw):
                def mark(q, at):
                    s, c = at(2)
                    for w in range(nw):
                        hold(dve, turned[s], c * nw + w)
                        for j in range(J):
                            mk = dve.tensor_scalar(onehot[:, s, j, :], iota[:, w * KEYS:(w + 1) * KEYS],
                                                   key_t[:, bass.ds(q * J + j, 1)], None, ALU.is_equal)
                        mk.then_inc(marked[s], 1)

                def add(q, at):
                    s, c = at(2)
                    s4, c4 = at(S)
                    dve.wait_ge(used[s4], (c4 + 1) * nw)
                    dve.wait_ge(src_in[s4], 16 * J * (c4 + 1))
                    hold(dve, dotted[s], c)
                    dve.tensor_tensor(low[:, s, :, :], gathered[:, s4, :, :], ps_r[s][:, :, :], ALU.add).then_inc(added[s], 1)

                def score(q, at):
                    s, c = at(2)
                    s4, c4 = at(S)
                    dve.wait_ge(added[s], c + 1)
                    hold(dve, rel_st[s4], 16 * c4)
                    dve.scalar_tensor_tensor(out=rel[:, s4, :, :], in0=low[:, s, :, :], scalar=0.2, in1=low[:, s, :, :],
                                             op0=ALU.mult, op1=ALU.max).then_inc(rel_made[s4], 1)

                def dot(q, at):
                    s, c = at(2)
                    s4, c4 = at(S)
                    dve.wait_ge(rel_made[s4], c4 + 1)
                    hold(dve, e_made[s], c)
                    for j in range(J):
                        dt = dve.tensor_tensor_reduce(junk[:, s, j, :], rel[:, s4, j, :], ps_u[s][:, j, :], 1.0, 0.0, ALU.mult, ALU.add, e_now[:, s, j:j + 1])
                    dt.then_inc(dotted[s], 1)
                    dve.wait_ge(dotted[s], c + 1)
                    dve.tensor_copy(e_t[:, bass.ds(q * J, J)], e_now[:, s, :]).then_inc(e_made[s], 1)
                pipeline(dve, (mark, 0), (add, lags(nw, 2)), (score, lags(nw, 2)), (dot, lags(nw, 2)))

            with nc.Block() as block:
                @block.gpsimd
                def _(pool):
                    gathers(pool, S, idx, rel_idx, staged, gathered, rel_table, src_in, [(rel_made, 1)])

                @block.sync
                def _(sp):
                    both_ways(sp, lambda nw: sync_program(sp, nw))

                @block.tensor
                def _(pe):
                    both_ways(pe, lambda nw: pe_program(pe, nw))

                @block.scalar
                def _(act):
                    both_ways(act, lambda nw: act_program(act, nw))

                @block.vector
                def _(dve):
                    both_ways(dve, lambda nw: dve_program(dve, nw))

    def segment_totals(ctx, tag, n):
        tmp, psum, sem, pair = scope(ctx, tag)
        ends, rows = tmp("ends", [Q, 2, n]), tmp("rows", [n, 2, Q + 2])
        chain, gate, links = tmp("chain", [n, 2, Q]), tmp("gate", [n, 2, Q]), tmp("links", [n, 2, Q])
        back = tmp("back", [Q, 2, n])
        ps_rows, ps_back = psum("ps_rows", [n, 2, Q + 2]), psum("ps_back", [Q, 2, n])
        done, turned = sem("done"), sem("turned")
        mine = 2 * n + 9 + 2 * n

        def vector(dve, call, largest, values, scratch):
            at = call * mine
            for k in range(n):
                gates = pen if largest else same
                dve.tensor_tensor_scan(scratch[k], gates[:, 0:GE], values[k], -BIG if largest else 0.0,
                                       ALU.add if largest else ALU.mult, ALU.max if largest else ALU.add).then_inc(done, 1)
            for k in range(n):
                dve.wait_ge(done, at + k + 1)
                dve.tensor_tensor_scan(values[k][:, ::-1], pen[:, GE:0:-1], scratch[k][:, ::-1], -BIG, ALU.add, ALU.max).then_inc(done, 1)
            at += 2 * n
            dve.wait_ge(done, at)
            for k in range(n):
                dve.tensor_copy(ends[:, 0, k:k + 1], values[k][:, 0:1])
                last = dve.tensor_copy(ends[:, 1, k:k + 1], values[k][:, GE - 1:GE])
            last.then_inc(done, 1)
            dve.memset(rows[:, :, :], -NEG if largest else 0.0).then_inc(done, 1)
            dve.tensor_tensor(links[:, 0, :], cont[0:n, 0:Q], through[0:n, 0:Q], ALU.mult).then_inc(done, 1)
            dve.tensor_tensor(links[:, 1, :], cont[0:n, 1:Q + 1], through[0:n, 2:Q + 2], ALU.mult).then_inc(done, 1)
            dve.wait_ge(done, at + 4)
            dve.wait_ge(turned, 2 * call + 1)
            dve.tensor_copy(rows[:, :, 1:Q + 1], ps_rows[:, :, 0:Q]).then_inc(done, 1)
            dve.wait_ge(done, at + 5)
            for way, (which, other) in enumerate(((cont[0:n, 0:Q], rows[:, 1, 0:Q]), (cont[0:n, 1:Q + 1], rows[:, 0, 2:Q + 2]))):
                if largest:
                    dve.tensor_scalar(chain[:, way, :], which, 1.0, BIG, ALU.subtract, ALU.mult)
                    got = dve.tensor_scalar(gate[:, way, :], links[:, way, :], 1.0, BIG, ALU.subtract, ALU.mult)
                else:
                    dve.tensor_tensor(chain[:, way, :], which, other, ALU.mult)
                    got = dve.tensor_copy(gate[:, way, :], links[:, way, :])
            got.then_inc(done, 1)
            dve.wait_ge(done, at + 6)
            if largest:
                dve.tensor_tensor(chain[:, 0, :], chain[:, 0, :], rows[:, 1, 0:Q], ALU.add)
                dve.tensor_tensor(chain[:, 1, :], chain[:, 1, :], rows[:, 0, 2:Q + 2], ALU.add).then_inc(done, 1)
            else:
                dve.tensor_copy(rows[:, 0, 0:1], rows[:, 0, 0:1]).then_inc(done, 1)
            dve.wait_ge(done, at + 7)
            op0, op1, start = (ALU.add, ALU.max, -NEG) if largest else (ALU.mult, ALU.add, 0.0)
            dve.tensor_tensor_scan(links[:, 0, :], gate[:, 0, :], chain[:, 0, :], start, op0, op1)
            dve.tensor_tensor_scan(links[:, 1, ::-1], gate[:, 1, ::-1], chain[:, 1, ::-1], start, op0, op1).then_inc(done, 1)
            dve.wait_ge(turned, 2 * call + 2)
            dve.tensor_copy(back[:, :, :], ps_back[:, :, :]).then_inc(done, 1)
            at += 9
            dve.wait_ge(done, at)
            for way, where in enumerate((pen_first, pen_last) if largest else (in_first, in_last)):
                for k in range(n):
                    dve.wait_ge(done, at + way * n)
                    dve.scalar_tensor_tensor(out=values[k], in0=where[:, :], scalar=back[:, way, k:k + 1], in1=values[k],
                                             op0=op0, op1=op1).then_inc(done, 1)
            dve.wait_ge(done, at + 2 * n)

        def tensor(pe, call):
            pe.wait_ge(done, call * mine + 2 * n + 1)
            for way in range(2):
                mm = pe.transpose(ps_rows[:, way, 0:Q], ends[:, way, :], ident[0:Q, 0:Q])
            mm.then_inc(turned, 1)
            pe.wait_ge(done, call * mine + 2 * n + 8)
            for way in range(2):
                mm = pe.transpose(ps_back[:, way, :], links[:, way, :], ident[0:n, 0:n])
            mm.then_inc(turned, 1)

        return vector, tensor

    def rel_softmax(e_t, e_bias):
        with ExitStack() as ctx:
            tmp, psum, sem, pair = scope(ctx, "s0")
            e_s, top_s, ex, total = (tmp(n, [Q, GE]) for n in ("e_s", "top_s", "ex", "total"))
            mask, val, scratch = tmp("mask", [Q, R, GE]), tmp("val", [Q, R, GE]), tmp("scratch", [Q, R, GE])
            ps_e = psum("ps_e", [Q, J, P])
            ps_a = psum("ps_a", [P, J, Q])
            zero_x = tmp("zero_x", [P, 4 * D])
            zeroed, zeroed_sides = sem("zeroed"), sem("zeroed_sides")
            turned, step, exped = sem("turned"), sem("step"), sem("exped")
            totals_v, totals_t = segment_totals(ctx, "s0t", R)
            vals, scr = [val[:, r, :] for r in range(R)], [scratch[:, r, :] for r in range(R)]
            n_select = 2 * R

            with nc.Block() as block:
                @block.gpsimd
                def _(pool):
                    pool.memset(zero_x[:, :], 0.0).then_inc(zeroed, 1)

                @block.sync
                def _(sp):
                    sp.wait_ge(zeroed, 1)
                    n_zero = 0
                    for c in range(COPIES):
                        a = 0
                        full = (N // (4 * P)) * 4 * P
                        while a < full:
                            sp.dma_start(side[c][a:a + 4 * P, :].rearrange("(p k) f -> p (k f)", k=4), zero_x[:, :]).then_inc(zeroed_sides, 16)
                            a += 4 * P
                            n_zero += 1
                        while a < N + P:
                            n = min(P, N + P - a)
                            sp.dma_start(side[c][a:a + n, :], zero_x[0:n, 0:D]).then_inc(zeroed_sides, 16)
                            a += n
                            n_zero += 1
                    sp.wait_ge(zeroed_sides, 16 * n_zero)

                @block.tensor
                def _(pe):
                    for j in range(J):
                        mm = pe.transpose(ps_e[:, j, :], e_t[:, j::J], ident[:, :])
                    mm.then_inc(turned, 1)
                    totals_t(pe, 0)
                    totals_t(pe, 1)
                    pe.wait_ge(step, 4 + 3 * R + n_select + 2 + R + n_select + 3)
                    for j in range(J):
                        mm = pe.transpose(ps_a[:, j, :], total[:, j * P:(j + 1) * P], ident[0:Q, 0:Q])
                    mm.then_inc(turned, 1)

                @block.scalar
                def _(act):
                    act.wait_ge(step, 4 + 3 * R + n_select + 2)
                    act.activation(ex[:, :], e_s[:, :], ACT.Exp).then_inc(exped, 1)

                @block.vector
                def _(dve):
                    for r in range(R):
                        dve.tensor_scalar(mask[:, r, :], typ_s[:, :], float(r), None, ALU.is_equal).then_inc(step, 1)
                    dve.wait_ge(turned, 1)
                    dve.wait_ge(step, R)
                    dve.tensor_copy(e_s[:, :], ps_e[:, :, :].rearrange("q j e -> q (j e)")).then_inc(step, 1)
                    for r in range(R):
                        dve.wait_ge(step, R + 1 + r)
                        dve.scalar_tensor_tensor(out=e_s[:, :], in0=mask[:, r, :], scalar=e_bias[:, r:r + 1], in1=e_s[:, :],
                                                 op0=ALU.mult, op1=ALU.add).then_inc(step, 1)
                    dve.wait_ge(step, 2 * R + 1)
                    dve.scalar_tensor_tensor(out=top_s[:, :], in0=e_s[:, :], scalar=0.2, in1=e_s[:, :],
                                             op0=ALU.mult, op1=ALU.max).then_inc(step, 1)
                    dve.wait_ge(step, 2 * R + 2)
                    dve.tensor_copy(e_s[:, :], top_s[:, :]).then_inc(step, 1)
                    dve.wait_ge(step, 2 * R + 3)
                    for r in range(R):
                        dve.tensor_scalar(vals[r], mask[:, r, :], 1.0, NEG, ALU.subtract, ALU.mult)
                    dve.memset(total[:, :], 0.0).then_inc(step, 1)
                    dve.wait_ge(step, 2 * R + 4)
                    for r in range(R):
                        dve.tensor_tensor(vals[r], vals[r], e_s[:, :], ALU.add).then_inc(step, 1)
                    at = 3 * R + 4
                    dve.wait_ge(step, at)
                    totals_v(dve, 0, True, vals, scr)

                    def select(at):
                        for r in range(R):
                            dve.tensor_tensor(scr[r], mask[:, r, :], vals[r], ALU.mult).then_inc(step, 1)
                        for r in range(R):
                            dve.wait_ge(step, at + R + r)
                            dve.tensor_tensor(total[:, :], total[:, :], scr[r], ALU.add).then_inc(step, 1)
                        dve.wait_ge(step, at + 2 * R)

                    select(at)
                    at += n_select
                    dve.tensor_tensor(e_s[:, :], e_s[:, :], total[:, :], ALU.subtract).then_inc(step, 1)
                    dve.wait_ge(step, at + 1)
                    dve.memset(total[:, :], 0.0).then_inc(step, 1)
                    at += 2 + R
                    dve.wait_ge(exped, 1)
                    for r in range(R):
                        dve.tensor_tensor(vals[r], mask[:, r, :], ex[:, :], ALU.mult).then_inc(step, 1)
                    at += 0
                    dve.wait_ge(step, at)
                    totals_v(dve, 1, False, vals, scr)
                    select(at)
                    at += n_select
                    dve.tensor_scalar(total[:, :], total[:, :], 1e-16, None, ALU.max).then_inc(step, 1)
                    dve.wait_ge(step, at + 1)
                    dve.reciprocal(top_s[:, :], total[:, :]).then_inc(step, 1)
                    dve.wait_ge(step, at + 2)
                    dve.tensor_tensor(total[:, :], top_s[:, :], ex[:, :], ALU.mult).then_inc(step, 1)
                    dve.wait_ge(turned, 2)
                    dve.tensor_copy(attn_t[:, :].rearrange("p (q j) -> p j q", j=J), ps_a[:, :, :]).then_inc(step, 1)

    def rel_sums(agg, share):
        with ExitStack() as ctx:
            tmp, psum, sem, pair = scope(ctx, "g0")
            S = 4
            rel, onehot = tmp("rel", [P, S, J, D]), tmp("onehot", [P, 2, J, KEYS])
            ps_g = [psum(f"ps_g{s}", [P, J, KEYS]) for s in range(2)]
            ps_w = [psum(f"ps_w{s}", [1, J, KEYS]) for s in range(2)]
            shares = tmp("shares", [1, 2, J, KEYS])
            rel_in = pair("rel_in", S)
            marked, used, moved = (pair(n) for n in ("marked", "used", "moved"))
            added, shared = sem("added"), sem("shared")

            def sync_program(sp, nw):
                def load(q, at):
                    s, c = at(2)
                    s4, c4 = at(S)
                    if not isinstance(q, int) or q >= S:
                        sp.wait_ge(used[s], (c - 1) * nw)
                    sp.dma_start(rel[:, s4, :, :].rearrange("p j f -> p (j f)"),
                                 rel_edges[bass.ds(q, 1), :, :].rearrange("a p f -> (a p) f")).then_inc(rel_in[s4], 16)
                pipeline(sp, (load, 0))

            def pe_program(pe, nw):
                def total(q, at):
                    s, c = at(2)
                    s4, c4 = at(S)
                    pe.wait_ge(rel_in[s4], 16 * (c4 + 1))
                    for w in range(nw):
                        pe.wait_ge(marked[s], c * nw + w + 1)
                        if w > 0 or not isinstance(q, int) or q >= 2:
                            pe.wait_ge(added, J * (q * nw + w if w > 0 else (q - 1) * nw))
                            pe.wait_ge(moved[s], c * nw + w)
                        for j in range(J):
                            pe.matmul(ps_g[s][:, j, :], rel[:, s4, j, :], onehot[:, s, j, :], start=True, stop=True)
                        pe.matmul(ps_w[s][:, :, :], ones[:, 0:1], onehot[:, s, :, :], start=True, stop=True).then_inc(used[s], 1)
                pipeline(pe, (total, 0))

            def dve_program(dve, nw):
                bases = []

                def mark(q, at, w=0, tiles=range(J)):
                    s, c = at(2)
                    if tiles[0] == 0:
                        hold(dve, used[s], c * nw + w)
                    for j in tiles:
                        t = q * J + j
                        mk = dve.tensor_scalar(onehot[:, s, j, :], iota[:, w * KEYS:(w + 1) * KEYS], key_t[:, bass.ds(t, 1)],
                                               attn_t[:, bass.ds(t, 1)], ALU.is_equal, ALU.mult)
                    if tiles[-1] == J - 1:
                        mk.then_inc(marked[s], 1)

                def add(q, at, w=0, tiles=range(J)):
                    s, c = at(2)
                    if tiles[0] == 0:
                        bases[:] = window_bases([dve.engine], q)
                        dve.wait_ge(used[s], c * nw + w + 1)
                        dve.nop(nofuse=True)
                    for j in tiles:
                        base = bases[j]
                        n = (q * nw + w) * J + j
                        to = bass.ds(base * R + w * KEYS, KEYS)
                        hold(dve, added, n)
                        dve.tensor_tensor(agg[:, to], agg[:, to], ps_g[s][:, j, :], ALU.add).then_inc(added, 1)

                def both(q, at):
                    for w in range(nw):
                        mark(q, at, w)
                        add(q, at, w)
                if nw == 1:
                    pipeline(dve, *(stage for j in range(J) for stage in
                                    ((lambda q, at, j=j: add(q, at, tiles=(j,)), 2), (lambda q, at, j=j: mark(q, at, tiles=(j,)), 0))))
                else:
                    pipeline(dve, (both, 0))

            def pool_program(pool, nw):
                def add_shares(q, at):
                    s, c = at(2)
                    for w in range(nw):
                        bases = window_bases([pool.engine], q)
                        pool.wait_ge(moved[s], c * nw + w + 1)
                        pool.nop(nofuse=True)
                        for j in range(J):
                            base = bases[j]
                            n = (q * nw + w) * J + j
                            to = bass.ds(base * R + w * KEYS, KEYS)
                            hold(pool, shared, n)
                            pool.tensor_tensor(share[0:1, to], share[0:1, to], shares[:, s, j, :], ALU.add).then_inc(shared, 1)
                pipeline(pool, (add_shares, 0))

            def act_program(act, nw):
                def move(q, at):
                    s, c = at(2)
                    for w in range(nw):
                        act.wait_ge(used[s], c * nw + w + 1)
                        if w > 0:
                            act.wait_ge(shared, J * (q * nw + w))
                        elif not isinstance(q, int) or q >= 2:
                            act.wait_ge(shared, J * (q - 1) * nw)
                        act.copy(shares[:, s, :, :], ps_w[s][:, :, :]).then_inc(moved[s], 1)
                pipeline(act, (move, 0))

            with nc.Block() as block:
                @block.gpsimd
                def _(pool):
                    both_ways(pool, lambda nw: pool_program(pool, nw))

                @block.scalar
                def _(act):
                    both_ways(act, lambda nw: act_program(act, nw))

                @block.sync
                def _(sp):
                    both_ways(sp, lambda nw: sync_program(sp, nw))

                @block.tensor
                def _(pe):
                    both_ways(pe, lambda nw: pe_program(pe, nw))

                @block.vector
                def _(dve):
                    both_ways(dve, lambda nw: dve_program(dve, nw))

    def norm_stats(dve, rows, stats, mean_var, var_eps, done, at):
        for k in range(K4):
            st = dve.bn_stats(stats[:, k, :], rows[:, k, :])
        st.then_inc(done, 1)
        dve.wait_ge(done, at + 1)
        dve.nop(nofuse=True)
        for k in range(K4):
            st = dve.bn_aggr(mean_var[:, k, :], stats[:, k, :])
        st.then_inc(done, 1)
        dve.wait_ge(done, at + 2)
        dve.tensor_scalar(var_eps[:, :], mean_var[:, :, 1], EPS, None, ALU.add).then_inc(done, 1)

    def norm_apply(dve, out_rows, rows, mean_var, root, inverse, done, at):
        dve.reciprocal(inverse[:, :], root[:, :]).then_inc(done, 1)
        dve.wait_ge(done, at + 1)
        for k in range(K4):
            st = dve.tensor_scalar(out_rows[:, k, :], rows[:, k, :], mean_var[:, k, 0:1], inverse[:, k:k + 1], ALU.subtract, ALU.mult)
        st.then_inc(done, 1)

    def rel_nodes(agg, share):
        with ExitStack() as ctx:
            tmp, psum, sem, pair = scope(ctx, "n0")
            wv, bv = tmp("wv", [P, R, D]), tmp("bv", [1, R, D])
            w_src, w_dst, b1 = tmp("w_src", [P, D]), tmp("w_dst", [P, D]), tmp("b1", [P, D])
            part, part_w = tmp("part", [P, GE * R]), tmp("part_w", [1, GE * R])
            xg, low, ex, h, y, x1, xt = (tmp(n, [P, K4, D]) for n in ("xg", "low", "ex", "h", "y", "x1", "xt"))
            src_rows, dst_rows = tmp("src_rows", [P, K4, D]), tmp("dst_rows", [P, K4, D])
            stats, mean_var = tmp("stats", [P, K4, 6]), tmp("mean_var", [P, K4, 2])
            var_eps, root, inverse = (tmp(n, [P, K4]) for n in ("var_eps", "root", "inverse"))
            ps_h, ps_x, ps_s, ps_d = (psum(n, [P, K4, D]) for n in ("ps_h", "ps_x", "ps_s", "ps_d"))
            weights_in, x_in, parts, h_mm, exped, rooted, vec, turned, xt_ready, tab_mm, src_out, dst_out, x_st, stored = (sem(n) for n in
                ("weights_in", "x_in", "parts", "h_mm", "exped", "rooted", "vec", "turned", "xt_ready", "tab_mm", "src_out", "dst_out", "x_st", "stored"))
            V = 8

            with nc.Block() as block:
                @block.sync
                def _(sp):
                    sp.dma_start(wv[:, :, :], L0_gnn_W_V.rearrange("r f g -> f r g")).then_inc(weights_in, 16)
                    sp.dma_start(bv[:, :, :].rearrange("a r f -> a (r f)"), across(L0_gnn_b_V.rearrange("r f -> (r f)"), R * D, 1)).then_inc(weights_in, 16)
                    sp.dma_start(w_src[:, :], L1_gnn_W1[0:D, :]).then_inc(weights_in, 16)
                    sp.dma_start(w_dst[:, :], L1_gnn_W1[D:2 * D, :]).then_inc(weights_in, 16)
                    sp.dma_start(b1[:, :], across(L1_gnn_b1, D)).then_inc(weights_in, 16)

                    def store_rows(g):
                        sp.wait_ge(src_out, g + 1)
                        sp.dma_start(rows_of(msg_table, g, D), src_rows[:, :, :]).then_inc(stored, 16)
                        sp.wait_ge(dst_out, g + 1)
                        sp.dma_start(rows_of(msg_window, g, D), dst_rows[:, :, :]).then_inc(stored, 16)

                    def group(g, last):
                        if not last:
                            sp.wait_ge(vec, V * g + 3)
                            sp.dma_start(xg[:, :, :], rows_of(xs[0], g + 1, D)).then_inc(x_in, 16)
                        sp.wait_ge(vec, V * g + 8)
                        sp.dma_start(rows_of(xs[1], g, D), x1[:, :, :]).then_inc(x_st, 16)
                        if not isinstance(g, int) or g > 0:
                            store_rows(g - 1)
                    sp.dma_start(xg[:, :, :], rows_of(xs[0], 0, D)).then_inc(x_in, 16)
                    over_groups(sp, group)
                    store_rows(NGRP - 1)
                    sp.wait_ge(x_st, 16 * NGRP)
                    sp.wait_ge(stored, 32 * NGRP)

                @block.tensor
                def _(pe):
                    pe.wait_ge(weights_in, 16 * 5)

                    def sums(g):
                        pe.wait_ge(parts, 2 * (g + 1))
                        by_node = part[:, :].rearrange("f (n k r) -> f n k r", k=K4, r=R)
                        by_node_w = part_w[:, :].rearrange("f (n k r) -> f n k r", k=K4, r=R)
                        for k in range(K4):
                            for r in range(R):
                                pe.matmul(ps_h[:, k, :], by_node[:, :, k, r], wv[:, r, :], start=(r == 0), stop=False, skip_group_check=True)
                                mm = pe.matmul(ps_h[:, k, :], by_node_w[:, :, k, r], bv[:, r, :], start=False, stop=(r == R - 1), skip_group_check=True)
                        mm.then_inc(h_mm, 1)

                    def group(g, last):
                        if not last:
                            pe.wait_ge(vec, V * g + 2)
                            sums(g + 1)
                        pe.wait_ge(vec, V * g + 8)
                        for k in range(K4):
                            mm = pe.transpose(ps_x[:, k, :], x1[:, k, :], ident[:, :])
                        mm.then_inc(turned, 1)
                        pe.wait_ge(xt_ready, g + 1)
                        hold(pe, src_out, g)
                        hold(pe, dst_out, g)
                        for k in range(K4):
                            pe.matmul(ps_s[:, k, :], xt[:, k, :], w_src[:, :], start=True, stop=True)
                            mm = pe.matmul(ps_d[:, k, :], xt[:, k, :], w_dst[:, :], start=True, stop=True)
                        mm.then_inc(tab_mm, 1)
                    sums(0)
                    over_groups(pe, group)

                @block.scalar
                def _(act):
                    def cut(g):
                        hold(act, h_mm, g)
                        act.copy(part[:, :], agg[:, bass.ds(g * (GE * R), GE * R)]).then_inc(parts, 1)
                        act.copy(part_w[:, :], share[0:1, bass.ds(g * (GE * R), GE * R)]).then_inc(parts, 1)

                    def source_rows(g):
                        act.wait_ge(tab_mm, g + 1)
                        hold(act, stored, 32 * g)
                        act.copy(src_rows[:, :, :], ps_s[:, :, :]).then_inc(src_out, 1)

                    def group(g, last):
                        act.wait_ge(vec, V * g + 1)
                        act.activation(ex[:, :, :], low[:, :, :], ACT.Exp).then_inc(exped, 1)
                        if not isinstance(g, int) or g > 0:
                            source_rows(g - 1)
                        if not last:
                            cut(g + 1)
                        act.wait_ge(vec, V * g + 6)
                        act.activation(root[:, :], var_eps[:, :], ACT.Sqrt).then_inc(rooted, 1)
                        act.wait_ge(turned, g + 1)
                        act.copy(xt[:, :, :], ps_x[:, :, :]).then_inc(xt_ready, 1)
                    cut(0)
                    over_groups(act, group)
                    source_rows(NGRP - 1)

                @block.vector
                def _(dve):
                    dve.wait_ge(weights_in, 16 * 5)

                    def dst_side(g):
                        dve.wait_ge(tab_mm, g + 1)
                        hold(dve, stored, 32 * g)
                        dve.tensor_tensor(dst_rows[:, :, :], ps_d[:, :, :], b1[:, :].unsqueeze(1).to_broadcast([P, K4, D]), ALU.add).then_inc(dst_out, 1)

                    def group(g, last):
                        dve.wait_ge(h_mm, g + 1)
                        dve.tensor_scalar(low[:, :, :], ps_h[:, :, :], 0.0, None, ALU.min).then_inc(vec, 1)
                        dve.wait_ge(exped, g + 1)
                        dve.scalar_tensor_tensor(out=h[:, :, :], in0=ps_h[:, :, :], scalar=0.0, in1=ex[:, :, :],
                                                 op0=ALU.max, op1=ALU.add).then_inc(vec, 1)
                        dve.wait_ge(vec, V * g + 2)
                        dve.wait_ge(x_in, 16 * (g + 1))
                        dve.scalar_tensor_tensor(out=y[:, :, :], in0=h[:, :, :], scalar=-1.0, in1=xg[:, :, :],
                                                 op0=ALU.add, op1=ALU.add).then_inc(vec, 1)
                        dve.wait_ge(vec, V * g + 3)
                        norm_stats(dve, y, stats, mean_var, var_eps, vec, V * g + 3)
                        if not isinstance(g, int) or g > 0:
                            dst_side(g - 1)
                        dve.wait_ge(rooted, g + 1)
                        hold(dve, x_st, 16 * g)
                        hold(dve, turned, g)
                        norm_apply(dve, x1, y, mean_var, root, inverse, vec, V * g + 6)
                    over_groups(dve, group)
                    dst_side(NGRP - 1)

    def mark_nodes(dve, onehot, s, q, nw):
        for w in range(nw):
            mk = dve.tensor_tensor(onehot[:, s, w, :, :], iota[:, w * WIN:(w + 1) * WIN].unsqueeze(1).to_broadcast([P, J, WIN]),
                                   dl_t[:, bass.ds(q * J, J)].unsqueeze(2).to_broadcast([P, J, WIN]), ALU.is_equal)
        return mk

    def spread_nodes(act, spread, ps_t, s, nw):
        for w in range(nw):
            for j in range(J):
                cp = act.copy(spread[j * WIN:(j + 1) * WIN, s, w, j, :], ps_t[j * WIN:(j + 1) * WIN, w, :])
        return cp

    def load_windows(sp, window, s, table, q, nw, loaded):
        for j, base in enumerate(window_bases([sp.engine], q)):
            for w in range(nw):
                sp.dma_start(window[j * WIN:(j + 1) * WIN, s, w, :], table[bass.ds(base + w * WIN, WIN), :]).then_inc(loaded, 16)

    def add_windows(dve, sums, ps_a, s, q, nw, summed, count, added):
        bases = window_bases([dve.engine], q)
        dve.wait_ge(summed, count)
        dve.nop(nofuse=True)
        for j in range(J):
            for w in range(nw):
                to = bass.ds(bases[j] + w * WIN, WIN)
                hold(dve, added, q * (J * nw) + j * nw + w)
                dve.tensor_tensor(sums[:, to], sums[:, to], ps_a[s][:, w, j, :], ALU.add).then_inc(added, 1)

    def messages(agg1):
        with ExitStack() as ctx:
            tmp, psum, sem, pair = scope(ctx, "e1")
            S = 4
            NWM = P // WIN
            idx = tmp("idx", [P, S, J], I32)
            w_edge, w2 = tmp("w_edge", [P, 2, D]), tmp("w2", [P, D])
            b2 = tmp("b2", [P, J, D])
            gathered = tmp("gathered", [P, S, J, D])
            hidden, shifted, message = (tmp(n, [P, 2, J, D]) for n in ("hidden", "shifted", "message"))
            attr, attr_t = tmp("attr", [P, S, J, REL]), tmp("attr_t", [P, 2, 2, P])
            onehot, window = tmp("onehot", [P, S, NWM, J, WIN]), tmp("window", [P, S, NWM, D])
            spread = tmp("spread", [P, 2, NWM, J, P])
            ps_t, ps_e = psum("ps_t", [P, NWM, P]), psum("ps_e", [P, 2, P])
            ps_h, ps_m = ([psum(f"{n}{s}", [P, J, D]) for s in range(2)] for n in ("ps_h", "ps_m"))
            ps_a = [psum(f"ps_a{s}", [P, NWM, J, WIN]) for s in range(2)]
            cleared, weights_in, turned, copied, added, tail_in = (sem(n) for n in
                ("cleared", "weights_in", "turned", "copied", "added", "tail_in"))
            staged, src_in, win_in, attr_in, marked, h_mm = (pair(n, S) for n in ("staged", "src_in", "win_in", "attr_in", "marked", "h_mm"))
            h_out, m_mm, biased, m_out, a_mm = (pair(n) for n in ("h_out", "m_mm", "biased", "m_out", "a_mm"))
            full = (E - (Q - 1) * GE) // P
            rest = E - (Q - 1) * GE - full * P
            LOADS = Q // S

            def sync_program(sp, nw):
                sp.wait_ge(cleared, 1)
                for n in range(2):
                    sp.dma_start(w_edge[n * REL:(n + 1) * REL, n, :], L1_gnn_W1[2 * D:, :]).then_inc(weights_in, 16)
                sp.dma_start(w2[:, :], L1_gnn_W2).then_inc(weights_in, 16)
                for j in range(J):
                    sp.dma_start(b2[:, j, :], across(L1_gnn_b2, D)).then_inc(weights_in, 16)

                def load(q, s, c, last=False):
                    hold(sp, h_mm[s], c)
                    sp.nop(nofuse=True)
                    if last:
                        rows = edge_attr_64[(Q - 1) * GE:(Q - 1) * GE + full * P, :]
                        sp.dma_start(attr[0:rest, s, full, :], edge_attr_64[E - rest:E, :]).then_inc(tail_in, 16)
                        sp.wait_ge(tail_in, 16)
                        sp.dma_start(attr[:, s, 0:full, :], rows.rearrange("(j p) f -> p j f", p=P)).then_inc(attr_in[s], 16)
                    else:
                        rows = edge_attr_64[bass.ds(q * GE, GE), :]
                        sp.dma_start(attr[:, s, :, :], rows.rearrange("(j p) f -> p j f", p=P)).then_inc(attr_in[s], 16)
                    load_windows(sp, window, s, msg_window, q, nw, win_in[s])

                for u in range(U):
                    load(u, u, 0)
                with sp.Fori(1, LOADS - 1) as i:
                    for u in range(U):
                        load(U * i + u, u, i)
                for u in range(U):
                    load(Q - U + u, u, LOADS - 1, last=(u == U - 1))

            def pe_program(pe, nw):
                pe.wait_ge(weights_in, 16 * (3 + J))

                def turn(q, at):
                    s, c = at(S)
                    hold(pe, copied, 2 * q)
                    pe.wait_ge(attr_in[s], 16 * (c + 1))
                    pe.wait_ge(marked[s], c + 1)
                    for w in range(nw):
                        mm = pe.transpose(ps_t[:, w, :], onehot[:, s, w, :, :].rearrange("p j n -> p (j n)"), ident[:, :])
                    mm.then_inc(turned, 1)
                    for n in range(2):
                        mm = pe.transpose(ps_e[:, n, :], attr[:, s, 2 * n:2 * n + 2, :].rearrange("p j f -> p (j f)"), ident[:, :])
                    mm.then_inc(turned, 1)

                def hide(q, at):
                    s, c = at(S)
                    s2, c2 = at(2)
                    pe.wait_ge(win_in[s], 16 * J * nw * (c + 1))
                    pe.wait_ge(copied, 2 * (q + 1))
                    hold(pe, h_out[s2], c2)
                    pe.wait_ge(src_in[s], 16 * J * (c + 1))
                    for w in range(nw):
                        pe.matmul(ps_h[s2][:, :, :], window[:, s, w, :], spread[:, s2, w, :, :], start=(w == 0), stop=False, skip_group_check=True)
                    for j in range(J):
                        pe.matmul(ps_h[s2][:, j, :], w_edge[:, j % 2, :], attr_t[:, s2, j // 2, :], start=False, stop=False, skip_group_check=True)
                        mm = pe.matmul(ps_h[s2][:, j, :], gathered[:, s, j, :], ident[:, :], start=False, stop=True, skip_group_check=True)
                    mm.then_inc(h_mm[s], 1)

                def send(q, at):
                    s, c = at(2)
                    pe.wait_ge(h_out[s], c + 1)
                    hold(pe, biased[s], c)
                    for j in range(J):
                        mm = pe.matmul(ps_m[s][:, j, :], hidden[:, s, j, :], w2[:, :], start=True, stop=True)
                    mm.then_inc(m_mm[s], 1)

                def collect(q, at):
                    s, c = at(2)
                    s4, c4 = at(S)
                    pe.wait_ge(m_out[s], c + 1)
                    hold(pe, added, J * nw * (q - 1) if not isinstance(q, int) or q >= 2 else 0)
                    for w in range(nw):
                        for j in range(J):
                            mm = pe.matmul(ps_a[s][:, w, j, :], message[:, s, j, :], onehot[:, s4, w, j, :], start=True, stop=True)
                    mm.then_inc(a_mm[s], 1)
                pipeline(pe, (hide, 1), (turn, 0), (send, 2), (collect, 3))

            def act_program(act, nw):
                act.wait_ge(cleared, 2)

                def copy(q, at):
                    s, c = at(2)
                    if not isinstance(q, int) or q >= 2:
                        s4, c4 = at(S)
                        act.wait_ge(h_mm[(s4 + 2) % S], c4 + (1 if s4 >= 2 else 0))
                    act.wait_ge(turned, 2 * q + 1)
                    spread_nodes(act, spread, ps_t, s, nw).then_inc(copied, 1)
                    act.wait_ge(turned, 2 * q + 2)
                    act.copy(attr_t[:, s, :, :], ps_e[:, :, :]).then_inc(copied, 1)

                def hide(q, at):
                    s, c = at(2)
                    s4, c4 = at(S)
                    act.wait_ge(h_mm[s4], c4 + 1)
                    hold(act, m_mm[s], c)
                    act.activation(hidden[:, s, :, :], ps_h[s][:, :, :], ACT.Relu).then_inc(h_out[s], 1)

                def send(q, at):
                    s, c = at(2)
                    act.wait_ge(biased[s], c + 1)
                    hold(act, a_mm[s], c)
                    act.activation(message[:, s, :, :], shifted[:, s, :, :], ACT.Relu).then_inc(m_out[s], 1)
                pipeline(act, (hide, 1), (copy, 0), (send, 2))

            def dve_program(dve, nw):
                dve.memset(w_edge[:, :, :], 0.0).then_inc(cleared, 1)
                dve.memset(spread[:, :, :, :, :], 0.0).then_inc(cleared, 1)
                dve.memset(agg1[:, :], 0.0).then_inc(cleared, 1)
                dve.wait_ge(cleared, 3)
                dve.wait_ge(weights_in, 16 * (3 + J))

                def mark(q, at):
                    s, c = at(S)
                    s2, c2 = at(2)
                    hold(dve, a_mm[s2], c2 - 1 if not isinstance(c2, int) or c2 > 1 else 0)
                    mark_nodes(dve, onehot, s, q, nw).then_inc(marked[s], 1)

                def bias(q, at):
                    s, c = at(2)
                    dve.wait_ge(m_mm[s], c + 1)
                    hold(dve, m_out[s], c)
                    dve.tensor_tensor(shifted[:, s, :, :], ps_m[s][:, :, :], b2[:, :, :], ALU.add).then_inc(biased[s], 1)

                def add(q, at):
                    s, c = at(2)
                    add_windows(dve, agg1, ps_a, s, q, nw, a_mm[s], c + 1, added)
                pipeline(dve, (mark, 0), (add, 4), (bias, 2))

            with nc.Block() as block:
                @block.gpsimd
                def _(pool):
                    gathers(pool, S, idx, src_idx, staged, gathered, msg_table, src_in, [(h_mm, 1)])

                @block.sync
                def _(sp):
                    both_ways(sp, lambda nw: sync_program(sp, nw))

                @block.tensor
                def _(pe):
                    both_ways(pe, lambda nw: pe_program(pe, nw))

                @block.scalar
                def _(act):
                    both_ways(act, lambda nw: act_program(act, nw))

                @block.vector
                def _(dve):
                    both_ways(dve, lambda nw: dve_program(dve, nw))

    def message_nodes(agg1):
        with ExitStack() as ctx:
            tmp, psum, sem, pair = scope(ctx, "n1")
            C = 3 * D
            wn, bn, gamma, beta = tmp("wn", [P, D]), tmp("bn", [P, D]), tmp("gamma", [P, D]), tmp("beta", [P, D])
            wk, wv, wkt = tmp("wk", [P, NT, D]), tmp("wv", [P, NT, D]), tmp("wkt", [P, 2, NT, D])
            w_all = tmp("w_all", [P, NT, C])
            att, msg, pri = tmp("att", [P, H, DH]), tmp("msg", [P, H, DH]), tmp("pri", [P, H])
            types, mask = tmp("types", [P, NGRP, K4], I32), tmp("mask", [P, NT, NGRP * K4])
            part = tmp("part", [P, GE])
            xg, r1, y, z, v, x2 = (tmp(n, [P, K4, D]) for n in ("xg", "r1", "y", "z", "v", "x2"))
            masked, xt = tmp("masked", [P, NT, K4, D]), tmp("xt", [P, NT, K4, D])
            rows = tmp("rows", [P, K4, C])
            stats, mean_var = tmp("stats", [P, K4, 6]), tmp("mean_var", [P, K4, 2])
            var_eps, root, inverse = (tmp(n, [P, K4]) for n in ("var_eps", "root", "inverse"))
            ps_h = psum("ps_h", [P, K4, D])
            ps_x = [psum(f"ps_x{n}", [P, K4, D]) for n in range(NT)]
            ps_r = [psum(f"ps_r{k}", [P, 512]) for k in range(K4)]
            weights_in, x_in, parts, h_mm, rooted, vec, turned, xt_ready, tab_mm, rows_out, x_st, stored, ready, w_mm, w_out = (sem(n) for n in
                ("weights_in", "x_in", "parts", "h_mm", "rooted", "vec", "turned", "xt_ready", "tab_mm", "rows_out", "x_st", "stored", "ready", "w_mm", "w_out"))
            V = 17

            with nc.Block() as block:
                @block.gpsimd
                def _(pool):
                    pool.memset(att[:, :, :], 0.0).then_inc(ready, 1)
                    pool.memset(msg[:, :, :], 0.0).then_inc(ready, 1)

                @block.sync
                def _(sp):
                    sp.dma_start(wn[:, :], L1_gnn_Wn).then_inc(weights_in, 16)
                    for to, frm in ((bn, L1_gnn_bn), (gamma, L1_gnn_gamma), (beta, L1_gnn_beta)):
                        sp.dma_start(to[:, :], across(frm, D)).then_inc(weights_in, 16)
                    sp.dma_start(wk[:, :, :], L2_gnn_Wk.rearrange("t f c -> f t c")).then_inc(weights_in, 16)
                    sp.dma_start(wv[:, :, :], L2_gnn_Wv.rearrange("t f c -> f t c")).then_inc(weights_in, 16)
                    sp.dma_start(w_all[:, :, 2 * D:3 * D], L2_gnn_Wq.rearrange("t f c -> f t c")).then_inc(weights_in, 16)
                    sp.dma_start(pri[:, :], across(L2_gnn_rel_pri, H)).then_inc(weights_in, 16)
                    sp.dma_start(types[:, :, :], type_pad.rearrange("(g p k) -> p g k", p=P, k=K4)).then_inc(weights_in, 16)
                    sp.wait_ge(ready, 2)
                    for h in range(H):
                        sp.dma_start(att[h * DH:(h + 1) * DH, h, :], L2_gnn_rel_att[h, :, :]).then_inc(weights_in, 16)
                        sp.dma_start(msg[h * DH:(h + 1) * DH, h, :], L2_gnn_rel_msg[h, :, :]).then_inc(weights_in, 16)

                    def store_rows(g):
                        sp.wait_ge(rows_out, K4 * (g + 1))
                        sp.dma_start(rows_of(kv_table, g, 2 * D), rows[:, :, 0:2 * D]).then_inc(stored, 16)
                        sp.dma_start(rows_of(q_window, g, D), rows[:, :, 2 * D:3 * D]).then_inc(stored, 16)

                    def group(g, last):
                        if not last:
                            sp.wait_ge(vec, 7 + V * g + 11)
                            sp.dma_start(xg[:, :, :], rows_of(xs[1], g + 1, D)).then_inc(x_in, 16)
                        sp.wait_ge(vec, 7 + V * g + 16)
                        sp.dma_start(rows_of(xs[2], g, D), x2[:, :, :]).then_inc(x_st, 16)
                        if not isinstance(g, int) or g > 0:
                            store_rows(g - 1)
                    sp.dma_start(xg[:, :, :], rows_of(xs[1], 0, D)).then_inc(x_in, 16)
                    over_groups(sp, group)
                    store_rows(NGRP - 1)
                    sp.wait_ge(x_st, 16 * NGRP)
                    sp.wait_ge(stored, 32 * NGRP)

                @block.tensor
                def _(pe):
                    pe.wait_ge(weights_in, 16 * (9 + 2 * H))
                    for n, w in enumerate((wk, wv)):
                        for t in range(NT):
                            mm = pe.transpose(ps_x[n][:, t, :], w[:, t, :], ident[:, :])
                        mm.then_inc(w_mm, 1)
                    pe.wait_ge(w_out, 2)
                    pe.wait_ge(vec, 1)
                    for t in range(NT):
                        pe.matmul(ps_r[t][:, 0:D], wkt[:, 0, t, :], att[:, :, :].rearrange("c h o -> c (h o)"), start=True, stop=True)
                        mm = pe.matmul(ps_r[t][:, D:2 * D], wkt[:, 1, t, :], msg[:, :, :].rearrange("c h o -> c (h o)"), start=True, stop=True)
                    mm.then_inc(w_mm, 1)
                    pe.wait_ge(w_out, 3)

                    def hidden(g):
                        pe.wait_ge(parts, g + 1)
                        for k in range(K4):
                            mm = pe.matmul(ps_h[:, k, :], part[:, k::K4], wn[:, :], start=True, stop=True)
                        mm.then_inc(h_mm, 1)

                    def group(g, last):
                        if not last:
                            pe.wait_ge(vec, 7 + V * g + 1)
                            hidden(g + 1)
                        pe.wait_ge(vec, 7 + V * g + 17)
                        for t in range(NT):
                            for k in range(K4):
                                mm = pe.transpose(ps_x[t][:, k, :], masked[:, t, k, :], ident[:, :])
                            mm.then_inc(turned, 1)
                        pe.wait_ge(xt_ready, NT * (g + 1))
                        hold(pe, rows_out, K4 * g)
                        for k in range(K4):
                            for t in range(NT):
                                mm = pe.matmul(ps_r[k][:, 0:C], xt[:, t, k, :], w_all[:, t, :], start=(t == 0), stop=(t == NT - 1))
                            mm.then_inc(tab_mm, 1)
                    hidden(0)
                    over_groups(pe, group)

                @block.scalar
                def _(act):
                    for n in range(2):
                        act.wait_ge(w_mm, n + 1)
                        act.copy(wkt[:, n, :, :], ps_x[n][:, 0:NT, :]).then_inc(w_out, 1)
                    act.wait_ge(w_mm, 3)
                    act.wait_ge(weights_in, 16 * (9 + 2 * H))
                    for t in range(NT):
                        cp = act.copy(w_all[:, t, 0:2 * D], ps_r[t][:, 0:2 * D])
                    cp.then_inc(w_out, 1)

                    def cut(g):
                        hold(act, h_mm, g)
                        act.copy(part[:, :], agg1[:, bass.ds(g * GE, GE)]).then_inc(parts, 1)

                    def table_rows(g):
                        hold(act, stored, 32 * g)
                        for k in range(K4):
                            act.wait_ge(tab_mm, K4 * g + k + 1)
                            act.copy(rows[:, k, :], ps_r[k][:, 0:C]).then_inc(rows_out, 1)

                    def group(g, last):
                        if not last:
                            cut(g + 1)
                        act.wait_ge(vec, 7 + V * g + 6)
                        act.activation(root[:, :], var_eps[:, :], ACT.Sqrt).then_inc(rooted, 1)
                        if not isinstance(g, int) or g > 0:
                            table_rows(g - 1)
                        act.wait_ge(vec, 7 + V * g + 14)
                        act.activation(root[:, :], var_eps[:, :], ACT.Sqrt).then_inc(rooted, 1)
                        for t in range(NT):
                            act.wait_ge(turned, NT * g + t + 1)
                            act.copy(xt[:, t, :, :], ps_x[t][:, :, :]).then_inc(xt_ready, 1)
                    cut(0)
                    over_groups(act, group)
                    table_rows(NGRP - 1)

                @block.vector
                def _(dve):
                    dve.wait_ge(weights_in, 16 * (9 + 2 * H))
                    dve.tensor_scalar(pri[:, :], pri[:, :], DH ** -0.5, None, ALU.mult).then_inc(ready, 1)
                    dve.wait_ge(ready, 3)
                    dve.tensor_tensor(att[:, :, :], att[:, :, :], pri[:, :].unsqueeze(2).to_broadcast([P, H, DH]), ALU.mult).then_inc(vec, 1)
                    for t in range(NT):
                        dve.tensor_scalar(mask[:, t, :], types[:, :, :].rearrange("p g k -> p (g k)"), float(t), None, ALU.is_equal).then_inc(vec, 2)
                    dve.wait_ge(vec, 7)
                    wide_b = lambda a: a[:, :].unsqueeze(1).to_broadcast([P, K4, D])

                    def group(g, last):
                        at = 7 + V * g
                        dve.wait_ge(h_mm, g + 1)
                        dve.tensor_tensor(r1[:, :, :], ps_h[:, :, :], wide_b(bn), ALU.add).then_inc(vec, 1)
                        dve.wait_ge(vec, at + 1)
                        dve.wait_ge(x_in, 16 * (g + 1))
                        dve.scalar_tensor_tensor(out=y[:, :, :], in0=r1[:, :, :], scalar=0.0, in1=xg[:, :, :],
                                                 op0=ALU.max, op1=ALU.add).then_inc(vec, 2)
                        dve.wait_ge(vec, at + 3)
                        norm_stats(dve, y, stats, mean_var, var_eps, vec, at + 3)
                        dve.wait_ge(rooted, 2 * g + 1)
                        norm_apply(dve, z, y, mean_var, root, inverse, vec, at + 6)
                        dve.wait_ge(vec, at + 8)
                        dve.tensor_tensor(v[:, :, :], z[:, :, :], wide_b(gamma), ALU.mult).then_inc(vec, 1)
                        dve.wait_ge(vec, at + 9)
                        dve.tensor_tensor(z[:, :, :], v[:, :, :], wide_b(beta), ALU.add).then_inc(vec, 1)
                        dve.wait_ge(vec, at + 10)
                        dve.tensor_tensor(y[:, :, :], z[:, :, :], xg[:, :, :], ALU.add).then_inc(vec, 1)
                        dve.wait_ge(vec, at + 11)
                        norm_stats(dve, y, stats, mean_var, var_eps, vec, at + 11)
                        dve.wait_ge(rooted, 2 * g + 2)
                        hold(dve, x_st, 16 * g)
                        norm_apply(dve, x2, y, mean_var, root, inverse, vec, at + 14)
                        dve.wait_ge(vec, at + 16)
                        hold(dve, turned, NT * g)
                        for t in range(NT):
                            for k in range(K4):
                                mk = dve.tensor_scalar(masked[:, t, k, :], x2[:, k, :], mask[:, t, bass.ds(g * K4 + k, 1)], None, ALU.mult)
                        mk.then_inc(vec, 1)
                    over_groups(dve, group)

    def head_scores(a_t):
        with ExitStack() as ctx:
            tmp, psum, sem, pair = scope(ctx, "e2")
            NWM = P // WIN
            S = 4
            idx = tmp("idx", [P, S, J], I32)
            gathered = tmp("gathered", [P, S, J, 2 * D])
            product = tmp("product", [P, J, D])
            onehot = tmp("onehot", [P, 2, NWM, J, WIN])
            spread, window = tmp("spread", [P, 2, NWM, J, P]), tmp("window", [P, S, NWM, D])
            ps_t = [psum(f"ps_t{s}", [P, NWM, P]) for s in range(2)]
            ps_q = [psum(f"ps_q{s}", [P, J, D]) for s in range(2)]
            cleared = sem("cleared")
            staged, src_in, win_in, q_mm, multiplied, v_st = (pair(n, S) for n in ("staged", "src_in", "win_in", "q_mm", "multiplied", "v_st"))
            marked, turned, copied, reduced = (pair(n) for n in ("marked", "turned", "copied", "reduced"))

            def sync_program(sp, nw):
                def store(q, at):
                    s, c = at(S)
                    sp.wait_ge(src_in[s], 16 * J * (c + 1))
                    sp.dma_start(v_edges[bass.ds(q, 1), :, :].rearrange("a p (j f) -> (a p) j f", f=D), gathered[:, s, :, D:2 * D]).then_inc(v_st[s], 16)

                def load(q, at):
                    s, c = at(S)
                    hold(sp, q_mm[s], c)
                    sp.nop(nofuse=True)
                    load_windows(sp, window, s, q_window, q, nw, win_in[s])
                pipeline(sp, (load, 0), (store, 2))
                for s in range(S):
                    sp.wait_ge(v_st[s], 16 * (Q // S))

            def pe_program(pe, nw):
                def expand(q, at):
                    s, c = at(2)
                    s4, c4 = at(S)
                    pe.wait_ge(win_in[s4], 16 * J * nw * (c4 + 1))
                    pe.wait_ge(copied[s], c + 1)
                    before = (s4 + 2) % S
                    hold(pe, multiplied[before], c4 + (1 if s4 >= 2 else 0))
                    for j in range(J):
                        for w in range(nw):
                            mm = pe.matmul(ps_q[s][:, j, :], spread[:, s, w, j, :], window[:, s4, w, :], start=(w == 0), stop=(w == nw - 1))
                    mm.then_inc(q_mm[s4], 1)

                def turn(q, at):
                    s, c = at(2)
                    pe.wait_ge(marked[s], c + 1)
                    hold(pe, copied[s], c)
                    for w in range(nw):
                        mm = pe.transpose(ps_t[s][:, w, :], onehot[:, s, w, :, :].rearrange("p j n -> p (j n)"), ident[:, :])
                    mm.then_inc(turned[s], 1)
                pipeline(pe, (turn, 0), (expand, 1))

            def act_program(act, nw):
                act.wait_ge(cleared, 1)

                def copy(q, at):
                    s, c = at(2)
                    s4, c4 = at(S)
                    act.wait_ge(turned[s], c + 1)
                    before = (s4 + 2) % S
                    hold(act, q_mm[before], c4 + (1 if s4 >= 2 else 0))
                    spread_nodes(act, spread, ps_t[s], s, nw).then_inc(copied[s], 1)
                pipeline(act, (copy, 0))

            def dve_program(dve, nw):
                dve.memset(spread[:, :, :, :, :], 0.0).then_inc(cleared, 1)

                def mark(q, at):
                    s, c = at(2)
                    hold(dve, turned[s], c)
                    mark_nodes(dve, onehot, s, q, nw).then_inc(marked[s], 1)

                def score(q, at):
                    s, c = at(2)
                    s4, c4 = at(S)
                    dve.wait_ge(q_mm[s4], c4 + 1)
                    dve.wait_ge(src_in[s4], 16 * J * (c4 + 1))
                    hold(dve, reduced[1 - s], c + s)
                    dve.tensor_tensor(product[:, :, :], gathered[:, s4, :, 0:D], ps_q[s][:, :, :], ALU.mult).then_inc(multiplied[s4], 1)
                    dve.wait_ge(multiplied[s4], c4 + 1)
                    dve.tensor_reduce(a_t[:, bass.ds(q * (J * H), J * H)], product[:, :, :].rearrange("p j (h o) -> p (j h) o", o=DH),
                                      AX.X, ALU.add).then_inc(reduced[s], 1)

                pipeline(dve, (mark, 0), (score, 2))

            with nc.Block() as block:
                @block.gpsimd
                def _(pool):
                    gathers(pool, S, idx, src_idx, staged, gathered, kv_table, src_in, [(multiplied, 1), (v_st, 16)])

                @block.sync
                def _(sp):
                    both_ways(sp, lambda nw: sync_program(sp, nw))

                @block.tensor
                def _(pe):
                    both_ways(pe, lambda nw: pe_program(pe, nw))

                @block.scalar
                def _(act):
                    both_ways(act, lambda nw: act_program(act, nw))

                @block.vector
                def _(dve):
                    both_ways(dve, lambda nw: dve_program(dve, nw))

    def head_softmax(a_t):
        with ExitStack() as ctx:
            tmp, psum, sem, pair = scope(ctx, "s2")
            val, ex, scratch = (tmp(n, [Q, H, GE]) for n in ("val", "ex", "scratch"))
            ps_s = [psum(f"ps_s{n}", [Q, J, P]) for n in range(2)]
            ps_b = [psum(f"ps_b{n}", [P, J, Q]) for n in range(2)]
            turned, moved, step, exped, back, placed = (sem(n) for n in ("turned", "moved", "step", "exped", "back", "placed"))
            totals_v, totals_t = segment_totals(ctx, "s2t", H)
            heads = lambda a: [a[:, h, :] for h in range(H)]
            scores = a_t[:, :].rearrange("p (q j h) -> p q j h", j=J, h=H)

            with nc.Block() as block:
                @block.tensor
                def _(pe):
                    for h in range(H):
                        if h >= 2:
                            pe.wait_ge(moved, h - 1)
                        for j in range(J):
                            mm = pe.transpose(ps_s[h % 2][:, j, :], scores[:, :, j, h], ident[:, :])
                        mm.then_inc(turned, 1)
                    totals_t(pe, 0)
                    totals_t(pe, 1)
                    for h in range(H):
                        pe.wait_ge(step, 2 * H + h + 1)
                        if h >= 2:
                            pe.wait_ge(placed, 2 * H + h - 1)
                        for j in range(J):
                            mm = pe.transpose(ps_b[h % 2][:, j, :], val[:, h, j * P:(j + 1) * P], ident[0:Q, 0:Q])
                        mm.then_inc(back, 1)

                @block.scalar
                def _(act):
                    for h in range(H):
                        act.wait_ge(turned, h + 1)
                        act.copy(ex[:, h, :], ps_s[h % 2][:, :, :].rearrange("q j e -> q (j e)")).then_inc(moved, 1)
                    for h in range(H):
                        act.wait_ge(step, H + h + 1)
                        act.activation(ex[:, h, :], ex[:, h, :], ACT.Exp).then_inc(exped, 1)

                @block.vector
                def _(dve):
                    for h in range(H):
                        dve.wait_ge(moved, h + 1)
                        dve.tensor_copy(val[:, h, :], ex[:, h, :]).then_inc(step, 1)
                    dve.wait_ge(step, H)
                    totals_v(dve, 0, True, heads(val), heads(scratch))
                    for h in range(H):
                        dve.tensor_tensor(ex[:, h, :], ex[:, h, :], val[:, h, :], ALU.subtract).then_inc(step, 1)
                    dve.wait_ge(exped, H)
                    for h in range(H):
                        cp = dve.tensor_copy(val[:, h, :], ex[:, h, :]).then_inc(placed, 1)
                    dve.wait_ge(placed, H)
                    totals_v(dve, 1, False, heads(val), heads(scratch))
                    for h in range(H):
                        dve.reciprocal(scratch[:, h, :], val[:, h, :]).then_inc(placed, 1)
                    for h in range(H):
                        dve.wait_ge(placed, H + h + 1)
                        dve.tensor_tensor(val[:, h, :], ex[:, h, :], scratch[:, h, :], ALU.mult).then_inc(step, 1)
                    for h in range(H):
                        dve.wait_ge(back, h + 1)
                        dve.tensor_copy(scores[:, :, :, h].rearrange("p q j -> p j q"), ps_b[h % 2][:, :, :]).then_inc(placed, 1)

    def head_sums(a_t, agg2):
        with ExitStack() as ctx:
            tmp, psum, sem, pair = scope(ctx, "g2")
            NWM = P // WIN
            S = 4
            v, weighted = tmp("v", [P, S, J, D]), tmp("weighted", [P, 2, J, D])
            onehot = tmp("onehot", [P, 2, NWM, J, WIN])
            ps_a = [psum(f"ps_a{s}", [P, NWM, J, WIN]) for s in range(2)]
            cleared, added = sem("cleared"), sem("added")
            v_in, made, a_mm = pair("v_in", S), pair("made", S), pair("a_mm")

            def pe_program(pe, nw):
                def total(q, at):
                    s, c = at(2)
                    s4, c4 = at(S)
                    pe.wait_ge(made[s4], c4 + 1)
                    if not isinstance(q, int) or q >= 2:
                        pe.wait_ge(added, J * nw * (q - 1))
                    for w in range(nw):
                        for j in range(J):
                            mm = pe.matmul(ps_a[s][:, w, j, :], weighted[:, s, j, :], onehot[:, s, w, j, :], start=True, stop=True)
                    mm.then_inc(a_mm[s], 1)
                pipeline(pe, (total, 0))

            def dve_program(dve, nw):
                dve.memset(agg2[:, :], 0.0).then_inc(cleared, 1)
                dve.wait_ge(cleared, 1)

                def add(q, at):
                    s, c = at(2)
                    add_windows(dve, agg2, ps_a, s, q, nw, a_mm[s], c + 1, added)

                def weigh(q, at):
                    s, c = at(2)
                    s4, c4 = at(S)
                    hold(dve, a_mm[s], c)
                    dve.wait_ge(v_in[s4], 16 * (c4 + 1))
                    mark_nodes(dve, onehot, s, q, nw)
                    dve.tensor_tensor(weighted[:, s, :, :].rearrange("p j (h o) -> p (j h) o", o=DH),
                                      v[:, s4, :, :].rearrange("p j (h o) -> p (j h) o", o=DH),
                                      a_t[:, bass.ds(q * (J * H), J * H)].unsqueeze(2).to_broadcast([P, J * H, DH]), ALU.mult).then_inc(made[s4], 1)
                pipeline(dve, (weigh, 0), (add, 2))

            with nc.Block() as block:
                @block.sync
                def _(sp):
                    def load(q, at):
                        s, c = at(S)
                        hold(sp, made[s], c)
                        sp.dma_start(v[:, s, :, :].rearrange("p j f -> p (j f)"),
                                     v_edges[bass.ds(q, 1), :, :].rearrange("a p f -> (a p) f")).then_inc(v_in[s], 16)
                    pipeline(sp, (load, 0))

                @block.tensor
                def _(pe):
                    both_ways(pe, lambda nw: pe_program(pe, nw))

                @block.vector
                def _(dve):
                    both_ways(dve, lambda nw: dve_program(dve, nw))

    def head_nodes(agg2):
        with ExitStack() as ctx:
            tmp, psum, sem, pair = scope(ctx, "n2")
            wa = tmp("wa", [P, NT, D])
            ln_g, ln_b, film_b, film = tmp("ln_g", [P, D]), tmp("ln_b", [P, D]), tmp("film_b", [P, 2 * D]), tmp("film", [P, 2 * D])
            film_w, context, context_all = tmp("film_w", [CTX, 2 * D]), tmp("context", [CTX, 1]), tmp("context_all", [CTX, P])
            skip, alpha = tmp("skip", [P, NT]), tmp("alpha", [P, NT])
            types, mask = tmp("types", [P, NGRP, K4], I32), tmp("mask", [P, NT, NGRP * K4])
            keep = tmp("keep", [P, NGRP * K4])
            part = tmp("part", [P, GE])
            xg, y, z, v, x3 = (tmp(n, [P, K4, D]) for n in ("xg", "y", "z", "v", "x3"))
            stats, mean_var = tmp("stats", [P, K4, 6]), tmp("mean_var", [P, K4, 2])
            var_eps, root, inverse = (tmp(n, [P, K4]) for n in ("var_eps", "root", "inverse"))
            ps_h = [psum(f"ps_h{k}", [P, 512]) for k in range(K4)]
            ps_f = psum("ps_f", [P, 2 * D])
            weights_in, x_in, parts, h_mm, rooted, vec, pre, stored, film_mm, sig = (sem(n) for n in
                ("weights_in", "x_in", "parts", "h_mm", "rooted", "vec", "pre", "stored", "film_mm", "sig"))
            V = 20
            n_pre = 1 + NT + NT + 2 + NT

            with nc.Block() as block:
                @block.sync
                def _(sp):
                    sp.dma_start(wa[:, :, :], L2_gnn_Wa.rearrange("t f c -> f t c")).then_inc(weights_in, 16)
                    for to, frm, n in ((ln_g, L2_gnn_ln_g, D), (ln_b, L2_gnn_ln_b, D), (film_b, L2_gnn_film_b, 2 * D), (skip, L2_gnn_skip, NT)):
                        sp.dma_start(to[:, :], across(frm, n)).then_inc(weights_in, 16)
                    sp.dma_start(film_w[:, :], L2_gnn_film_w).then_inc(weights_in, 16)
                    sp.dma_start(context[:, :], L2_gnn_global_context.rearrange("(c a) -> c a", a=1)).then_inc(weights_in, 16)
                    sp.dma_start(types[:, :, :], type_pad.rearrange("(g p k) -> p g k", p=P, k=K4)).then_inc(weights_in, 16)

                    def group(g, last):
                        if not last:
                            sp.wait_ge(vec, V * g + 15)
                            sp.dma_start(xg[:, :, :], rows_of(xs[2], g + 1, D)).then_inc(x_in, 16)
                        sp.wait_ge(vec, V * g + V)
                        sp.dma_start(rows_of(xs[3], g, D), x3[:, :, :]).then_inc(stored, 16)
                    sp.dma_start(xg[:, :, :], rows_of(xs[2], 0, D)).then_inc(x_in, 16)
                    over_groups(sp, group)
                    sp.wait_ge(stored, 16 * NGRP)

                @block.tensor
                def _(pe):
                    pe.wait_ge(weights_in, 16 * 8)
                    pe.wait_ge(pre, 1)
                    pe.matmul(ps_f[:, :], context_all[:, :], film_w[:, :], start=True, stop=True).then_inc(film_mm, 1)

                    def hidden(g):
                        pe.wait_ge(parts, g + 1)
                        for k in range(K4):
                            mm = pe.matmul(ps_h[k][:, 0:NT * D], part[:, k::K4], wa[:, :, :].rearrange("f t c -> f (t c)"), start=True, stop=True)
                        mm.then_inc(h_mm, 1)

                    def group(g, last):
                        if not last:
                            pe.wait_ge(vec, V * g + 4)
                            hidden(g + 1)
                    hidden(0)
                    over_groups(pe, group)

                @block.scalar
                def _(act):
                    act.wait_ge(weights_in, 16 * 8)
                    act.activation(alpha[:, :], skip[:, :], ACT.Sigmoid).then_inc(sig, 1)

                    def cut(g):
                        hold(act, h_mm, g)
                        act.copy(part[:, :], agg2[:, bass.ds(g * GE, GE)]).then_inc(parts, 1)

                    def group(g, last):
                        if not last:
                            cut(g + 1)
                        act.wait_ge(vec, V * g + 7)
                        act.activation(root[:, :], var_eps[:, :], ACT.Sqrt).then_inc(rooted, 1)
                        act.wait_ge(vec, V * g + 18)
                        act.activation(root[:, :], var_eps[:, :], ACT.Sqrt).then_inc(rooted, 1)
                    cut(0)
                    over_groups(act, group)

                @block.vector
                def _(dve):
                    dve.wait_ge(weights_in, 16 * 8)
                    dve.tensor_copy(context_all[:, :], context[:, 0:1].to_broadcast([CTX, P])).then_inc(pre, 1)
                    for t in range(NT):
                        dve.tensor_scalar(mask[:, t, :], types[:, :, :].rearrange("p g k -> p (g k)"), float(t), None, ALU.is_equal).then_inc(pre, 1)
                    dve.wait_ge(pre, 1 + NT)
                    dve.wait_ge(sig, 1)
                    for t in range(NT):
                        dve.tensor_scalar(mask[:, t, :], mask[:, t, :], alpha[:, t:t + 1], None, ALU.mult).then_inc(pre, 1)
                    dve.wait_ge(film_mm, 1)
                    dve.tensor_tensor(film[:, :], ps_f[:, :], film_b[:, :], ALU.add).then_inc(pre, 1)
                    dve.memset(keep[:, :], 1.0).then_inc(pre, 1)
                    for t in range(NT):
                        dve.wait_ge(pre, 1 + 2 * NT + 2 + t)
                        dve.tensor_tensor(keep[:, :], keep[:, :], mask[:, t, :], ALU.subtract).then_inc(pre, 1)
                    dve.wait_ge(pre, n_pre)
                    wide_b = lambda a: a.unsqueeze(1).to_broadcast([P, K4, D])

                    def group(g, last):
                        at = V * g
                        dve.wait_ge(h_mm, g + 1)
                        dve.wait_ge(x_in, 16 * (g + 1))
                        for k in range(K4):
                            st = dve.tensor_scalar(y[:, k, :], xg[:, k, :], keep[:, bass.ds(g * K4 + k, 1)], None, ALU.mult)
                        st.then_inc(vec, 1)
                        for t in range(NT):
                            dve.wait_ge(vec, at + 1 + t)
                            to, frm = ((z, y), (y, z), (z, y))[t]
                            for k in range(K4):
                                st = dve.scalar_tensor_tensor(out=to[:, k, :], in0=ps_h[k][:, t * D:(t + 1) * D], scalar=mask[:, t, bass.ds(g * K4 + k, 1)],
                                                              in1=frm[:, k, :], op0=ALU.mult, op1=ALU.add)
                            st.then_inc(vec, 1)
                        dve.wait_ge(vec, at + 4)
                        norm_stats(dve, z, stats, mean_var, var_eps, vec, at + 4)
                        dve.wait_ge(rooted, 2 * g + 1)
                        norm_apply(dve, y, z, mean_var, root, inverse, vec, at + 7)
                        at = at + 9
                        dve.wait_ge(vec, at)
                        dve.tensor_tensor(v[:, :, :], y[:, :, :], wide_b(ln_g[:, :]), ALU.mult).then_inc(vec, 1)
                        dve.wait_ge(vec, at + 1)
                        dve.tensor_tensor(y[:, :, :], v[:, :, :], wide_b(ln_b[:, :]), ALU.add).then_inc(vec, 1)
                        dve.wait_ge(vec, at + 2)
                        dve.tensor_tensor(v[:, :, :], y[:, :, :], xg[:, :, :], ALU.add).then_inc(vec, 1)
                        dve.wait_ge(vec, at + 3)
                        dve.tensor_tensor(y[:, :, :], v[:, :, :], wide_b(film[:, 0:D]), ALU.mult).then_inc(vec, 1)
                        dve.wait_ge(vec, at + 4)
                        dve.tensor_tensor(v[:, :, :], y[:, :, :], wide_b(film[:, D:2 * D]), ALU.add).then_inc(vec, 1)
                        at = at + 5
                        dve.wait_ge(vec, at)
                        dve.tensor_tensor(z[:, :, :], v[:, :, :], xg[:, :, :], ALU.add).then_inc(vec, 1)
                        dve.wait_ge(vec, at + 1)
                        norm_stats(dve, z, stats, mean_var, var_eps, vec, at + 1)
                        dve.wait_ge(rooted, 2 * g + 2)
                        hold(dve, stored, 16 * g)
                        norm_apply(dve, x3, z, mean_var, root, inverse, vec, at + 4)
                    over_groups(dve, group)

    def propagate():
        with ExitStack() as ctx:
            tmp, psum, sem, pair = scope(ctx, "e3")
            NWM = P // WIN
            S = 4
            src_all = tmp("src_all", [P, S, J, P])
            equal = tmp("equal", [P, 2, J, P])
            junk, below, spare = tmp("junk", [P, J, P]), tmp("below", [P, P]), tmp("spare", [P, 1])
            earlier, again, shift = tmp("earlier", [P, 2, J]), tmp("again", [P, 2, J]), tmp("shift", [P, 2, J])
            row = tmp("row", [P, S, J], I32)
            weighted, merged = tmp("weighted", [P, 2, J, D]), tmp("merged", [P, S, J, D])
            onehot = tmp("onehot", [P, 2, NWM, J, WIN])
            spread, window = tmp("spread", [P, 2, NWM, J, P]), tmp("window", [P, S, NWM, D])
            ps_t = [psum(f"ps_t{s}", [P, NWM, P]) for s in range(2)]
            ps_y = [psum(f"ps_y{s}", [P, J, D]) for s in range(2)]
            ps_z = [psum(f"ps_z{s}", [P, J, D]) for s in range(2)]
            cleared = sem("cleared")
            src_in, win_in, y_mm, counted = (pair(n, S) for n in ("src_in", "win_in", "y_mm", "counted"))
            marked, turned, copied, y_out, compared, z_mm, z_out, placed = (pair(n) for n in
                ("marked", "turned", "copied", "y_out", "compared", "z_mm", "z_out", "placed"))
            sent = [sem(f"sent{c}") for c in range(COPIES)]

            def sync_program(sp, nw):
                def load(q, at):
                    s, c = at(S)
                    hold(sp, counted[s], c)
                    sp.dma_start(src_all[:, s, :, :].rearrange("p j e -> p (j e)"),
                                 src_row.rearrange("(q e) -> q e", e=GE)[bass.ds(q, 1), :].broadcast_to([P, GE])).then_inc(src_in[s], 16)
                    hold(sp, y_mm[s], c)
                    sp.nop(nofuse=True)
                    load_windows(sp, window, s, xs[3], q, nw, win_in[s])
                pipeline(sp, (load, 0))

            def pe_program(pe, nw):
                def expand(q, at):
                    s, c = at(2)
                    s4, c4 = at(S)
                    pe.wait_ge(win_in[s4], 16 * J * nw * (c4 + 1))
                    pe.wait_ge(copied[s], c + 1)
                    hold(pe, y_out[s], c)
                    for j in range(J):
                        for w in range(nw):
                            mm = pe.matmul(ps_y[s][:, j, :], spread[:, s, w, j, :], window[:, s4, w, :], start=(w == 0), stop=(w == nw - 1))
                    mm.then_inc(y_mm[s4], 1)

                def merge(q, at):
                    s, c = at(2)
                    pe.wait_ge(compared[s], c + 1)
                    pe.wait_ge(y_out[s], c + 1)
                    hold(pe, z_out[s], c)
                    for j in range(J):
                        mm = pe.matmul(ps_z[s][:, j, :], equal[:, s, j, :], weighted[:, s, j, :], start=True, stop=True)
                    mm.then_inc(z_mm[s], 1)

                def turn(q, at):
                    s, c = at(2)
                    pe.wait_ge(marked[s], c + 1)
                    hold(pe, copied[s], c)
                    for w in range(nw):
                        mm = pe.transpose(ps_t[s][:, w, :], onehot[:, s, w, :, :].rearrange("p j n -> p (j n)"), ident[:, :])
                    mm.then_inc(turned[s], 1)
                pipeline(pe, (turn, 0), (expand, 1), (merge, 2))

            def act_program(act, nw):
                act.wait_ge(cleared, 3)

                def copy(q, at):
                    s, c = at(2)
                    s4, c4 = at(S)
                    act.wait_ge(turned[s], c + 1)
                    before = (s4 + 2) % S
                    hold(act, y_mm[before], c4 + (1 if s4 >= 2 else 0))
                    spread_nodes(act, spread, ps_t[s], s, nw).then_inc(copied[s], 1)

                def move(q, at):
                    s, c = at(2)
                    s4, c4 = at(S)
                    act.wait_ge(z_mm[s], c + 1)
                    if not isinstance(q, int) or q >= S:
                        for j in range(J):
                            act.wait_ge(sent[s * J + j], 16 * (c - 1))
                    act.copy(merged[:, s4, :, :], ps_z[s][:, :, :]).then_inc(z_out[s], 1)
                pipeline(act, (copy, 0), (move, 2))

            def dve_program(dve, nw):
                dve.memset(spread[:, :, :, :, :], 0.0).then_inc(cleared, 1)
                dve.tensor_scalar(spare[:, :], ident[:, 0:1], 0.0, None, ALU.mult).then_inc(cleared, 1)
                dve.wait_ge(cleared, 3)
                dve.tensor_tensor_reduce(junk[:, 0, :], ident[:, :], iota[:, 0:P], 1.0, 0.0, ALU.mult, ALU.add, spare[:, :]).then_inc(cleared, 1)
                dve.wait_ge(cleared, 4)
                dve.tensor_scalar(below[:, :], iota[:, 0:P], spare[:, 0:1], None, ALU.is_lt).then_inc(cleared, 1)
                dve.wait_ge(cleared, 5)
                dve.tensor_scalar(spare[:, :], spare[:, :], float(N), None, ALU.add).then_inc(cleared, 1)
                dve.wait_ge(cleared, 6)

                def mark(q, at):
                    s, c = at(2)
                    hold(dve, turned[s], c)
                    mark_nodes(dve, onehot, s, q, nw).then_inc(marked[s], 1)

                def weigh(q, at):
                    s, c = at(2)
                    s4, c4 = at(S)
                    dve.wait_ge(y_mm[s4], c4 + 1)
                    hold(dve, z_mm[s], c)
                    dve.tensor_tensor(weighted[:, s, :, :], ps_y[s][:, :, :],
                                      w_t[:, bass.ds(q * J, J)].unsqueeze(2).to_broadcast([P, J, D]), ALU.mult).then_inc(y_out[s], 1)

                def compare(q, at):
                    s, c = at(2)
                    s4, c4 = at(S)
                    dve.wait_ge(src_in[s4], 16 * (c4 + 1))
                    hold(dve, z_mm[s], c)
                    for j in range(J):
                        eq = dve.tensor_scalar(equal[:, s, j, :], src_all[:, s4, j, :], src_t[:, bass.ds(q * J + j, 1)], None, ALU.is_equal)
                    eq.then_inc(compared[s], 1)
                    dve.wait_ge(compared[s], c + 1)
                    hold(dve, counted[(s4 + 3) % S], c4 + (1 if s4 >= 1 else 0))
                    for j in range(J):
                        cnt = dve.tensor_tensor_reduce(junk[:, j, :], equal[:, s, j, :], below[:, :], 1.0, 0.0, ALU.mult, ALU.add, earlier[:, s, j:j + 1])
                    cnt.then_inc(counted[s4], 1)
                    dve.wait_ge(counted[s4], c4 + 1)
                    dve.tensor_scalar(again[:, s, :], earlier[:, s, :], 0.0, None, ALU.is_gt)
                    dve.tensor_scalar(shift[:, s, :], src_t[:, bass.ds(q * J, J)], spare[:, 0:1], -1.0, ALU.subtract, ALU.mult).then_inc(placed[s], 1)
                    dve.wait_ge(placed[s], 3 * c + 1)
                    dve.tensor_tensor(shift[:, s, :], shift[:, s, :], again[:, s, :], ALU.mult).then_inc(placed[s], 1)
                    dve.wait_ge(placed[s], 3 * c + 2)
                    if not isinstance(q, int) or q >= S:
                        for j in range(J):
                            dve.wait_ge(sent[s * J + j], 16 * (c - 1))
                    dve.tensor_tensor(row[:, s4, :], shift[:, s, :], src_t[:, bass.ds(q * J, J)], ALU.add).then_inc(placed[s], 1)

                pipeline(dve, (mark, 0), (compare, 1), (weigh, 1))

            with nc.Block() as block:
                @block.gpsimd
                def _(pool):
                    pool.memset(junk[:, 1, 0:1], 0.0).then_inc(cleared, 1)

                    def send(q, at):
                        s, c = at(2)
                        s4, c4 = at(S)
                        pool.wait_ge(z_out[s], c + 1)
                        pool.wait_ge(placed[s], 3 * (c + 1))
                        for j in range(J):
                            copy = s * J + j
                            hold(pool, sent[copy], 16 * c)
                            pool.nop(nofuse=True)
                            pool.indirect_dma_start(side[copy], bass.IndirectOffsetOnAxis(ap=row[:, s4, j:j + 1], axis=0),
                                                    merged[:, s4, j, :], None, compute_op=ALU.add).then_inc(sent[copy], 16)
                    pipeline(pool, (send, 0))
                    for c in range(COPIES):
                        pool.wait_ge(sent[c], 16 * (Q // 2))

                @block.sync
                def _(sp):
                    both_ways(sp, lambda nw: sync_program(sp, nw))

                @block.tensor
                def _(pe):
                    both_ways(pe, lambda nw: pe_program(pe, nw))

                @block.scalar
                def _(act):
                    both_ways(act, lambda nw: act_program(act, nw))

                @block.vector
                def _(dve):
                    both_ways(dve, lambda nw: dve_program(dve, nw))

    def last_nodes():
        with ExitStack() as ctx:
            tmp, psum, sem, pair = scope(ctx, "n3")
            xg = tmp("xg", [P, 2, K4, D])
            total, y, z = (tmp(n, [P, K4, D]) for n in ("total", "y", "z"))
            parts = tmp("parts", [P, 2, COPIES, K4, D])
            stats, mean_var = tmp("stats", [P, K4, 6]), tmp("mean_var", [P, K4, 2])
            var_eps, root, inverse = (tmp(n, [P, K4]) for n in ("var_eps", "root", "inverse"))
            x_in = pair("x_in")
            rooted, vec, stored = sem("rooted"), sem("vec"), sem("stored")
            V = COPIES + 7
            whole = N // GE
            rest = N - whole * GE

            def two_by_two(eng, group):
                for s in range(2):
                    group(0, s)
                with eng.Fori(1, whole // 2) as i:
                    for s in range(2):
                        group(i, s)

            with nc.Block() as block:
                @block.sync
                def _(sp):
                    def load(i, s):
                        g = 2 * i + s
                        hold(sp, vec, V * (g - 1) if not isinstance(i, int) or i > 0 else 0)
                        sp.dma_start(xg[:, s, :, :], rows_of(xs[3], g, D)).then_inc(x_in[s], 16)
                        for c in range(COPIES):
                            flat = side[c][0:whole * GE, :].rearrange("(a k) f -> a (k f)", k=K4)
                            sp.dma_start(parts[:, s, c, :, :].rearrange("p k f -> p (k f)"), flat[bass.ds(g * P, P), :]).then_inc(x_in[s], 16)

                    def store(g):
                        sp.wait_ge(vec, V * (g + 1))
                        flat = out[0:whole * GE, :].rearrange("(a k) f -> a (k f)", k=K4)
                        sp.dma_start(flat[bass.ds(g * P, P), :], z[:, :, :].rearrange("p k f -> p (k f)")).then_inc(stored, 16)

                    def both(i, s):
                        load(i, s)
                        if not isinstance(i, int) or i > 0 or s > 0:
                            store(2 * i + s - 1)
                    two_by_two(sp, both)
                    sp.wait_ge(vec, V * (whole - 1))
                    parts_n = -(-rest // K4)
                    sp.dma_start(xg[:, 0, :, :], rows_of(xs[3], whole, D)).then_inc(x_in[0], 16)
                    for c in range(COPIES):
                        flat = side[c][whole * GE:whole * GE + parts_n * K4, :].rearrange("(a k) f -> a (k f)", k=K4)
                        sp.dma_start(parts[0:parts_n, 0, c, :, :].rearrange("p k f -> p (k f)"), flat).then_inc(x_in[0], 16)
                    store(whole - 1)
                    sp.wait_ge(vec, V * (whole + 1))
                    n = rest // K4
                    sp.dma_start(out[whole * GE:whole * GE + n * K4, :].rearrange("(a k) f -> a (k f)", k=K4),
                                 z[0:n, :, :].rearrange("p k f -> p (k f)")).then_inc(stored, 16)
                    left = rest - n * K4
                    sp.dma_start(out[N - left:N, :].rearrange("(a k) f -> a (k f)", k=left),
                                 z[n:n + 1, 0:left, :].rearrange("p k f -> p (k f)")).then_inc(stored, 16)
                    sp.wait_ge(stored, 16 * (whole + 2))

                @block.scalar
                def _(act):
                    with act.Fori(0, whole + 1) as g:
                        act.wait_ge(vec, V * g + V - 2)
                        act.activation(root[:, :], var_eps[:, :], ACT.Sqrt).then_inc(rooted, 1)

                @block.vector
                def _(dve):
                    def group(i, s):
                        g = 2 * i + s
                        at = V * g
                        dve.wait_ge(x_in[s], 16 * (COPIES + 1) * (i + 1))
                        hold(dve, vec, at)
                        dve.tensor_tensor(total[:, :, :], parts[:, s, 0, :, :], parts[:, s, 1, :, :], ALU.add).then_inc(vec, 1)
                        for c in range(2, COPIES):
                            dve.wait_ge(vec, at + c - 1)
                            dve.tensor_tensor(total[:, :, :], total[:, :, :], parts[:, s, c, :, :], ALU.add).then_inc(vec, 1)
                        at = at + COPIES - 1
                        dve.wait_ge(vec, at)
                        dve.scalar_tensor_tensor(out=y[:, :, :], in0=total[:, :, :], scalar=3.0, in1=xg[:, s, :, :],
                                                 op0=ALU.mult, op1=ALU.add).then_inc(vec, 1)
                        dve.wait_ge(vec, at + 1)
                        dve.tensor_scalar(y[:, :, :], y[:, :, :], 0.25, None, ALU.mult).then_inc(vec, 1)
                        dve.wait_ge(vec, at + 2)
                        dve.tensor_tensor(total[:, :, :], y[:, :, :], xg[:, s, :, :], ALU.add).then_inc(vec, 1)
                        dve.wait_ge(vec, at + 3)
                        norm_stats(dve, total, stats, mean_var, var_eps, vec, at + 3)
                        dve.wait_ge(rooted, g + 1)
                        hold(dve, stored, 16 * g)
                        norm_apply(dve, z, total, mean_var, root, inverse, vec, at + 6)
                    two_by_two(dve, group)
                    group(whole // 2, 0)

    lay_out()
    with ExitStack() as layer0:
        agg = layer0.enter_context(nc.sbuf_tensor("agg0", [P, NP * R], F32))
        share = layer0.enter_context(nc.sbuf_tensor("share", [1, NP * R], F32))
        with ExitStack() as edges0:
            u_keys = edges0.enter_context(nc.sbuf_tensor("u_keys", [P, D], F32))
            e_bias = edges0.enter_context(nc.sbuf_tensor("e_bias", [Q, R], F32))
            e_t = edges0.enter_context(nc.sbuf_tensor("e_t", [P, T], F32))
            rel_tables(u_keys, e_bias, agg, share)
            rel_scores(u_keys, e_t)
            rel_softmax(e_t, e_bias)
        rel_sums(agg, share)
        rel_nodes(agg, share)
    layer1 = top.enter_context(ExitStack())
    agg1 = layer1.enter_context(nc.sbuf_tensor("agg1", [P, NP], F32))
    messages(agg1)
    message_nodes(agg1)
    layer1.close()
    with ExitStack() as layer2:
        a_t = layer2.enter_context(nc.sbuf_tensor("a_t", [P, T * H], F32))
        agg2 = layer2.enter_context(nc.sbuf_tensor("agg2", [P, NP], F32))
        head_scores(a_t)
        head_softmax(a_t)
        head_sums(a_t, agg2)
        head_nodes(agg2)
    propagate()
    last_nodes()
    top.close()


OUT = ((N, D), "float32")


def kernel(**inputs):
    import numpy as np
    import concourse.bacc as bacc
    from concourse.bass_utils import run_bass_kernel_spmd

    nc = bacc.Bacc("TRN2", target_bir_lowering=False, num_devices=1)
    arrays, args = {}, {}
    for name, value in inputs.items():
        a = np.ascontiguousarray(value)
        arrays[f"in_{name}_dram"] = a
        args[name] = nc.dram_tensor(f"in_{name}_dram", a.shape, mybir.dt.from_np(a.dtype), kind="ExternalInput").ap()
    args["out"] = nc.dram_tensor("out_0_dram", OUT[0], mybir.dt.from_np(np.dtype(OUT[1])), kind="ExternalOutput").ap()
    build(nc, **args)
    result = run_bass_kernel_spmd(nc, [arrays], core_ids=[0])
    return result.results[0]["out_0_dram"]
```
